# Optimizing a Trainium2 kernel written in Bass

```python
import numpy as np
import jax
import jax.numpy as jnp

def _softmax(x, axis=-1):
    return jax.nn.softmax(x, axis=axis)

def _gelu(x):
    return jax.nn.gelu(x, approximate=True)

def _silu(x):
    return jax.nn.silu(x)

def _sigmoid(x):
    return jax.nn.sigmoid(x)

def _layernorm(x, axis=-1, eps=1e-05):
    m = jnp.mean(x, axis=axis, keepdims=True)
    v = jnp.var(x, axis=axis, keepdims=True)
    return (x - m) / jnp.sqrt(v + eps)

def _scatter_add(tgt, idx, src, axis=0):
    return tgt.at[idx].add(src)

def _segment_sum(src, seg, n):
    return jax.ops.segment_sum(src, seg, n)
kernel_name = 'mk_decoder_preln_d1_seqx_r8_06e241'

def setup_inputs(seed: int=0):
    np.random.seed(seed)
    _w = jnp.asarray

    def _rec_inputs():
        import jax
        import jax.numpy as jnp
        _rk = jax.random.key(seed)
        x = -0.0003929 + 0.9999 * jax.random.normal(jax.random.fold_in(_rk, 1), (32, 64, 256), jnp.float32)
        _lenS = 64 - jax.random.randint(jax.random.fold_in(_rk, 7), (32,), 0, max(1, 64 // 4) + 1, jnp.int32)
        _lenS2 = 64 - jax.random.randint(jax.random.fold_in(_rk, 8), (32,), 0, max(1, 64 // 4) + 1, jnp.int32)
        _ctx_1024P = jax.random.normal(jax.random.fold_in(_rk, 11), (32, 16, 128), jnp.float32)
        _ctx_1024c = jax.random.dirichlet(jax.random.fold_in(_rk, 511), 0.3 * jnp.ones((16,), jnp.float32), (32, 64))
        _ctx_1024t = jnp.einsum('bsk,bkd->bsd', _ctx_1024c, _ctx_1024P)
        _ctx_1024t = _ctx_1024t * jax.lax.rsqrt(jnp.mean(jnp.square(_ctx_1024t)) + 1e-12) * 0.953939
        ctx_1024 = 0.000227908 + 0.99994 * (_ctx_1024t + 0.3 * jax.random.normal(jax.random.fold_in(_rk, 611), (32, 64, 128), jnp.float32))
        return (x, ctx_1024)
    x, ctx_1024 = _rec_inputs()

    def _L0_attn_setup():
        import jax, jax.numpy as jnp
        import numpy as np
        B, T, HID = (1, 128, 256)
        H, DK, DV, M, KW = (16, 128, 128, 128, 4)
        SCALE = DK ** (-0.5)
        EPS = 1e-05

        def short_conv(x, w):
            K = w.shape[1]
            xp = jnp.pad(x, ((0, 0), (K - 1, 0), (0, 0)))
            t = x.shape[1]
            y = sum((xp[:, i:i + t] * w[:, i] for i in range(K)))
            return jax.nn.silu(y)

        def l2norm(x):
            return x * jax.lax.rsqrt(jnp.sum(x * x, axis=-1, keepdims=True) + 1e-06)

        def gsa2_scan(q, k, v, w, g, beta):
            b = q.shape[0]
            tm = lambda x: jnp.moveaxis(x, 1, 0)
            Sk0 = jnp.zeros((b, H, DK, M), q.dtype)
            Sv0 = jnp.zeros((b, H, M, DV), q.dtype)

            def step(carry, xs):
                Sk, Sv = carry
                q_t, k_t, v_t, w_t, g_t, b_t = xs
                gt = jnp.exp(g_t)
                bw = b_t[:, :, None] * w_t
                Sk = Sk * gt[:, :, None, :] + k_t[..., :, None] * bw[:, :, None, :]
                Sv = Sv * gt[..., None] + bw[..., None] * v_t[:, :, None, :]
                s = jnp.einsum('bhd,bhdm->bhm', q_t, Sk) * SCALE
                a = jax.nn.softmax(s, axis=-1)
                o_t = jnp.einsum('bhm,bhmd->bhd', a, Sv)
                return ((Sk, Sv), o_t)
            (_, _), o = jax.lax.scan(step, (Sk0, Sv0), (tm(q), tm(k), tm(v), tm(w), tm(g), tm(beta)))
            return jnp.moveaxis(o, 0, 1)
        key = jax.random.key(seed)
        ks = jax.random.split(key, 16)
        s = 0.02
        return {'hidden_states': jax.random.normal(ks[0], (B, T, HID), jnp.float32), 'Wq': jax.random.normal(ks[1], (HID, H * DK), jnp.float32) * s, 'Wk': jax.random.normal(ks[2], (HID, H * DK), jnp.float32) * s, 'Wv': jax.random.normal(ks[3], (HID, H * DV), jnp.float32) * s, 'Ww': jax.random.normal(ks[4], (HID, H * M), jnp.float32) * s, 'cq': jax.random.normal(ks[5], (H * DK, KW), jnp.float32) * 0.2, 'ck': jax.random.normal(ks[6], (H * DK, KW), jnp.float32) * 0.2, 'cv': jax.random.normal(ks[7], (H * DV, KW), jnp.float32) * 0.2, 'Wf1': jax.random.normal(ks[8], (HID, DV), jnp.float32) * s, 'Wf2': jax.random.normal(ks[9], (DV, H * M), jnp.float32) * s, 'Wb': jax.random.normal(ks[10], (HID, H), jnp.float32) * s, 'Wg1': jax.random.normal(ks[11], (HID, DV), jnp.float32) * s, 'Wg2': jax.random.normal(ks[12], (DV, H * DV), jnp.float32) * s, 'bg2': jnp.zeros((H * DV,), jnp.float32), 'norm_w': jnp.ones((DV,), jnp.float32), 'Wo': jax.random.normal(ks[13], (H * DV, HID), jnp.float32) * s}
    _L0_attn_all = _L0_attn_setup()
    _L0_attn_in = {k: v for k, v in _L0_attn_all.items() if k in ('Wq', 'Wk', 'Wv', 'Ww', 'cq', 'ck', 'cv', 'Wf1', 'Wf2', 'Wb', 'Wg1', 'Wg2', 'bg2', 'norm_w', 'Wo')}
    del _L0_attn_all

    def _L0_xattn_setup():
        import jax, jax.numpy as jnp
        import numpy as np
        EPS = 1e-05

        def rmsnorm(x, g, eps=EPS):
            var = jnp.mean(jnp.square(x), axis=-1, keepdims=True)
            return x * jax.lax.rsqrt(var + eps) * g
        key = jax.random.key(seed)
        ks = jax.random.split(key, 8)
        B, Sq, Skv = (2, 512, 64)
        dim, cdim, H, D = (256, 128, 16, 128)
        inner = H * D
        s = lambda f: 1.0 / np.sqrt(f)
        return {'hidden_states': jax.random.normal(ks[0], (B, Sq, dim), jnp.float32), 'encoder_hidden_states': jax.random.normal(ks[1], (B, Skv, cdim), jnp.float32), 'Wq': jax.random.normal(ks[2], (dim, inner), jnp.float32) * s(dim), 'Wk': jax.random.normal(ks[3], (cdim, inner), jnp.float32) * s(cdim), 'Wv': jax.random.normal(ks[4], (cdim, inner), jnp.float32) * s(cdim), 'Wo': jax.random.normal(ks[5], (inner, dim), jnp.float32) * s(inner), 'gq': jnp.ones((D,), jnp.float32), 'gk': jnp.ones((D,), jnp.float32)}
    _L0_xattn_all = _L0_xattn_setup()
    _L0_xattn_in = {k: v for k, v in _L0_xattn_all.items() if k in ('Wq', 'Wk', 'Wv', 'Wo', 'gq', 'gk')}
    del _L0_xattn_all

    def _L0_ffn_setup():
        import jax, jax.numpy as jnp
        import numpy as np
        B, S, D, E, TOPK = (4, 256, 256, 8, 2)
        key = jax.random.key(seed)
        k1, k2, k3 = jax.random.split(key, 3)
        x = jax.random.normal(k1, (B, S, D), dtype=jnp.float32)
        gate_w = jax.random.normal(k2, (E, D), dtype=jnp.float32) * 0.02
        expert_w = jax.random.normal(k3, (E, D, D), dtype=jnp.float32) / np.sqrt(D)
        expert_b = jnp.zeros((E, D), dtype=jnp.float32)
        return {'x': x, 'gate_w': gate_w, 'expert_w': expert_w, 'expert_b': expert_b}
    _L0_ffn_all = _L0_ffn_setup()
    _L0_ffn_in = {k: v for k, v in _L0_ffn_all.items() if k in ('gate_w', 'expert_w', 'expert_b')}
    del _L0_ffn_all
    return {'x': x, 'ctx_1024': ctx_1024, 'L0_attn_Wq': _L0_attn_in['Wq'], 'L0_attn_Wk': _L0_attn_in['Wk'], 'L0_attn_Wv': _L0_attn_in['Wv'], 'L0_attn_Ww': _L0_attn_in['Ww'], 'L0_attn_cq': _L0_attn_in['cq'], 'L0_attn_ck': _L0_attn_in['ck'], 'L0_attn_cv': _L0_attn_in['cv'], 'L0_attn_Wf1': _L0_attn_in['Wf1'], 'L0_attn_Wf2': _L0_attn_in['Wf2'], 'L0_attn_Wb': _L0_attn_in['Wb'], 'L0_attn_Wg1': _L0_attn_in['Wg1'], 'L0_attn_Wg2': _L0_attn_in['Wg2'], 'L0_attn_bg2': _L0_attn_in['bg2'], 'L0_attn_norm_w': _L0_attn_in['norm_w'], 'L0_attn_Wo': _L0_attn_in['Wo'], 'L0_xattn_Wq': _L0_xattn_in['Wq'], 'L0_xattn_Wk': _L0_xattn_in['Wk'], 'L0_xattn_Wv': _L0_xattn_in['Wv'], 'L0_xattn_Wo': _L0_xattn_in['Wo'], 'L0_xattn_gq': _L0_xattn_in['gq'], 'L0_xattn_gk': _L0_xattn_in['gk'], 'L0_ffn_gate_w': _L0_ffn_in['gate_w'], 'L0_ffn_expert_w': _L0_ffn_in['expert_w'], 'L0_ffn_expert_b': _L0_ffn_in['expert_b']}

def reference(x, ctx_1024, L0_attn_Wq, L0_attn_Wk, L0_attn_Wv, L0_attn_Ww, L0_attn_cq, L0_attn_ck, L0_attn_cv, L0_attn_Wf1, L0_attn_Wf2, L0_attn_Wb, L0_attn_Wg1, L0_attn_Wg2, L0_attn_bg2, L0_attn_norm_w, L0_attn_Wo, L0_xattn_Wq, L0_xattn_Wk, L0_xattn_Wv, L0_xattn_Wo, L0_xattn_gq, L0_xattn_gk, L0_ffn_gate_w, L0_ffn_expert_w, L0_ffn_expert_b):
    import jax
    import jax.numpy as jnp

    def _L0_attn_ref(hidden_states, Wq, Wk, Wv, Ww, cq, ck, cv, Wf1, Wf2, Wb, Wg1, Wg2, bg2, norm_w, Wo):
        import jax, jax.numpy as jnp
        import numpy as np
        B, T, HID = (1, 128, 256)
        H, DK, DV, M, KW = (16, 128, 128, 128, 4)
        SCALE = DK ** (-0.5)
        EPS = 1e-05

        def short_conv(x, w):
            K = w.shape[1]
            xp = jnp.pad(x, ((0, 0), (K - 1, 0), (0, 0)))
            t = x.shape[1]
            y = sum((xp[:, i:i + t] * w[:, i] for i in range(K)))
            return jax.nn.silu(y)

        def l2norm(x):
            return x * jax.lax.rsqrt(jnp.sum(x * x, axis=-1, keepdims=True) + 1e-06)

        def gsa2_scan(q, k, v, w, g, beta):
            b = q.shape[0]
            tm = lambda x: jnp.moveaxis(x, 1, 0)
            Sk0 = jnp.zeros((b, H, DK, M), q.dtype)
            Sv0 = jnp.zeros((b, H, M, DV), q.dtype)

            def step(carry, xs):
                Sk, Sv = carry
                q_t, k_t, v_t, w_t, g_t, b_t = xs
                gt = jnp.exp(g_t)
                bw = b_t[:, :, None] * w_t
                Sk = Sk * gt[:, :, None, :] + k_t[..., :, None] * bw[:, :, None, :]
                Sv = Sv * gt[..., None] + bw[..., None] * v_t[:, :, None, :]
                s = jnp.einsum('bhd,bhdm->bhm', q_t, Sk) * SCALE
                a = jax.nn.softmax(s, axis=-1)
                o_t = jnp.einsum('bhm,bhmd->bhd', a, Sv)
                return ((Sk, Sv), o_t)
            (_, _), o = jax.lax.scan(step, (Sk0, Sv0), (tm(q), tm(k), tm(v), tm(w), tm(g), tm(beta)))
            return jnp.moveaxis(o, 0, 1)
        h = hidden_states
        q = short_conv(h @ Wq, cq)
        k = short_conv(h @ Wk, ck)
        v = short_conv(h @ Wv, cv)
        w = short_conv(h @ Ww, cv)
        g = jax.nn.log_sigmoid(h @ Wf1 @ Wf2)
        beta = jax.nn.sigmoid(h @ Wb)
        rs = lambda x, d: x.reshape(x.shape[0], x.shape[1], -1, d)
        q, k = (rs(q, DK), rs(k, DK))
        v = rs(v, DV)
        w = l2norm(rs(w, M))
        g = rs(g, M)
        o = gsa2_scan(q, k, v, w, g, beta)
        gate = rs(h @ Wg1 @ Wg2 + bg2, DV)
        o = o * jax.lax.rsqrt(jnp.mean(o * o, axis=-1, keepdims=True) + EPS)
        o = o * norm_w * jax.nn.sigmoid(gate)
        o = o.reshape(o.shape[0], o.shape[1], -1)
        return o @ Wo

    def _L0_xattn_ref(hidden_states, encoder_hidden_states, Wq, Wk, Wv, Wo, gq, gk):
        import jax, jax.numpy as jnp
        import numpy as np
        EPS = 1e-05

        def rmsnorm(x, g, eps=EPS):
            var = jnp.mean(jnp.square(x), axis=-1, keepdims=True)
            return x * jax.lax.rsqrt(var + eps) * g
        B, Sq, _ = hidden_states.shape
        Skv = encoder_hidden_states.shape[1]
        D = gq.shape[0]
        H = Wq.shape[1] // D
        scale = 1.0 / np.sqrt(D)
        q = (hidden_states @ Wq).reshape(B, Sq, H, D)
        k = (encoder_hidden_states @ Wk).reshape(B, Skv, H, D)
        v = (encoder_hidden_states @ Wv).reshape(B, Skv, H, D)
        q = rmsnorm(q, gq)
        k = rmsnorm(k, gk)
        scores = jnp.einsum('bqhd,bkhd->bhqk', q, k) * scale
        attn = jax.nn.softmax(scores, axis=-1)
        out = jnp.einsum('bhqk,bkhd->bqhd', attn, v)
        out = out.reshape(B, Sq, H * D)
        return out @ Wo

    def _L0_ffn_ref(x, gate_w, expert_w, expert_b):
        import jax, jax.numpy as jnp
        import numpy as np
        B, S, D, E, TOPK = (4, 256, 256, 8, 2)
        batch_shape = x.shape[:-1]
        xf = x.reshape(-1, x.shape[-1])
        T = xf.shape[0]
        logits = jnp.einsum('td,ed->te', xf, gate_w)
        top_w, top_i = jax.lax.top_k(logits, TOPK)
        top_w = jax.nn.softmax(top_w.astype(jnp.float32), axis=-1).astype(x.dtype)
        gates = jnp.zeros((T, logits.shape[-1]), dtype=x.dtype)
        gates = gates.at[jnp.arange(T)[:, None], top_i].set(top_w)
        y = jnp.einsum('td,edo->eto', xf, expert_w) + expert_b[:, None, :]
        out = jnp.einsum('te,eto->to', gates, y)
        return out.reshape(*batch_shape, -1)
    x = x + _L0_attn_ref(_layernorm(x, axis=-1), L0_attn_Wq, L0_attn_Wk, L0_attn_Wv, L0_attn_Ww, L0_attn_cq, L0_attn_ck, L0_attn_cv, L0_attn_Wf1, L0_attn_Wf2, L0_attn_Wb, L0_attn_Wg1, L0_attn_Wg2, L0_attn_bg2, L0_attn_norm_w, L0_attn_Wo)
    x = x + _L0_xattn_ref(_layernorm(x, axis=-1), ctx_1024, L0_xattn_Wq, L0_xattn_Wk, L0_xattn_Wv, L0_xattn_Wo, L0_xattn_gq, L0_xattn_gk)
    x = x + _L0_ffn_ref(_layernorm(x, axis=-1), L0_ffn_gate_w, L0_ffn_expert_w, L0_ffn_expert_b)
    return x

_drawn_inputs = setup_inputs


def setup_inputs(seed=0):
    import zlib

    import numpy as np

    out = dict(_drawn_inputs(seed))
    spreads = {'L0_attn_bg2': (0.0, 0.1),
     'L0_attn_norm_w': (1.0, 0.2),
     'L0_xattn_gq': (1.0, 0.2),
     'L0_xattn_gk': (1.0, 0.2),
     'L0_ffn_expert_b': (0.0, 0.1)}
    factors = {'L0_attn_Wq': 8.0,
     'L0_attn_Wk': 8.0,
     'L0_attn_cq': 8.0,
     'L0_attn_ck': 8.0,
     'L0_attn_Wf1': 3.938,
     'L0_attn_Wf2': 5.581,
     'L0_attn_Wg1': 2.855,
     'L0_attn_Wg2': 2.882}
    for name, (base, spread) in spreads.items():
        noise = np.random.default_rng([zlib.crc32(name.encode()), seed]).standard_normal(out[name].shape)
        drawn = base * np.exp(spread * noise) if base else spread * noise
        out[name] = jnp.asarray(drawn.astype(out[name].dtype))
    for name, factor in factors.items():
        out[name] = (out[name] * factor).astype(out[name].dtype)
    return out
```

```python
from contextlib import ExitStack, contextmanager

import numpy as np

import concourse.bass as bass
from concourse import mybir

F32 = mybir.dt.float32
BF16 = mybir.dt.bfloat16
ALU = mybir.AluOpType
ACT = mybir.ActivationFunctionType
AX = mybir.AxisListType

P = 128
B, T, HID = 32, 64, 256
TOKENS = B * T
CDIM = 128
H = 16
KH = HID // P
PAIRS = TOKENS // P
G = 512
NP = G // P
NS = G // T
GROUPS = TOKENS // G
UNITS = GROUPS * H
TAPS = 4
E = 8
TOPK = 2
EPS = 1e-5
L2EPS = 1e-6
SCALE = float(P) ** -0.5

W_Q, W_K, W_V, W_W = (n * KH * P for n in range(4))
W_F2 = 4 * KH * P
W_G2 = W_F2 + P
W_CONV = W_G2 + P
W_BIAS = W_CONV + 4 * TAPS
W_HEAD = W_BIAS + 1
X_Q, X_K, X_V = 0, KH * P, KH * P + P
X_HEAD = KH * P + 2 * P


def shape_constants():
    s, t = np.meshgrid(np.arange(P), np.arange(P), indexing="ij")
    same = (s // T) == (t // T)
    mid = T // 2
    after = same & (s % T >= mid) & (s <= t)
    before = same & (s % T < mid) & (s > t)
    span = after.astype(np.float32) - before.astype(np.float32)
    causal = (same & (s <= t)).astype(np.float32)
    earlier = np.tril(np.ones((E, E), np.float32), -1).reshape(1, E * E).repeat(P, axis=0)
    return np.concatenate([np.eye(P, dtype=np.float32), span, causal, earlier], axis=1)


@contextmanager
def stage_semaphores(nc):
    with ExitStack() as ctx:
        used = []

        def sem(name):
            used.append(ctx.enter_context(nc.semaphore(name)))
            return used[-1]

        yield sem
        with nc.Block() as block:
            @block.sync
            def _(sp):
                for s in used:
                    sp.sem_clear(s)


def layernorm_block(nc, sems, tag, x_all, xT_all, ident, load=None):
    with ExitStack() as ctx:
        def sb(name, shape, dt=F32):
            return ctx.enter_context(nc.sbuf_tensor(f"{tag}_{name}", shape, dt))

        def sem(name):
            return sems(f"{tag}_{name}")

        stats = sb("stats", [P, PAIRS, 6])
        moments = sb("moments", [P, PAIRS, 2])
        eps = sb("eps", [P, 1])
        std = sb("std", [P, PAIRS])
        rstd = sb("rstd", [P, PAIRS])
        xn = sb("xn", [P, 2, NP, HID])
        turned = [ctx.enter_context(nc.psum_tensor(f"{tag}_turned{k}", [P, G], F32)) for k in range(2 * KH)]
        loaded = sem("loaded")
        eps_set = sem("eps_set")
        stats_done = sem("stats_done")
        moments_done = sem("moments_done")
        std_done = sem("std_done")
        rstd_done = sem("rstd_done")
        xn_done = sem("xn_done")
        turned_done = sem("turned_done")
        kept = sem("kept")
        block = ctx.enter_context(nc.Block())

        @block.sync
        def _(sp):
            if load is not None:
                for dst, src in load:
                    sp.dma_start(dst, src).then_inc(loaded, 16)

        @block.vector
        def _(dve):
            dve.memset(eps[:], EPS).then_inc(eps_set, 1)
            if load is not None:
                dve.wait_ge(loaded, 16 * len(load))
            for p in range(PAIRS):
                dve.bn_stats(stats[:, p, :], x_all[:, p, :]).then_inc(stats_done, 1)
            for p in range(PAIRS):
                dve.wait_ge(stats_done, p + 1)
                last = dve.bn_aggr(moments[:, p, :], stats[:, p, :])
            last.then_inc(moments_done, 1)
            dve.wait_ge(std_done, 1)
            dve.reciprocal(rstd[:], std[:]).then_inc(rstd_done, 1)
            dve.wait_ge(rstd_done, 1)
            for g in range(GROUPS):
                if g >= 2:
                    dve.wait_ge(turned_done, g - 1)
                for p in range(NP):
                    q = g * NP + p
                    last = dve.tensor_scalar(xn[:, g % 2, p, :], x_all[:, q, :], moments[:, q, 0:1],
                                             rstd[:, q:q + 1], ALU.subtract, ALU.mult)
                last.then_inc(xn_done, 1)

        @block.scalar
        def _(act):
            act.wait_ge(eps_set, 1)
            act.wait_ge(moments_done, 1)
            act.activation(std[:], moments[:, :, 1], ACT.Sqrt, bias=eps[:]).then_inc(std_done, 1)
            for g in range(GROUPS):
                act.wait_ge(turned_done, g + 1)
                for k in range(KH):
                    last = act.copy(xT_all[:, k, g * G:(g + 1) * G], turned[g % 2 * KH + k][:])
                last.then_inc(kept, 1)

        @block.tensor
        def _(pe):
            for g in range(GROUPS):
                pe.wait_ge(xn_done, g + 1)
                if g >= 2:
                    pe.wait_ge(kept, g - 1)
                for k in range(KH):
                    for p in range(NP):
                        last = pe.transpose(turned[g % 2 * KH + k][:, p * P:(p + 1) * P],
                                            xn[:, g % 2, p, k * P:(k + 1) * P], ident)
                last.then_inc(turned_done, 1)


def lowrank_block(nc, sems, xT_all, f1T, g1T, beta, Wf1g1, Wb, ident, small):
    with ExitStack() as ctx:
        def sb(name, shape, dt=F32):
            return ctx.enter_context(nc.sbuf_tensor(name, shape, dt))

        def sem(name):
            return sems(name)

        bT = sb("bT", [H, TOKENS])
        banks = [ctx.enter_context(nc.psum_tensor(f"low{k}", [P, G], F32)) for k in range(3)]
        beta_ps = ctx.enter_context(nc.psum_tensor("beta_ps", [P, PAIRS, H], F32))
        low_done = sem("low_done")
        low_kept = sem("low_kept")
        bT_kept = sem("bT_kept")
        beta_turned = sem("beta_turned")
        beta_done = sem("beta_done")
        block = ctx.enter_context(nc.Block())

        @block.tensor
        def _(pe):
            for g in range(GROUPS):
                cols = slice(g * G, (g + 1) * G)
                if g >= 1:
                    pe.wait_ge(low_kept, 2 * g)
                    pe.wait_ge(bT_kept, g)
                for n in range(2):
                    for k in range(KH):
                        last = pe.matmul(banks[n][:], Wf1g1[:, k, n, :], xT_all[:, k, cols],
                                         start=(k == 0), stop=(k == KH - 1))
                for k in range(KH):
                    last = pe.matmul(banks[2][0:H, :], Wb[:, k, :], xT_all[:, k, cols],
                                     start=(k == 0), stop=(k == KH - 1))
                last.then_inc(low_done, 1)
            pe.wait_ge(bT_kept, GROUPS)
            for q in range(PAIRS):
                last = pe.transpose(beta_ps[:, q, :], bT[:, q * P:(q + 1) * P], ident[0:H, 0:H])
            last.then_inc(beta_turned, 1)

        @block.scalar
        def _(act):
            for g in range(GROUPS):
                cols = slice(g * G, (g + 1) * G)
                act.wait_ge(low_done, g + 1)
                act.activation(bT[:, cols], banks[2][0:H, :], ACT.Sigmoid).then_inc(bT_kept, 1)
                act.copy(f1T[:, cols], banks[0][:]).then_inc(low_kept, 1)

        @block.vector
        def _(dve):
            for g in range(GROUPS):
                dve.wait_ge(low_done, g + 1)
                dve.tensor_copy(g1T[:, g * G:(g + 1) * G], banks[1][:]).then_inc(low_kept, 1)
            dve.wait_ge(beta_turned, 1)
            dve.tensor_copy(beta.rearrange("p g h q -> p g q h"),
                            beta_ps[:].rearrange("p (g q) h -> p g q h", g=GROUPS)).then_inc(beta_done, 1)


def gsa_block(nc, sems, w_heads, x_all, xT_all, f1T, g1T, beta, Wo, consts):
    ident, span, causal = consts
    with ExitStack() as ctx:
        def sb(name, shape, dt=F32):
            return ctx.enter_context(nc.sbuf_tensor(name, shape, dt))

        def psum(name, shape, dt=F32):
            return ctx.enter_context(nc.psum_tensor(name, shape, dt))

        def sem(name):
            return sems(name)

        hw = [sb(f"head_weights{i}", [P, W_HEAD]) for i in range(2)]
        q, k, v, w = (sb(f"{n}_chan", [P, G]) for n in "qkvw")
        f1 = sb("f1_static", [P, G])
        glog = sb("glog", [P, G])
        gtmp = sb("gtmp", [P, G])
        expD = sb("expD", [P, G])
        expDneg = sb("expDneg", [P, G])
        gate = sb("gate", [P, G])
        w2 = sb("w2", [P, G])
        wdec = sb("wdec", [P, G])
        wdec_tok = sb("wdec_tok", [P, G])
        v_tok = sb("v_tok", [P, G])
        qk = sb("qk", [P, G])
        score = sb("score", [P, G])
        probs = sb("probs", [P, G])
        pdec = sb("pdec", [P, G])
        pdec_chan = sb("pdec_chan", [P, G])
        mix = sb("mix", [P, G])
        osq = sb("osq", [P, G])
        o_tok = sb("o_tok", [P, G])
        o_chan = sb("o_chan", [P, G])
        ones = sb("ones", [P, 1])
        half = sb("half", [P, 1])
        l2eps = sb("l2eps", [P, 1])
        zeros = sb("zeros", [P, G], BF16)
        hbias = sb("hbias", [P, 1])
        lnw = sb("lnw", [P, NP])
        rw = sb("rw", [P, NP])
        coef = sb("coef", [P, NP])
        smax = sb("smax", [P, NP])
        nmax = sb("nmax", [P, NP])
        Z = sb("Z", [P, NP])
        Zeps = sb("Zeps", [P, NP])
        ssq = sb("ssq", [P, NP])
        y = sb("y", [P, NP])
        lny = sb("lny", [P, NP])
        rho = sb("rho", [P, NP])

        bank0, bank1, bank2, bank3, bank4, bank5 = (psum(f"bank{n}", [P, G]) for n in range(6))
        outacc = [psum(f"outacc{n}", [P, 2, HID]) for n in range(2)]

        names = """xq xk xv xw gx gate_x dtok dchan wsq att wdecT vT scores pdecT pv o oT wo
            tapq tapk tapv tapw gabs gexp gln decay ndecay gate_th siluq siluk siluv siluw lnw_s rw_s
            wdec_tok_s v_tok_s exps pdec_chan_s osq_s lny_s rho_s
            convq convk convv convw glog_s coef_s qk_s score_s smax_s nmax_s Zeps_s y_s mix_s o_tok_s o_chan_s
            w2_s wdec_s f1_s hbias_s pdec_s""".split()
        S = {n: sem(n) for n in names}
        primed = {
            "tensor": "xq xk xv xw gx gate_x dtok dchan wsq att wdecT vT scores pdecT pv o oT wo",
            "scalar": "tapq tapk tapv tapw gabs gexp gln decay ndecay gate_th siluq siluk siluv siluw lnw_s rw_s "
                      "wdec_tok_s v_tok_s exps pdec_chan_s osq_s lny_s rho_s",
            "vector": "convq convk convv convw glog_s coef_s qk_s score_s smax_s nmax_s Zeps_s y_s mix_s "
                      "o_tok_s o_chan_s",
            "gpsimd": "w2_s wdec_s f1_s hbias_s pdec_s",
        }
        weights_in = [sem(f"weights_in{i}") for i in range(2)]
        consts_set = sem("consts_set")
        zeroed = sem("zeroed")
        group_out = sem("group_out")
        block = ctx.enter_context(nc.Block())

        CONV = TAPS - 1

        def prime(eng, who):
            for n in primed[who].split():
                eng.sem_inc(S[n], 1)

        def done(n, times=1):
            return times * (n + 1) + 1

        def before(n, times=1):
            return times * n + 1

        def run_units(eng, front, merged, group_start=None, group_end=None):
            front(0, 0)
            with eng.Fori(0, GROUPS) as g:
                if group_start is not None:
                    group_start(g)
                with eng.Fori(0, H // 2) as j:
                    for par in range(2):
                        merged(g * H + j * 2 + par, j * 2 + par, par)
                if group_end is not None:
                    group_end(g)

        def pairs(t):
            return t[:].rearrange("p (q c) -> p q c", q=NP)

        def pc(t, p):
            return t[:, p * P:(p + 1) * P]

        @block.sync
        def _(sp):
            def load(n, h, par):
                sp.dma_start(hw[par][:], w_heads[h]).then_inc(weights_in[par], 16)

            load(0, 0, 0)
            load(1, 1, 1)
            with sp.Fori(0, UNITS // 2 - 1) as m:
                for par in range(2):
                    n = 2 * m + par
                    sp.wait_ge(S["gate_x"], done(n))
                    sp.wait_ge(S["gate_th"], done(n))
                    sp.wait_ge(S["convw"], done(n, CONV))
                    load(n + 2, (n + 2) % H, par)
            sp.wait_ge(S["gate_th"], done(UNITS - 2))
            sp.wait_ge(S["convw"], done(UNITS - 2, CONV))
            load(UNITS, 0, 0)

        @block.gpsimd
        def _(pool):
            prime(pool, "gpsimd")
            pool.memset(ones[:], 1.0).then_inc(consts_set, 1)
            pool.memset(half[:], 0.5).then_inc(consts_set, 1)
            pool.memset(l2eps[:], L2EPS).then_inc(consts_set, 1)
            pool.memset(zeros[:], 0.0).then_inc(consts_set, 1)

            def front(n, par):
                pool.wait_ge(S["gx"], before(n))
                pool.tensor_copy(f1[:], f1T[:, bass.ts(n // H, G)]).then_inc(S["f1_s"], 1)
                pool.wait_ge(weights_in[par], 16 * (n // 2 + 1))
                pool.wait_ge(consts_set, 4)
                pool.wait_ge(S["gate_th"], before(n))
                pool.tensor_tensor(hbias[:], hw[par][:, W_BIAS:W_BIAS + 1], half[:], ALU.mult)\
                    .then_inc(S["hbias_s"], 1)

            def merged(i, h, par):
                pool.wait_ge(S["siluw"], done(i))
                pool.wait_ge(S["wsq"], before(i))
                pool.tensor_tensor(w2[:], w[:], w[:], ALU.mult).then_inc(S["w2_s"], 1)
                pool.wait_ge(S["ndecay"], done(i))
                pool.wait_ge(S["pv"], before(i))
                pool.tensor_tensor(wdec[:], w[:], expDneg[:], ALU.mult).then_inc(S["wdec_s"], 1)
                front(i + 1, 1 - par)
                pool.wait_ge(S["exps"], done(i, NP))
                pool.wait_ge(S["pdecT"], before(i))
                pool.tensor_tensor(pdec[:], probs[:], expD[:], ALU.mult).then_inc(S["pdec_s"], 1)

            run_units(pool, front, merged)

        @block.tensor
        def _(pe):
            prime(pe, "tensor")
            pe.wait_ge(consts_set, 4)

            def project(n, par, bank, w_col, step):
                cols = bass.ts(n // H, G)
                for kk in range(KH):
                    last = pe.matmul(bank[:], hw[par][:, w_col + kk * P:w_col + (kk + 1) * P], xT_all[:, kk, cols],
                                     start=(kk == 0), stop=(kk == KH - 1))
                last.then_inc(S[step], 1)

            def f_q(n, par):
                pe.wait_ge(weights_in[par], 16 * (n // 2 + 1))
                pe.wait_ge(S["convv"], before(n, CONV))
                project(n, par, bank0, W_Q, "xq")

            def f_k(n, par):
                pe.wait_ge(S["convw"], before(n, CONV))
                project(n, par, bank1, W_K, "xk")

            def f_v(n, par):
                pe.wait_ge(S["convq"], done(n, CONV))
                project(n, par, bank0, W_V, "xv")

            def f_w(n, par):
                pe.wait_ge(S["convk"], done(n, CONV))
                project(n, par, bank1, W_W, "xw")

            def f_decay_logits(n, par):
                pe.wait_ge(S["f1_s"], done(n))
                pe.wait_ge(S["wdec_tok_s"], before(n))
                for p in range(NP):
                    last = pe.matmul(pc(bank4, p), pc(f1, p), hw[par][:, W_F2:W_F2 + P], start=True, stop=True)
                last.then_inc(S["gx"], 1)

            def f_decays(n, par):
                pe.wait_ge(S["glog_s"], done(n))
                pe.wait_ge(S["pdec_chan_s"], before(n))
                pe.matmul(bank3[:], span, glog[:], start=True, stop=True).then_inc(S["dtok"], 1)
                for p in range(NP):
                    last = pe.matmul(pc(bank4, p), pc(glog, p), span, start=True, stop=True)
                last.then_inc(S["dchan"], 1)

            def f_gate(n, par):
                pe.wait_ge(S["o_tok_s"], before(n))
                cols = bass.ts(n // H, G)
                pe.matmul(bank5[:], hw[par][:, W_G2:W_G2 + P], g1T[:, cols], start=True, stop=True)\
                    .then_inc(S["gate_x"], 1)

            def front(n, par):
                f_q(n, par)
                f_k(n, par)
                f_decay_logits(n, par)
                f_v(n, par)
                f_w(n, par)
                f_decays(n, par)
                f_gate(n, par)

            def merged(i, h, par):
                n, npar = i + 1, 1 - par
                pe.wait_ge(S["siluk"], done(i))
                pe.wait_ge(S["siluq"], done(i))
                pe.wait_ge(S["o_chan_s"], before(i))
                for p in range(NP):
                    last = pe.matmul(pc(bank2, p), pc(k, p), pc(q, p), start=True, stop=True)
                last.then_inc(S["att"], 1)
                f_q(n, npar)
                pe.wait_ge(S["w2_s"], done(i))
                pe.wait_ge(S["decay"], done(i))
                for p in range(NP):
                    last = pe.matmul(bank3[:, p:p + 1], pc(w2, p), ones[:], start=True, stop=True)
                last.then_inc(S["wsq"], 1)
                pe.wait_ge(S["wdec_s"], done(i))
                for p in range(NP):
                    last = pe.transpose(pc(bank4, p), pc(wdec, p), ident)
                last.then_inc(S["wdecT"], 1)
                f_k(n, npar)
                pe.wait_ge(S["siluv"], done(i))
                pe.wait_ge(S["lnw_s"], done(i))
                for p in range(NP):
                    last = pe.transpose(pc(bank3, p), pc(v, p), ident)
                last.then_inc(S["vT"], 1)
                pe.wait_ge(S["qk_s"], done(i))
                pe.wait_ge(S["wdec_tok_s"], done(i))
                for p in range(NP):
                    last = pe.matmul(pc(bank2, p), pc(qk, p), pc(wdec_tok, p), start=True, stop=True)
                last.then_inc(S["scores"], 1)
                f_decay_logits(n, npar)
                f_v(n, npar)
                pe.wait_ge(S["pdec_s"], done(i))
                pe.wait_ge(S["v_tok_s"], done(i))
                for p in range(NP):
                    last = pe.transpose(pc(bank3, p), pc(pdec, p), ident)
                last.then_inc(S["pdecT"], 1)
                f_w(n, npar)
                pe.wait_ge(S["pdec_chan_s"], done(i))
                for s0 in range(0, G, T):
                    rows = s0 % P
                    pe.matmul(bank2[rows:rows + T, s0 + T // 2:s0 + T], wdec[:, s0:s0 + T],
                              pdec_chan[:, s0 + T // 2:s0 + T], start=True, stop=True)
                    last = pe.matmul(bank2[rows:rows + T // 2, s0:s0 + T // 2], wdec[:, s0:s0 + T // 2],
                                     pdec_chan[:, s0:s0 + T // 2], start=True, stop=True)
                last.then_inc(S["pv"], 1)
                f_decays(n, npar)
                pe.wait_ge(S["mix_s"], done(i))
                pe.wait_ge(S["gate_th"], done(i))
                for p in range(NP):
                    last = pe.matmul(pc(bank5, p), pc(mix, p), pc(v_tok, p), start=True, stop=True)
                last.then_inc(S["o"], 1)
                pe.wait_ge(S["o_tok_s"], done(i))
                for p in range(NP):
                    last = pe.transpose(pc(bank2, p), pc(o_tok, p), ident)
                last.then_inc(S["oT"], 1)
                f_gate(n, npar)
                pe.wait_ge(S["o_chan_s"], done(i))
                for p in range(NP):
                    last = pe.matmul(outacc[p // 2][:, p % 2, :], pc(o_chan, p), Wo[:, bass.ts(h, HID)],
                                     start=False, stop=False, skip_group_check=True)
                last.then_inc(S["wo"], 1)

            def group_start(g):
                pe.wait_ge(group_out, g + 1)
                for n in range(2):
                    pe.matmul(outacc[n][:].rearrange("p a c -> p (a c)"), zeros[:, 0:P], zeros[:],
                              start=True, stop=False, skip_group_check=True)

            run_units(pe, front, merged, group_start=group_start)

        @block.scalar
        def _(act):
            prime(act, "scalar")
            act.wait_ge(consts_set, 4)

            def tap(n, par, bank, dst, col, x_step, conv_step, free_waits):
                act.wait_ge(S[x_step], done(n))
                for s, v_ in free_waits:
                    act.wait_ge(S[s], v_)
                c = W_CONV + TAPS * col + TAPS - 1
                act.activation(dst[:], bank[:], ACT.Copy, scale=hw[par][:, c:c + 1])\
                    .then_inc(S[conv_step], 1)

            def f_tapq(n, par):
                tap(n, par, bank0, q, 0, "xq", "tapq", [("att", before(n))])

            def f_tapk(n, par):
                tap(n, par, bank1, k, 1, "xk", "tapk", [("att", before(n))])

            def f_tapv(n, par):
                tap(n, par, bank0, v, 2, "xv", "tapv", [("vT", before(n))])

            def f_tapw(n, par):
                tap(n, par, bank1, w, 3, "xw", "tapw", [("w2_s", before(n)), ("wdec_s", before(n))])

            def f_log_sigmoid(n, par):
                act.wait_ge(S["gx"], done(n))
                act.wait_ge(S["glog_s"], before(n))
                act.activation(gtmp[:], bank4[:], ACT.Abs).then_inc(S["gabs"], 1)
                act.wait_ge(S["gabs"], done(n))
                act.activation(gtmp[:], gtmp[:], ACT.Exp, scale=-1.0).then_inc(S["gexp"], 1)
                act.wait_ge(S["gexp"], done(n))
                act.activation(gtmp[:], gtmp[:], ACT.Ln, bias=1.0).then_inc(S["gln"], 1)

            def f_decays(n, par):
                act.wait_ge(S["dtok"], done(n))
                act.wait_ge(S["pdec_s"], before(n))
                act.activation(expD[:], bank3[:], ACT.Exp).then_inc(S["decay"], 1)
                act.wait_ge(S["dchan"], done(n))
                act.wait_ge(S["wdec_s"], before(n))
                act.activation(expDneg[:], bank4[:], ACT.Exp, scale=-1.0).then_inc(S["ndecay"], 1)

            def f_silus(n, par):
                act.preload_act_table_set("silu_and_others")
                act.wait_ge(S["gate_x"], done(n))
                act.wait_ge(S["o_chan_s"], before(n))
                act.wait_ge(S["hbias_s"], done(n))
                act.activation(gate[:], bank5[:], ACT.Tanh, bias=hbias[:], scale=0.5).then_inc(S["gate_th"], 1)
                for t, c, s in ((q, "convq", "siluq"), (k, "convk", "siluk"), (v, "convv", "siluv"),
                                (w, "convw", "siluw")):
                    act.wait_ge(S[c], done(n, CONV))
                    act.activation(t[:], t[:], ACT.Silu).then_inc(S[s], 1)
                act.preload_act_table_set("natural_log_exp_and_others")

            def front(n, par):
                f_tapq(n, par)
                f_tapk(n, par)
                f_log_sigmoid(n, par)
                f_tapv(n, par)
                f_tapw(n, par)
                f_decays(n, par)
                f_silus(n, par)

            def merged(i, h, par):
                n, npar = i + 1, 1 - par
                act.wait_ge(S["wsq"], done(i))
                act.activation(lnw[:], bank3[:, 0:NP], ACT.Ln, bias=l2eps[:]).then_inc(S["lnw_s"], 1)
                act.wait_ge(S["lnw_s"], done(i))
                act.wait_ge(S["coef_s"], before(i))
                act.activation(rw[:], lnw[:], ACT.Exp, scale=-0.5).then_inc(S["rw_s"], 1)
                act.wait_ge(S["wdecT"], done(i))
                act.wait_ge(S["scores"], before(i))
                act.copy(wdec_tok[:], bank4[:]).then_inc(S["wdec_tok_s"], 1)
                f_tapq(n, npar)
                act.wait_ge(S["vT"], done(i))
                act.wait_ge(S["o"], before(i))
                act.copy(v_tok[:], bank3[:]).then_inc(S["v_tok_s"], 1)
                f_tapk(n, npar)
                act.wait_ge(S["nmax_s"], done(i))
                act.wait_ge(S["pdec_s"], before(i))
                act.wait_ge(S["Zeps_s"], before(i))
                for p in range(NP):
                    act.activation(pc(probs, p), pc(score, p), ACT.Exp, bias=nmax[:, p:p + 1], scale=SCALE,
                                   accum_out=Z[:, p:p + 1]).then_inc(S["exps"], 1)
                f_log_sigmoid(n, npar)
                act.wait_ge(S["pdecT"], done(i))
                act.wait_ge(S["pv"], before(i))
                act.copy(pdec_chan[:], bank3[:]).then_inc(S["pdec_chan_s"], 1)
                f_tapv(n, npar)
                act.wait_ge(S["o"], done(i))
                act.wait_ge(S["y_s"], before(i))
                for p in range(NP):
                    act.activation(pc(osq, p), pc(bank5, p), ACT.Square, accum_out=ssq[:, p:p + 1])\
                        .then_inc(S["osq_s"], 1)
                f_tapw(n, npar)
                act.wait_ge(S["y_s"], done(i))
                act.activation(lny[:], y[:], ACT.Ln).then_inc(S["lny_s"], 1)
                act.wait_ge(S["lny_s"], done(i))
                act.wait_ge(S["o_tok_s"], before(i))
                act.activation(rho[:], lny[:], ACT.Exp, scale=-0.5).then_inc(S["rho_s"], 1)
                f_decays(n, npar)
                f_silus(n, npar)

            run_units(act, front, merged)

        @block.vector
        def _(dve):
            prime(dve, "vector")
            dve.sem_inc(group_out, 1)
            dve.wait_ge(consts_set, 4)

            def conv(n, par, bank, dst, col, tap_step, conv_step):
                x3 = bank[:].rearrange("p (s t) -> p s t", s=NS)
                d3 = dst[:].rearrange("p (s t) -> p s t", s=NS)
                dve.wait_ge(S[tap_step], done(n))
                for shift in range(1, TAPS):
                    if shift > 1:
                        dve.wait_ge(S[conv_step], before(n, CONV) + shift - 1)
                    c = W_CONV + TAPS * col + TAPS - 1 - shift
                    dve.scalar_tensor_tensor(out=d3[:, :, shift:T], in0=x3[:, :, 0:T - shift],
                                             scalar=hw[par][:, c:c + 1], in1=d3[:, :, shift:T],
                                             op0=ALU.mult, op1=ALU.add).then_inc(S[conv_step], 1)

            def f_convq(n, par):
                conv(n, par, bank0, q, 0, "tapq", "convq")

            def f_convk(n, par):
                conv(n, par, bank1, k, 1, "tapk", "convk")

            def f_convv(n, par):
                conv(n, par, bank0, v, 2, "tapv", "convv")

            def f_convw(n, par):
                conv(n, par, bank1, w, 3, "tapw", "convw")

            def f_glog(n, par):
                dve.wait_ge(S["gln"], done(n))
                dve.wait_ge(S["dchan"], before(n))
                dve.scalar_tensor_tensor(out=glog[:], in0=bank4[:], scalar=0.0, in1=gtmp[:], op0=ALU.min,
                                         op1=ALU.subtract).then_inc(S["glog_s"], 1)

            def front(n, par):
                f_convq(n, par)
                f_convk(n, par)
                f_glog(n, par)
                f_convv(n, par)
                f_convw(n, par)

            def merged(i, h, par):
                n, npar = i + 1, 1 - par
                dve.wait_ge(S["rw_s"], done(i))
                dve.wait_ge(S["mix_s"], before(i))
                dve.tensor_tensor(coef[:], rw[:], beta_of(i), ALU.mult).then_inc(S["coef_s"], 1)
                dve.wait_ge(S["coef_s"], done(i))
                dve.wait_ge(S["att"], done(i))
                dve.wait_ge(S["scores"], before(i))
                for p in range(NP):
                    last = dve.scalar_tensor_tensor(out=pc(qk, p), in0=pc(bank2, p), scalar=coef[:, p:p + 1],
                                                    in1=causal, op0=ALU.mult, op1=ALU.mult)
                last.then_inc(S["qk_s"], 1)
                f_convq(n, npar)
                dve.wait_ge(S["scores"], done(i))
                dve.wait_ge(S["exps"], before(i, NP))
                dve.tensor_tensor(score[:], bank2[:], expD[:], ALU.mult).then_inc(S["score_s"], 1)
                dve.wait_ge(S["score_s"], done(i))
                dve.tensor_reduce(smax[:], pairs(score), AX.X, ALU.max).then_inc(S["smax_s"], 1)
                dve.wait_ge(S["smax_s"], done(i))
                dve.tensor_scalar(nmax[:], smax[:], -SCALE, None, ALU.mult).then_inc(S["nmax_s"], 1)
                f_convk(n, npar)
                dve.wait_ge(S["exps"], done(i, NP))
                dve.scalar_tensor_tensor(out=Zeps[:], in0=Z[:], scalar=4.0 * EPS, in1=Z[:], op0=ALU.mult,
                                         op1=ALU.mult).then_inc(S["Zeps_s"], 1)
                f_glog(n, npar)
                dve.wait_ge(S["pv"], done(i))
                dve.wait_ge(S["o"], before(i))
                for p in range(NP):
                    last = dve.scalar_tensor_tensor(out=pc(mix, p), in0=pc(bank2, p), scalar=coef[:, p:p + 1],
                                                    in1=causal, op0=ALU.mult, op1=ALU.mult)
                last.then_inc(S["mix_s"], 1)
                f_convv(n, npar)
                dve.wait_ge(S["osq_s"], done(i, NP))
                dve.wait_ge(S["lny_s"], before(i))
                dve.scalar_tensor_tensor(out=y[:], in0=ssq[:], scalar=4.0 / P, in1=Zeps[:], op0=ALU.mult,
                                         op1=ALU.add).then_inc(S["y_s"], 1)
                f_convw(n, npar)
                dve.wait_ge(S["rho_s"], done(i))
                dve.wait_ge(S["oT"], before(i))
                for p in range(NP):
                    last = dve.tensor_scalar(pc(o_tok, p), pc(bank5, p), rho[:, p:p + 1], None, ALU.mult)
                last.then_inc(S["o_tok_s"], 1)
                dve.wait_ge(S["oT"], done(i))
                dve.wait_ge(S["gate_th"], done(i))
                dve.wait_ge(S["wo"], before(i))
                dve.scalar_tensor_tensor(out=o_chan[:], in0=gate[:], scalar=1.0, in1=bank2[:], op0=ALU.add,
                                         op1=ALU.mult).then_inc(S["o_chan_s"], 1)

            def beta_of(i):
                return beta.rearrange("p g h q -> p (g h q)")[:, bass.ts(i, NP)]

            def group_end(g):
                dve.wait_ge(S["wo"], before(g * H + H))
                for m in range(2):
                    xs = x_all[:, bass.ds(g * NP + 2 * m, 2), :]
                    last = dve.tensor_tensor(xs, xs, outacc[m][:], ALU.add)
                last.then_inc(group_out, 1)

            run_units(dve, front, merged, group_end=group_end)


def context_block(nc, sems, ctx_all, ctxT, gqk, xT_pad, ident, load):
    with ExitStack() as ctx:
        def sem(name):
            return sems(name)

        banks = [ctx.enter_context(nc.psum_tensor(f"ctx_turned{k}", [P, G], F32)) for k in range(2)]
        gq_gk = ctx.enter_context(nc.sbuf_tensor("gq_gk", [P, 2], F32))
        loaded = sem("ctx_loaded")
        turned = sem("ctx_turned")
        kept = sem("ctx_kept")
        gqk_done = sem("gqk_done")
        padded = sem("ctx_padded")
        block = ctx.enter_context(nc.Block())

        @block.sync
        def _(sp):
            for dst, src in load:
                sp.dma_start(gq_gk[:] if dst is None else dst, src).then_inc(loaded, 16)

        @block.gpsimd
        def _(pool):
            pool.memset(ctxT[:, TOKENS:TOKENS + G], 0.0).then_inc(padded, 1)
            pool.memset(xT_pad, 0.0).then_inc(padded, 1)

        @block.tensor
        def _(pe):
            pe.wait_ge(loaded, 16 * len(load))
            for g in range(GROUPS):
                if g >= 2:
                    pe.wait_ge(kept, g - 1)
                for p in range(NP):
                    last = pe.transpose(banks[g % 2][:, p * P:(p + 1) * P], ctx_all[:, g * NP + p, :], ident)
                last.then_inc(turned, 1)

        @block.scalar
        def _(act):
            for g in range(GROUPS):
                act.wait_ge(turned, g + 1)
                act.copy(ctxT[:, g * G:(g + 1) * G], banks[g % 2][:]).then_inc(kept, 1)

        @block.vector
        def _(dve):
            dve.wait_ge(loaded, 16 * len(load))
            dve.tensor_tensor(gqk[:], gq_gk[:, 0:1], gq_gk[:, 1:2], ALU.mult).then_inc(gqk_done, 1)


def cross_block(nc, sems, w_heads, x_all, xT_all, ctxT, gqk, Wo, ident):
    with ExitStack() as ctx:
        def sb(name, shape, dt=F32):
            return ctx.enter_context(nc.sbuf_tensor(f"x_{name}", shape, dt))

        def psum(name, shape, dt=F32):
            return ctx.enter_context(nc.psum_tensor(f"x_{name}", shape, dt))

        def sem(name):
            return sems(f"x_{name}")

        hw = [sb(f"head_weights{i}", [P, X_HEAD]) for i in range(2)]
        ctxg = sb("ctxg", [P, G])
        q = sb("q_chan", [P, G])
        q2 = sb("q2", [P, G])
        ksq = sb("ksq", [P, G])
        k_tok = sb("k_tok", [P, G])
        k = sb("k_chan", [P, G])
        v_tok = sb("v_tok", [P, G])
        score = sb("score", [P, NP, T])
        probs = sb("probs", [P, NP, T])
        wide = sb("wide", [P, NP, P])
        wide_chan = sb("wide_chan", [P, G])
        o_chan = sb("o_chan", [P, G])
        ones = sb("ones", [P, 1])
        eps = sb("eps", [P, 1])
        zeros = sb("zeros", [P, G], BF16)
        ssk = sb("ssk", [P, NP])
        ln2 = sb("ln2", [P, 2, NP])
        rk_rq = sb("rk_rq", [P, 2, NP])
        rq = sb("rq", [P, NP])
        smax = sb("smax", [P, NP])
        Z = sb("Z", [P, NP])
        rZ = sb("rZ", [P, NP])
        bank0, bank1, bank2, bank3, bank4, bank5 = (psum(f"bank{n}", [P, G]) for n in range(6))
        outacc = [psum(f"outacc{n}", [P, 2, HID]) for n in range(2)]

        primed = {
            "tensor": "xq xk xv qss kT scores probsT o wo",
            "scalar": "q_s q2_s ksq_s lnk lnq rkq exps wide_chan_s o_chan_s v_s k_s",
            "vector": "score_s smax_s sub_s Z_s rZ_s wide_s k_tok_s rq_s",
            "gpsimd": "ctxg_s",
        }
        S = {n: sem(n) for names in primed.values() for n in names.split()}
        weights_in = [sem(f"weights_in{i}") for i in range(2)]
        consts_set = sem("consts_set")
        group_out = sem("group_out")
        block = ctx.enter_context(nc.Block())

        def prime(eng, who):
            for n in primed[who].split():
                eng.sem_inc(S[n], 1)

        def done(n, times=1):
            return times * (n + 1) + 1

        def before(n, times=1):
            return times * n + 1

        def run_units(eng, front, merged, group_start=None, group_end=None):
            front(0, 0)
            with eng.Fori(0, GROUPS) as g:
                if group_start is not None:
                    group_start(g)
                with eng.Fori(0, H // 2) as j:
                    for par in range(2):
                        merged(g * H + j * 2 + par, j * 2 + par, par)
                if group_end is not None:
                    group_end(g)

        def pc(t, p):
            return t[:, p * P:(p + 1) * P]

        def over(t, n):
            return t.unsqueeze(2).broadcast_to([P, NP, n])

        @block.sync
        def _(sp):
            def load(n, h, par):
                sp.dma_start(hw[par][:], w_heads[h]).then_inc(weights_in[par], 16)

            load(0, 0, 0)
            load(1, 1, 1)
            with sp.Fori(0, UNITS // 2 - 1) as m:
                for par in range(2):
                    n = 2 * m + par
                    sp.wait_ge(S["xv"], done(n))
                    load(n + 2, (n + 2) % H, par)
            sp.wait_ge(S["xv"], done(UNITS - 2))
            load(UNITS, 0, 0)

        @block.gpsimd
        def _(pool):
            prime(pool, "gpsimd")
            pool.memset(ones[:], 1.0).then_inc(consts_set, 1)
            pool.memset(eps[:], EPS).then_inc(consts_set, 1)
            pool.memset(zeros[:], 0.0).then_inc(consts_set, 1)
            pool.memset(wide[:], 0.0).then_inc(consts_set, 1)

            def front(n, par):
                pool.wait_ge(S["xv"], before(n))
                pool.tensor_copy(ctxg[:], ctxT[:, bass.ts(n // H, G)]).then_inc(S["ctxg_s"], 1)

            def merged(i, h, par):
                front(i + 1, 1 - par)

            run_units(pool, front, merged)

        @block.tensor
        def _(pe):
            prime(pe, "tensor")
            pe.wait_ge(consts_set, 4)

            def f_q(n, par):
                pe.wait_ge(weights_in[par], 16 * (n // 2 + 1))
                pe.wait_ge(S["lnq"], before(n))
                for kk in range(KH):
                    last = pe.matmul(bank0[:], hw[par][:, X_Q + kk * P:X_Q + (kk + 1) * P],
                                     xT_all[:, kk, bass.ts(n // H, G)], start=(kk == 0), stop=(kk == KH - 1))
                last.then_inc(S["xq"], 1)

            def f_k(n, par):
                pe.wait_ge(S["ctxg_s"], done(n))
                pe.wait_ge(S["k_tok_s"], before(n))
                for p in range(NP):
                    last = pe.matmul(pc(bank1, p), pc(ctxg, p), hw[par][:, X_K:X_K + P], start=True, stop=True)
                last.then_inc(S["xk"], 1)

            def f_v(n, par):
                pe.wait_ge(S["v_s"], before(n))
                for p in range(NP):
                    last = pe.matmul(pc(bank4, p), pc(ctxg, p), hw[par][:, X_V:X_V + P], start=True, stop=True)
                last.then_inc(S["xv"], 1)

            def f_qss(n, par):
                pe.wait_ge(S["q2_s"], done(n))
                pe.wait_ge(S["q_s"], done(n))
                for p in range(NP):
                    last = pe.matmul(bank0[:, p:p + 1], pc(q2, p), ones[:], start=True, stop=True)
                last.then_inc(S["qss"], 1)

            def f_kT(n, par):
                pe.wait_ge(S["k_tok_s"], done(n))
                pe.wait_ge(S["k_s"], before(n))
                for p in range(NP):
                    last = pe.transpose(pc(bank3, p), pc(k_tok, p), ident)
                last.then_inc(S["kT"], 1)

            def front(n, par):
                f_q(n, par)
                f_k(n, par)
                f_v(n, par)
                f_qss(n, par)
                f_kT(n, par)

            def merged(i, h, par):
                n, npar = i + 1, 1 - par
                pe.wait_ge(S["k_s"], done(i))
                pe.wait_ge(S["q_s"], done(i))
                pe.wait_ge(S["o_chan_s"], before(i))
                for p in range(NP):
                    for half in range(2):
                        at = slice(p * P + half * T, p * P + (half + 1) * T)
                        last = pe.matmul(bank2[half * T:(half + 1) * T, p * T:(p + 1) * T], q[:, at], k[:, at],
                                         start=True, stop=True)
                last.then_inc(S["scores"], 1)
                f_q(n, npar)
                f_k(n, npar)
                pe.wait_ge(S["wide_s"], done(i, 2))
                pe.wait_ge(S["wide_chan_s"], before(i))
                for p in range(NP):
                    last = pe.transpose(pc(bank5, p), wide[:, p, :], ident)
                last.then_inc(S["probsT"], 1)
                f_v(n, npar)
                f_qss(n, npar)
                pe.wait_ge(S["wide_chan_s"], done(i))
                for p in range(NP):
                    last = pe.matmul(pc(bank2, p), pc(v_tok, p), pc(wide_chan, p), start=True, stop=True)
                last.then_inc(S["o"], 1)
                f_kT(n, npar)
                pe.wait_ge(S["o_chan_s"], done(i))
                for p in range(NP):
                    last = pe.matmul(outacc[p // 2][:, p % 2, :], pc(o_chan, p), Wo[:, bass.ts(h, HID)],
                                     start=False, stop=False, skip_group_check=True)
                last.then_inc(S["wo"], 1)

            def group_start(g):
                pe.wait_ge(group_out, g + 1)
                for n in range(2):
                    pe.matmul(outacc[n][:].rearrange("p a c -> p (a c)"), zeros[:, 0:P], zeros[:],
                              start=True, stop=False, skip_group_check=True)

            run_units(pe, front, merged, group_start=group_start)

        @block.scalar
        def _(act):
            act.preload_act_table_set("natural_log_exp_and_others")
            prime(act, "scalar")
            act.wait_ge(consts_set, 4)

            def f_q(n, par):
                act.wait_ge(S["xq"], done(n))
                act.wait_ge(S["scores"], before(n))
                act.copy(q[:], bank0[:]).then_inc(S["q_s"], 1)
                act.wait_ge(S["qss"], before(n))
                act.activation(q2[:], bank0[:], ACT.Square).then_inc(S["q2_s"], 1)

            def f_ksq(n, par):
                act.wait_ge(S["xk"], done(n))
                act.wait_ge(S["lnk"], before(n))
                for p in range(NP):
                    act.activation(pc(ksq, p), pc(bank1, p), ACT.Square, accum_out=ssk[:, p:p + 1])\
                        .then_inc(S["ksq_s"], 1)

            def f_norms(n, par):
                act.wait_ge(S["ksq_s"], done(n, NP))
                act.wait_ge(S["rkq"], before(n))
                act.activation(ln2[:, 0, :], ssk[:], ACT.Ln, bias=eps[:], scale=1.0 / P).then_inc(S["lnk"], 1)
                act.wait_ge(S["qss"], done(n))
                act.activation(ln2[:, 1, :], bank0[:, 0:NP], ACT.Ln, bias=eps[:], scale=1.0 / P)\
                    .then_inc(S["lnq"], 1)
                act.wait_ge(S["lnk"], done(n))
                act.wait_ge(S["lnq"], done(n))
                act.wait_ge(S["k_tok_s"], before(n))
                act.wait_ge(S["rq_s"], before(n))
                act.activation(rk_rq[:], ln2[:], ACT.Exp, scale=-0.5).then_inc(S["rkq"], 1)

            def f_v(n, par):
                act.wait_ge(S["xv"], done(n))
                act.wait_ge(S["o"], before(n))
                act.copy(v_tok[:], bank4[:]).then_inc(S["v_s"], 1)

            def f_k(n, par):
                act.wait_ge(S["kT"], done(n))
                act.wait_ge(S["scores"], before(n))
                act.activation(k[:], bank3[:], ACT.Copy, scale=gqk[:]).then_inc(S["k_s"], 1)

            def front(n, par):
                f_q(n, par)
                f_ksq(n, par)
                f_norms(n, par)
                f_v(n, par)
                f_k(n, par)

            def merged(i, h, par):
                n, npar = i + 1, 1 - par
                act.wait_ge(S["sub_s"], done(i))
                act.wait_ge(S["wide_s"], before(i, 2))
                act.activation(probs[:], score[:], ACT.Exp, scale=SCALE).then_inc(S["exps"], 1)
                f_q(n, npar)
                f_ksq(n, npar)
                act.wait_ge(S["probsT"], done(i))
                act.wait_ge(S["o"], before(i))
                act.copy(wide_chan[:], bank5[:]).then_inc(S["wide_chan_s"], 1)
                f_norms(n, npar)
                act.wait_ge(S["o"], done(i))
                act.wait_ge(S["wo"], before(i))
                act.copy(o_chan[:], bank2[:]).then_inc(S["o_chan_s"], 1)
                f_v(n, npar)
                f_k(n, npar)

            run_units(act, front, merged)

        @block.vector
        def _(dve):
            prime(dve, "vector")
            dve.sem_inc(group_out, 1)
            dve.wait_ge(consts_set, 4)

            def front(n, par):
                dve.wait_ge(S["rkq"], done(n))
                dve.wait_ge(S["score_s"], before(n))
                dve.tensor_copy(rq[:], rk_rq[:, 1, :]).then_inc(S["rq_s"], 1)
                dve.wait_ge(S["kT"], before(n))
                for p in range(NP):
                    last = dve.tensor_scalar(pc(k_tok, p), pc(bank1, p), rk_rq[:, 0, p:p + 1], None, ALU.mult)
                last.then_inc(S["k_tok_s"], 1)

            def merged(i, h, par):
                s3 = bank2[:, 0:NP * T].rearrange("p (q t) -> p q t", q=NP)
                dve.wait_ge(S["scores"], done(i))
                dve.wait_ge(S["rq_s"], done(i))
                dve.wait_ge(S["exps"], before(i))
                dve.tensor_tensor(score[:], s3, over(rq[:], T), ALU.mult).then_inc(S["score_s"], 1)
                dve.wait_ge(S["score_s"], done(i))
                dve.tensor_reduce(smax[:], score[:], AX.X, ALU.max).then_inc(S["smax_s"], 1)
                dve.wait_ge(S["smax_s"], done(i))
                dve.tensor_tensor(score[:], score[:], over(smax[:], T), ALU.subtract).then_inc(S["sub_s"], 1)
                dve.wait_ge(S["exps"], done(i))
                dve.tensor_reduce(Z[:], probs[:], AX.X, ALU.add).then_inc(S["Z_s"], 1)
                dve.wait_ge(S["Z_s"], done(i))
                dve.reciprocal(rZ[:], Z[:]).then_inc(S["rZ_s"], 1)
                dve.wait_ge(S["rZ_s"], done(i))
                dve.wait_ge(S["probsT"], before(i))
                for half in range(2):
                    rows = slice(half * T, (half + 1) * T)
                    dve.tensor_tensor(wide[rows, :, half * T:(half + 1) * T], probs[rows, :, :],
                                      over(rZ[:], T)[rows], ALU.mult).then_inc(S["wide_s"], 1)
                front(i + 1, 1 - par)

            def group_end(g):
                dve.wait_ge(S["wo"], before(g * H + H))
                for m in range(2):
                    xs = x_all[:, bass.ds(g * NP + 2 * m, 2), :]
                    last = dve.tensor_tensor(xs, xs, outacc[m][:], ALU.add)
                last.then_inc(group_out, 1)

            run_units(dve, front, merged, group_end=group_end)


def experts_block(nc, sems, x_all, xT_all, gate_w, experts, expert_b, lower, ident, load, out_view):
    EP = E // 2
    RING = 4
    with ExitStack() as ctx:
        def sb(name, shape, dt=F32):
            return ctx.enter_context(nc.sbuf_tensor(f"e_{name}", shape, dt))

        def psum(name, shape, dt=F32):
            return ctx.enter_context(nc.psum_tensor(f"e_{name}", shape, dt))

        def sem(name):
            return sems(f"e_{name}")

        xg = [sb(f"xg{i}", [P, KH, G]) for i in range(2)]
        logits = sb("logits", [P, NP, E])
        above = sb("above", [P, NP, E, E])
        ties = sb("ties", [P, NP, E, E])
        rank = sb("rank", [P, NP, E])
        top = sb("top", [P, NP])
        shifted = sb("shifted", [P, NP, E])
        ex = sb("ex", [P, NP, E])
        chosen = sb("chosen", [P, NP, E])
        Z = sb("Z", [P, NP])
        rZ = sb("rZ", [P, NP])
        gates = sb("gates", [P, NP, E])
        gatesT = sb("gatesT", [E, G])
        y = [psum(f"y{i}", [P, 2, HID]) for i in range(RING)]
        small = psum("small", [P, NP, E])
        gT = psum("gT", [E, G])
        bias = [psum(f"bias{i}", [P, 2, HID]) for i in range(2)]

        primed = {
            "tensor": "logit gatesT_x bias_x y_x",
            "scalar": "exps gatesT_s",
            "vector": "logits_s above_s ties_s tied_s beats_s rank_s top_s shifted_s chosen_s Z_s rZ_s gates_s "
                      "biased y_s",
            "gpsimd": "xg_s",
        }
        S = {n: sem(n) for names in primed.values() for n in names.split()}
        loaded = sem("loaded")
        stored = sem("stored")
        block = ctx.enter_context(nc.Block())
        YS = NP * EP

        def prime(eng, who):
            for n in primed[who].split():
                eng.sem_inc(S[n], 1)

        def done(n, times=1):
            return times * (n + 1) + 1

        def before(n, times=1):
            return times * n + 1

        def over(t, n):
            return t.unsqueeze(2).broadcast_to([P, NP, n])

        @block.sync
        def _(sp):
            for dst, src in load:
                sp.dma_start(dst, src).then_inc(loaded, 16)
            with sp.Fori(0, GROUPS) as g:
                sp.wait_ge(S["y_s"], done(g, 2 * YS))
                sp.dma_start(out_view[:, bass.ds(g * NP, NP), :], x_all[:, bass.ds(g * NP, NP), :])\
                    .then_inc(stored, 16)
            sp.wait_ge(stored, 16 * GROUPS)

        @block.gpsimd
        def _(pool):
            prime(pool, "gpsimd")
            with pool.Fori(0, GROUPS // 2) as m:
                for par in range(2):
                    g = 2 * m + par
                    pool.wait_ge(S["y_x"], before(g, YS))
                    pool.tensor_copy(xg[par][:], xT_all[:, :, bass.ts(g, G)]).then_inc(S["xg_s"], 1)

        @block.tensor
        def _(pe):
            prime(pe, "tensor")
            pe.wait_ge(loaded, 16 * len(load))
            with pe.Fori(0, GROUPS // 2) as m:
                for par in range(2):
                    g = 2 * m + par
                    pe.wait_ge(S["xg_s"], done(g))
                    pe.wait_ge(S["logits_s"], before(g))
                    for p in range(NP):
                        for k in range(KH):
                            last = pe.matmul(small[:, p, :], xg[par][:, k, p * P:(p + 1) * P], gate_w[:, k, :],
                                             start=(k == 0), stop=(k == KH - 1))
                    last.then_inc(S["logit"], 1)
                    for p in range(NP):
                        for ep in range(EP):
                            u = p * EP + ep
                            pe.wait_ge(S["y_s"], before(g, 2 * YS) + 2 * (u + 1 - RING) if u >= RING
                                       else before(g, 2 * YS))
                            for k in range(KH):
                                last = pe.matmul(y[u % RING][:].rearrange("p a c -> p (a c)"),
                                                 xg[par][:, k, p * P:(p + 1) * P],
                                                 experts[:, k, 2 * ep:2 * ep + 2, :].rearrange("p a c -> p (a c)"),
                                                 start=(k == 0), stop=(k == KH - 1))
                            last.then_inc(S["y_x"], 1)
                            if u == RING - 1:
                                pe.wait_ge(S["gates_s"], done(g))
                                for pp in range(NP):
                                    last = pe.transpose(gT[:, pp * P:(pp + 1) * P], gates[:, pp, :], ident)
                                last.then_inc(S["gatesT_x"], 1)
                                pe.wait_ge(S["gatesT_s"], done(g))
                                pe.wait_ge(S["biased"], before(g))
                                for pp in range(NP):
                                    last = pe.matmul(bias[pp // 2][:, pp % 2, :], gatesT[:, pp * P:(pp + 1) * P],
                                                     expert_b[:], start=True, stop=True)
                                last.then_inc(S["bias_x"], 1)

        @block.scalar
        def _(act):
            prime(act, "scalar")
            with act.Fori(0, GROUPS) as g:
                act.wait_ge(S["shifted_s"], done(g))
                act.wait_ge(S["chosen_s"], before(g))
                act.activation(ex[:], shifted[:], ACT.Exp).then_inc(S["exps"], 1)
                act.wait_ge(S["gatesT_x"], done(g))
                act.wait_ge(S["bias_x"], before(g))
                act.copy(gatesT[:], gT[:]).then_inc(S["gatesT_s"], 1)

        @block.vector
        def _(dve):
            prime(dve, "vector")
            dve.wait_ge(loaded, 16 * len(load))
            theirs = logits[:].unsqueeze(2).broadcast_to([P, NP, E, E])
            own = logits[:].unsqueeze(3).broadcast_to([P, NP, E, E])
            earlier = lower.rearrange("p (a b) -> p a b", a=E).unsqueeze(1).broadcast_to([P, NP, E, E])
            with dve.Fori(0, GROUPS) as g:
                dve.wait_ge(S["logit"], done(g))
                dve.wait_ge(S["shifted_s"], before(g))
                dve.tensor_copy(logits[:], small[:]).then_inc(S["logits_s"], 1)
                dve.wait_ge(S["logits_s"], done(g))
                dve.tensor_tensor(above[:], theirs, own, ALU.is_gt).then_inc(S["above_s"], 1)
                dve.tensor_tensor(ties[:], theirs, own, ALU.is_equal).then_inc(S["ties_s"], 1)
                dve.wait_ge(S["ties_s"], done(g))
                dve.tensor_tensor(ties[:], ties[:], earlier, ALU.mult).then_inc(S["tied_s"], 1)
                dve.wait_ge(S["tied_s"], done(g))
                dve.wait_ge(S["above_s"], done(g))
                dve.tensor_tensor(above[:], above[:], ties[:], ALU.add).then_inc(S["beats_s"], 1)
                dve.wait_ge(S["beats_s"], done(g))
                dve.tensor_reduce(rank[:], above[:], AX.X, ALU.add).then_inc(S["rank_s"], 1)
                dve.tensor_reduce(top[:], logits[:], AX.X, ALU.max).then_inc(S["top_s"], 1)
                dve.wait_ge(S["top_s"], done(g))
                dve.wait_ge(S["exps"], before(g))
                dve.tensor_tensor(shifted[:], logits[:], over(top[:], E), ALU.subtract).then_inc(S["shifted_s"], 1)
                dve.wait_ge(S["exps"], done(g))
                dve.wait_ge(S["rank_s"], done(g))
                dve.scalar_tensor_tensor(out=chosen[:], in0=rank[:], scalar=TOPK - 0.5, in1=ex[:], op0=ALU.is_lt,
                                         op1=ALU.mult).then_inc(S["chosen_s"], 1)
                dve.wait_ge(S["chosen_s"], done(g))
                dve.tensor_reduce(Z[:], chosen[:], AX.X, ALU.add).then_inc(S["Z_s"], 1)
                dve.wait_ge(S["Z_s"], done(g))
                dve.reciprocal(rZ[:], Z[:]).then_inc(S["rZ_s"], 1)
                dve.wait_ge(S["rZ_s"], done(g))
                dve.wait_ge(S["bias_x"], before(g))
                dve.tensor_tensor(gates[:], chosen[:], over(rZ[:], E), ALU.mult).then_inc(S["gates_s"], 1)
                dve.wait_ge(S["gates_s"], done(g))
                for p in range(NP):
                    xp = x_all[:, g * NP + p, :]
                    for ex_ in range(E):
                        u = p * EP + ex_ // 2
                        dve.wait_ge(S["y_x"], before(g, YS) + u + 1)
                        if p + ex_ > 0:
                            dve.wait_ge(S["y_s"], before(g, 2 * YS) + p * E + ex_)
                        dve.scalar_tensor_tensor(out=xp, in0=y[u % RING][:, ex_ % 2, :],
                                                 scalar=gates[:, p, ex_:ex_ + 1], in1=xp, op0=ALU.mult,
                                                 op1=ALU.add).then_inc(S["y_s"], 1)
                    if p == 0:
                        dve.wait_ge(S["bias_x"], done(g))
                        dve.wait_ge(S["y_s"], before(g, 2 * YS) + E)
                        for m in range(2):
                            xs = x_all[:, bass.ds(g * NP + 2 * m, 2), :]
                            last = dve.tensor_tensor(xs, xs, bias[m][:], ALU.add)
                        last.then_inc(S["biased"], 1)
                        dve.wait_ge(S["biased"], done(g))


def decoder_layer(nc, ins, outs):
    with ExitStack() as ctx:
        def sb(name, shape, dt=F32):
            return ctx.enter_context(nc.sbuf_tensor(name, shape, dt))

        x_all = sb("x_all", [P, PAIRS, HID])
        cst = sb("cst", [P, 3 * P + E * E])
        lower = cst[:, 3 * P:3 * P + E * E]
        ident, span, causal = cst[:, 0:P], cst[:, P:2 * P], cst[:, 2 * P:3 * P]
        x_view = ins["x"].rearrange("b t c -> (b t) c").rearrange("(q p) c -> p q c", p=P)
        o_view = outs[0].rearrange("b t c -> (b t) c").rearrange("(q p) c -> p q c", p=P)

        with ExitStack() as stage:
            sems = stage.enter_context(stage_semaphores(nc))

            def st(name, shape, dt=F32):
                return stage.enter_context(nc.sbuf_tensor(name, shape, dt))

            xT_all = st("xT_all", [P, KH, TOKENS + G])
            f1T = st("f1T", [P, TOKENS + G])
            g1T = st("g1T", [P, TOKENS + G])
            beta = st("beta", [P, GROUPS, H, NP])
            Wf1g1 = st("Wf1g1", [P, KH, 2, P])
            Wb = st("Wb", [P, KH, H])
            Wo = st("Wo", [P, H * HID])
            norm_w = st("norm_w", [P, 1])
            layernorm_block(nc, sems, "ln1", x_all, xT_all, ident, load=[
                (cst[:], ins["consts"]), (x_all[:], x_view), (Wf1g1[:], ins["Wf1g1"]), (Wb[:], ins["Wb"]),
                (norm_w[:], ins["norm_w"]), (Wo[:], ins["Wo"])])
            lowrank_block(nc, sems, xT_all, f1T, g1T, beta[:], Wf1g1, Wb, ident, None)
            wo_scaled = sems("wo_scaled")
            with nc.Block() as block:
                @block.vector
                def _(dve):
                    dve.tensor_scalar(Wo[:], Wo[:], norm_w[:], None, ALU.mult).then_inc(wo_scaled, 1)

                @block.gpsimd
                def _(pool):
                    pool.memset(xT_all[:, :, TOKENS:TOKENS + G], 0.0).then_inc(wo_scaled, 1)
                    pool.memset(f1T[:, TOKENS:TOKENS + G], 0.0).then_inc(wo_scaled, 1)
                    pool.memset(g1T[:, TOKENS:TOKENS + G], 0.0).then_inc(wo_scaled, 1)
            gsa_block(nc, sems, ins["w_heads"], x_all, xT_all, f1T, g1T, beta[:], Wo, (ident, span, causal))
        with ExitStack() as stage:
            sems = stage.enter_context(stage_semaphores(nc))

            def st(name, shape, dt=F32):
                return stage.enter_context(nc.sbuf_tensor(name, shape, dt))

            xT_all = st("xT2_all", [P, KH, TOKENS + G])
            ctxT = st("ctxT", [P, TOKENS + G])
            ctx_all = st("ctx_all", [P, PAIRS, CDIM])
            gqk = st("gqk", [P, 1])
            xWo = st("xWo", [P, H * HID])
            c_view = ins["ctx"].rearrange("b t c -> (b t) c").rearrange("(q p) c -> p q c", p=P)
            layernorm_block(nc, sems, "ln2", x_all, xT_all, ident)
            context_block(nc, sems, ctx_all, ctxT, gqk, xT_all[:, :, TOKENS:TOKENS + G], ident,
                          [(ctx_all[:], c_view), (None, ins["gq_gk"]), (xWo[:], ins["xWo"])])
            cross_block(nc, sems, ins["x_heads"], x_all, xT_all, ctxT, gqk, xWo, ident)
        with ExitStack() as stage:
            sems = stage.enter_context(stage_semaphores(nc))

            def st(name, shape, dt=F32):
                return stage.enter_context(nc.sbuf_tensor(name, shape, dt))

            xT_all = st("xT3_all", [P, KH, TOKENS])
            gate_w = st("gate_w", [P, KH, E])
            experts = st("experts", [P, KH, E, HID])
            expert_b = st("expert_b", [E, HID])
            layernorm_block(nc, sems, "ln3", x_all, xT_all, ident)
            experts_block(nc, sems, x_all, xT_all, gate_w, experts, expert_b, lower, ident,
                          [(gate_w[:], ins["gate_w"]), (experts[:], ins["experts"]), (expert_b[:], ins["expert_b"])],
                          o_view)


def layout(inputs):
    a = {n: np.ascontiguousarray(v) for n, v in inputs.items()}

    def by_head(w):
        rows = w.shape[0]
        return w.reshape(rows // P, P, H, P).transpose(2, 1, 0, 3).reshape(H, P, -1)

    conv = np.stack([a[f"L0_attn_c{n}"].reshape(H, P, TAPS) for n in "qkv"] +
                    [a["L0_attn_cv"].reshape(H, P, TAPS)], axis=2).reshape(H, P, 4 * TAPS)
    w_heads = np.concatenate(
        [by_head(a[f"L0_attn_W{n}"]) for n in "qkvw"] + [by_head(a["L0_attn_Wf2"]), by_head(a["L0_attn_Wg2"]),
         conv, a["L0_attn_bg2"].reshape(H, P, 1)], axis=2)
    f1g1 = np.stack([a["L0_attn_Wf1"].reshape(KH, P, P), a["L0_attn_Wg1"].reshape(KH, P, P)], axis=2)
    return {
        "x": a["x"],
        "consts": shape_constants(),
        "w_heads": w_heads,
        "Wf1g1": f1g1.transpose(1, 0, 2, 3),
        "Wb": a["L0_attn_Wb"].reshape(KH, P, H).transpose(1, 0, 2),
        "norm_w": a["L0_attn_norm_w"].reshape(P, 1),
        "ctx": a["ctx_1024"],
        "x_heads": np.concatenate([by_head(a[f"L0_xattn_W{n}"]) for n in "qkv"], axis=2),
        "gq_gk": np.stack([a["L0_xattn_gq"], a["L0_xattn_gk"]], axis=1),
        "xWo": a["L0_xattn_Wo"].reshape(H, P, HID).transpose(1, 0, 2).reshape(P, H * HID),
        "gate_w": a["L0_ffn_gate_w"].T.reshape(KH, P, E).transpose(1, 0, 2),
        "experts": a["L0_ffn_expert_w"].reshape(E, KH, P, HID).transpose(2, 1, 0, 3),
        "expert_b": a["L0_ffn_expert_b"],
        "Wo": a["L0_attn_Wo"].reshape(H, P, HID).transpose(1, 0, 2).reshape(P, H * HID),
    }


def kernel(**inputs):
    import concourse.bacc as _bacc
    from concourse.bass_utils import run_bass_kernel_spmd as _run

    nc = _bacc.Bacc("TRN2", target_bir_lowering=False, num_devices=1)
    arrays, aps = {}, {}
    for name, a in layout(inputs).items():
        a = np.ascontiguousarray(a)
        arrays[f"in_{name}"] = a
        aps[name] = nc.dram_tensor(f"in_{name}", a.shape, mybir.dt.from_np(a.dtype), kind="ExternalInput").ap()
    out = nc.dram_tensor("out_0", (B, T, HID), F32, kind="ExternalOutput").ap()
    decoder_layer(nc, aps, [out])
    r = _run(nc, [arrays], core_ids=[0])
    return r.results[0]["out_0"]
```

```python
from contextlib import ExitStack, contextmanager

import numpy as np

import concourse.bass as bass
from concourse import mybir

F32 = mybir.dt.float32
BF16 = mybir.dt.bfloat16
ALU = mybir.AluOpType
ACT = mybir.ActivationFunctionType
AX = mybir.AxisListType

P = 128
B, T, HID = 32, 64, 256
TOKENS = B * T
CDIM = 128
H = 16
KH = HID // P
PAIRS = TOKENS // P
G = 512
NP = G // P
NS = G // T
GROUPS = TOKENS // G
UNITS = GROUPS * H
TAPS = 4
E = 8
TOPK = 2
EPS = 1e-5
L2EPS = 1e-6
SCALE = float(P) ** -0.5
FAR = float(np.exp(70.0))
HALVES = [T >> n for n in range(1, 7)]
LEVELS = len(HALVES) + 1

W_Q, W_K, W_V, W_W = (n * KH * P for n in range(4))
W_F2 = 4 * KH * P
W_G2 = W_F2 + P
W_CONV = W_G2 + P
W_BIAS = W_CONV + 4 * TAPS
W_HEAD = W_BIAS + 1
X_Q, X_K, X_V = 0, KH * P, KH * P + P
X_HEAD = KH * P + 2 * P


def shape_constants():
    s, t = np.meshgrid(np.arange(P), np.arange(P), indexing="ij")
    same = (s // T) == (t // T)
    mid = T // 2
    after = same & (s % T >= mid) & (s <= t)
    before = same & (s % T < mid) & (s > t)
    span = after.astype(np.float32) - before.astype(np.float32)
    causal = (same & (s <= t)).astype(np.float32)
    earlier = np.tril(np.ones((E, E), np.float32), -1).reshape(1, E * E).repeat(P, axis=0)
    return np.concatenate([np.eye(P, dtype=np.float32), span, causal, earlier], axis=1)


def level_tables():
    s, t = np.meshgrid(np.arange(P), np.arange(P), indexing="ij")
    tables = []
    for c in HALVES:
        same = (s // (2 * c)) == (t // (2 * c))
        s_late, t_late = (s // c) % 2 == 1, (t // c) % 2 == 1
        sums = same & ((t_late & s_late & (s <= t)) | (~t_late & ~s_late & (s > t)))
        tables.append(np.concatenate([sums, same & ~s_late & t_late], axis=1))
    tables.append(np.concatenate([np.zeros((P, P), bool), np.eye(P, dtype=bool)], axis=1))
    return np.stack(tables).astype(np.float32)


@contextmanager
def stage_semaphores(nc):
    with ExitStack() as ctx:
        used = []

        def sem(name):
            used.append(ctx.enter_context(nc.semaphore(name)))
            return used[-1]

        yield sem
        with nc.Block() as block:
            @block.sync
            def _(sp):
                for s in used:
                    sp.sem_clear(s)


def layernorm_block(nc, sems, tag, x_all, xT_all, ident, load=None):
    with ExitStack() as ctx:
        def sb(name, shape, dt=F32):
            return ctx.enter_context(nc.sbuf_tensor(f"{tag}_{name}", shape, dt))

        def sem(name):
            return sems(f"{tag}_{name}")

        stats = sb("stats", [P, PAIRS, 6])
        moments = sb("moments", [P, PAIRS, 2])
        eps = sb("eps", [P, 1])
        std = sb("std", [P, PAIRS])
        rstd = sb("rstd", [P, PAIRS])
        xn = sb("xn", [P, 2, NP, HID])
        turned = [ctx.enter_context(nc.psum_tensor(f"{tag}_turned{k}", [P, G], F32)) for k in range(2 * KH)]
        loaded = sem("loaded")
        eps_set = sem("eps_set")
        stats_done = sem("stats_done")
        moments_done = sem("moments_done")
        std_done = sem("std_done")
        rstd_done = sem("rstd_done")
        xn_done = sem("xn_done")
        turned_done = sem("turned_done")
        kept = sem("kept")
        block = ctx.enter_context(nc.Block())

        @block.sync
        def _(sp):
            if load is not None:
                for dst, src in load:
                    sp.dma_start(dst, src).then_inc(loaded, 16)

        @block.vector
        def _(dve):
            dve.memset(eps[:], EPS).then_inc(eps_set, 1)
            if load is not None:
                dve.wait_ge(loaded, 16 * len(load))
            for p in range(PAIRS):
                dve.bn_stats(stats[:, p, :], x_all[:, p, :]).then_inc(stats_done, 1)
            for p in range(PAIRS):
                dve.wait_ge(stats_done, p + 1)
                last = dve.bn_aggr(moments[:, p, :], stats[:, p, :])
            last.then_inc(moments_done, 1)
            dve.wait_ge(std_done, 1)
            dve.reciprocal(rstd[:], std[:]).then_inc(rstd_done, 1)
            dve.wait_ge(rstd_done, 1)
            for g in range(GROUPS):
                if g >= 2:
                    dve.wait_ge(turned_done, g - 1)
                for p in range(NP):
                    q = g * NP + p
                    last = dve.tensor_scalar(xn[:, g % 2, p, :], x_all[:, q, :], moments[:, q, 0:1],
                                             rstd[:, q:q + 1], ALU.subtract, ALU.mult)
                last.then_inc(xn_done, 1)

        @block.scalar
        def _(act):
            act.wait_ge(eps_set, 1)
            act.wait_ge(moments_done, 1)
            act.activation(std[:], moments[:, :, 1], ACT.Sqrt, bias=eps[:]).then_inc(std_done, 1)
            for g in range(GROUPS):
                act.wait_ge(turned_done, g + 1)
                for k in range(KH):
                    last = act.copy(xT_all[:, k, g * G:(g + 1) * G], turned[g % 2 * KH + k][:])
                last.then_inc(kept, 1)

        @block.tensor
        def _(pe):
            for g in range(GROUPS):
                pe.wait_ge(xn_done, g + 1)
                if g >= 2:
                    pe.wait_ge(kept, g - 1)
                for k in range(KH):
                    for p in range(NP):
                        last = pe.transpose(turned[g % 2 * KH + k][:, p * P:(p + 1) * P],
                                            xn[:, g % 2, p, k * P:(k + 1) * P], ident)
                last.then_inc(turned_done, 1)


def lowrank_block(nc, sems, xT_all, f1T, g1T, beta, Wf1g1, Wb, ident, small):
    with ExitStack() as ctx:
        def sb(name, shape, dt=F32):
            return ctx.enter_context(nc.sbuf_tensor(name, shape, dt))

        def sem(name):
            return sems(name)

        bT = sb("bT", [H, TOKENS])
        banks = [ctx.enter_context(nc.psum_tensor(f"low{k}", [P, G], F32)) for k in range(3)]
        beta_ps = ctx.enter_context(nc.psum_tensor("beta_ps", [P, PAIRS, H], F32))
        low_done = sem("low_done")
        low_kept = sem("low_kept")
        bT_kept = sem("bT_kept")
        beta_turned = sem("beta_turned")
        beta_done = sem("beta_done")
        block = ctx.enter_context(nc.Block())

        @block.tensor
        def _(pe):
            for g in range(GROUPS):
                cols = slice(g * G, (g + 1) * G)
                if g >= 1:
                    pe.wait_ge(low_kept, 2 * g)
                    pe.wait_ge(bT_kept, g)
                for n in range(2):
                    for k in range(KH):
                        last = pe.matmul(banks[n][:], Wf1g1[:, k, n, :], xT_all[:, k, cols],
                                         start=(k == 0), stop=(k == KH - 1))
                for k in range(KH):
                    last = pe.matmul(banks[2][0:H, :], Wb[:, k, :], xT_all[:, k, cols],
                                     start=(k == 0), stop=(k == KH - 1))
                last.then_inc(low_done, 1)
            pe.wait_ge(bT_kept, GROUPS)
            for q in range(PAIRS):
                last = pe.transpose(beta_ps[:, q, :], bT[:, q * P:(q + 1) * P], ident[0:H, 0:H])
            last.then_inc(beta_turned, 1)

        @block.scalar
        def _(act):
            for g in range(GROUPS):
                cols = slice(g * G, (g + 1) * G)
                act.wait_ge(low_done, g + 1)
                act.activation(bT[:, cols], banks[2][0:H, :], ACT.Sigmoid).then_inc(bT_kept, 1)
                act.copy(f1T[:, cols], banks[0][:]).then_inc(low_kept, 1)

        @block.vector
        def _(dve):
            for g in range(GROUPS):
                dve.wait_ge(low_done, g + 1)
                dve.tensor_copy(g1T[:, g * G:(g + 1) * G], banks[1][:]).then_inc(low_kept, 1)
            dve.wait_ge(beta_turned, 1)
            dve.tensor_copy(beta.rearrange("p g h q -> p g q h"),
                            beta_ps[:].rearrange("p (g q) h -> p g q h", g=GROUPS)).then_inc(beta_done, 1)


def gsa_block(nc, sems, w_heads, x_all, xT_all, f1T, g1T, beta, Wo, consts, far_flag):
    ident, span, causal = consts
    with ExitStack() as ctx:
        def sb(name, shape, dt=F32):
            return ctx.enter_context(nc.sbuf_tensor(name, shape, dt))

        def psum(name, shape, dt=F32):
            return ctx.enter_context(nc.psum_tensor(name, shape, dt))

        def sem(name):
            return sems(name)

        hw = [sb(f"head_weights{i}", [P, W_HEAD]) for i in range(2)]
        q = [sb(f"q_chan{i}", [P, G]) for i in range(2)]
        k, v, w = (sb(f"{n}_chan", [P, G]) for n in "kvw")
        f1 = sb("f1_static", [P, G])
        glog = sb("glog", [P, G])
        gtmp = sb("gtmp", [P, G])
        expD = sb("expD", [P, G])
        expDneg = sb("expDneg", [P, G])
        gate = [sb(f"gate{i}", [P, G]) for i in range(2)]
        w2 = sb("w2", [P, G])
        wdec = [sb(f"wdec{i}", [P, G]) for i in range(2)]
        wdec_tok = sb("wdec_tok", [P, G])
        v_tok = [sb(f"v_tok{i}", [P, G]) for i in range(2)]
        qk = sb("qk", [P, G])
        score = sb("score", [P, G])
        probs = sb("probs", [P, G])
        pdec = sb("pdec", [P, G])
        pdec_chan = sb("pdec_chan", [P, G])
        mix = sb("mix", [P, G])
        osq = sb("osq", [P, G])
        o_tok = sb("o_tok", [P, G])
        o_chan = sb("o_chan", [P, G])
        ones = sb("ones", [P, P])
        half = sb("half", [P, 1])
        l2eps = sb("l2eps", [P, 1])
        zeros = sb("zeros", [P, G], BF16)
        hbias = sb("hbias", [P, 1])
        widest = sb("widest", [P, NS])
        narrowest = sb("narrowest", [P, NS])
        far = sb("far", [P, NS])
        far_any = sb("far_any", [P, 1])
        far_one = sb("far_one", [1, 1])
        lnw = sb("lnw", [P, NP])
        rw = sb("rw", [P, NP])
        coef = [sb(f"coef{i}", [P, NP]) for i in range(2)]
        smax = sb("smax", [P, NP])
        nmax = sb("nmax", [P, NP])
        Z = sb("Z", [P, NP])
        Zeps = [sb(f"Zeps{i}", [P, NP]) for i in range(2)]
        ssq = sb("ssq", [P, NP])
        y = sb("y", [P, NP])
        lny = sb("lny", [P, NP])
        rho = sb("rho", [P, NP])

        bank0, bank1, bank2, bank3, bank4, bank5 = (psum(f"bank{n}", [P, G]) for n in range(6))
        outacc = [psum(f"outacc{n}", [P, 2, HID]) for n in range(2)]

        primed = {
            "tensor": "xq xk xv xw gx gate_x dtok dchan wsq att wdecT vT scores pdecT pv o oT wo",
            "scalar": "tapq tapk tapv tapw gabs gexp gln decay ndecay gate_th siluq siluk siluv siluw lnw_s rw_s "
                      "wdec_tok_s v_tok_s exps osq_s lny_s rho_s",
            "vector": "convq convk convv convw glog_s coef_s qk_s score_s smax_s nmax_s Zeps_s y_s mix_s "
                      "o_tok_s o_chan_s pdec_chan_s range_s",
            "gpsimd": "w2_s wdec_s f1_s hbias_s pdec_s",
        }
        S = {n: sem(n) for names in primed.values() for n in names.split()}
        weights_in = [sem(f"weights_in{i}") for i in range(2)]
        consts_set = sem("consts_set")
        group_out = sem("group_out")
        range_set = sem("range_set")
        far_s = sem("far_s")
        far_turned = sem("far_turned")
        block = ctx.enter_context(nc.Block())

        CONV = TAPS - 1

        def prime(eng, who):
            for n in primed[who].split():
                eng.sem_inc(S[n], 1)

        def done(n, times=1):
            return times * (n + 1) + 1

        def before(n, times=1):
            return times * n + 1

        def two_before(n):
            return n

        def run_units(eng, front, merged, group_start=None, group_end=None):
            front(0, 0)
            merged(-1, None, 1, outputs=False)
            with eng.Fori(0, GROUPS) as g:
                if group_start is not None:
                    group_start(g)
                with eng.Fori(0, H // 2) as j:
                    for par in range(2):
                        merged(g * H + j * 2 + par, j * 2 + par, par)
                if group_end is not None:
                    group_end(g)

        def pairs(t):
            return t[:].rearrange("p (q c) -> p q c", q=NP)

        def pc(t, p):
            return t[:, p * P:(p + 1) * P]

        @block.sync
        def _(sp):
            def load(n, h, par):
                sp.dma_start(hw[par][:], w_heads[h]).then_inc(weights_in[par], 16)

            load(0, 0, 0)
            load(1, 1, 1)
            with sp.Fori(0, UNITS // 2) as m:
                for par in range(2):
                    n = 2 * m + par
                    sp.wait_ge(S["gate_x"], done(n))
                    sp.wait_ge(S["hbias_s"], done(n))
                    sp.wait_ge(S["convw"], done(n, CONV))
                    load(n + 2, (n + 2) % H, par)
            sp.wait_ge(S["gate_x"], done(UNITS))
            sp.wait_ge(S["hbias_s"], done(UNITS))
            sp.wait_ge(S["convw"], done(UNITS, CONV))
            load(UNITS + 2, 0, 0)

        @block.gpsimd
        def _(pool):
            prime(pool, "gpsimd")
            pool.memset(ones[:], 1.0).then_inc(consts_set, 1)
            pool.memset(half[:], 0.5).then_inc(consts_set, 1)
            pool.memset(l2eps[:], L2EPS).then_inc(consts_set, 1)
            pool.memset(zeros[:], 0.0).then_inc(consts_set, 1)
            pool.wait_ge(consts_set, 4)

            def front(n, par):
                pool.wait_ge(S["gx"], before(n))
                pool.tensor_copy(f1[:], f1T[:, bass.ts(n // H, G)]).then_inc(S["f1_s"], 1)
                pool.wait_ge(weights_in[par], 16 * (n // 2 + 1))
                pool.wait_ge(S["gate_th"], before(n))
                pool.tensor_tensor(hbias[:], hw[par][:, W_BIAS:W_BIAS + 1], half[:], ALU.mult)\
                    .then_inc(S["hbias_s"], 1)

            def merged(b, h, par, outputs=True):
                a, apar, n = b + 1, 1 - par, b + 2
                pool.wait_ge(S["siluw"], done(a))
                pool.wait_ge(S["wsq"], before(a))
                pool.tensor_tensor(w2[:], w[:], w[:], ALU.mult).then_inc(S["w2_s"], 1)
                pool.wait_ge(S["ndecay"], done(a))
                if outputs:
                    pool.wait_ge(S["pv"], two_before(a))
                pool.tensor_tensor(wdec[apar][:], w[:], expDneg[:], ALU.mult).then_inc(S["wdec_s"], 1)
                front(n, par)
                pool.wait_ge(S["exps"], done(a, NP))
                pool.wait_ge(S["pdecT"], before(a))
                pool.tensor_tensor(pdec[:], probs[:], expD[:], ALU.mult).then_inc(S["pdec_s"], 1)

            run_units(pool, front, merged)

        @block.tensor
        def _(pe):
            prime(pe, "tensor")
            pe.wait_ge(consts_set, 4)

            def project(n, par, bank, w_col, step):
                cols = bass.ts(n // H, G)
                for kk in range(KH):
                    last = pe.matmul(bank[:], hw[par][:, w_col + kk * P:w_col + (kk + 1) * P], xT_all[:, kk, cols],
                                     start=(kk == 0), stop=(kk == KH - 1))
                last.then_inc(S[step], 1)

            def f_q(n, par):
                pe.wait_ge(weights_in[par], 16 * (n // 2 + 1))
                pe.wait_ge(S["convv"], before(n, CONV))
                project(n, par, bank0, W_Q, "xq")

            def f_k(n, par):
                pe.wait_ge(S["convw"], before(n, CONV))
                project(n, par, bank1, W_K, "xk")

            def f_v(n, par):
                pe.wait_ge(S["convq"], done(n, CONV))
                project(n, par, bank0, W_V, "xv")

            def f_w(n, par):
                pe.wait_ge(S["convk"], done(n, CONV))
                project(n, par, bank1, W_W, "xw")

            def f_decay_logits(n, par):
                pe.wait_ge(S["f1_s"], done(n))
                pe.wait_ge(S["v_tok_s"], before(n))
                for p in range(NP):
                    last = pe.matmul(pc(bank5, p), pc(f1, p), hw[par][:, W_F2:W_F2 + P], start=True, stop=True)
                last.then_inc(S["gx"], 1)

            def f_decays(n, par):
                pe.wait_ge(S["glog_s"], done(n))
                for p in range(NP):
                    last = pe.matmul(pc(bank5, p), pc(glog, p), span, start=True, stop=True)
                last.then_inc(S["dchan"], 1)
                pe.wait_ge(S["score_s"], before(n))
                pe.matmul(bank2[:], span, glog[:], start=True, stop=True).then_inc(S["dtok"], 1)

            def f_gate(n, par, outputs=True):
                if outputs:
                    pe.wait_ge(S["o_tok_s"], two_before(n))
                cols = bass.ts(n // H, G)
                if not outputs:
                    pe.wait_ge(S["gate_th"], before(n))
                pe.matmul(bank4[:], hw[par][:, W_G2:W_G2 + P], g1T[:, cols], start=True, stop=True)\
                    .then_inc(S["gate_x"], 1)

            def front(n, par):
                f_q(n, par)
                f_k(n, par)
                f_decay_logits(n, par)
                f_v(n, par)
                f_w(n, par)
                f_q(n + 1, 1 - par)
                f_decays(n, par)
                f_gate(n, par, outputs=False)

            def merged(b, h, par, outputs=True):
                a, apar, n = b + 1, 1 - par, b + 2
                if outputs:
                    pe.wait_ge(S["pdec_s"], done(b))
                    pe.wait_ge(S["o_chan_s"], before(b))
                    for p in range(NP):
                        last = pe.transpose(pc(bank3, p), pc(pdec, p), ident)
                    last.then_inc(S["pdecT"], 1)
                pe.wait_ge(S["siluk"], done(a))
                pe.wait_ge(S["siluq"], done(a))
                pe.wait_ge(S["decay"], done(a))
                for p in range(NP):
                    last = pe.matmul(pc(bank2, p), pc(k, p), pc(q[apar], p), start=True, stop=True)
                last.then_inc(S["att"], 1)
                pe.wait_ge(S["w2_s"], done(a))
                pe.wait_ge(S["ndecay"], done(a))
                for p in range(NP):
                    last = pe.matmul(pc(bank5, p), pc(w2, p), ones[:], start=True, stop=True)
                last.then_inc(S["wsq"], 1)
                if outputs:
                    pe.wait_ge(S["pdec_chan_s"], done(b))
                    for s0 in range(0, G, T):
                        rows, p0 = s0 % P, s0 // P * P
                        t_halves = pdec_chan[:, p0:p0 + P].rearrange("m (u v t) -> m v u t", u=2, v=2)
                        o_halves = bank3[:, p0:p0 + P].rearrange("m (u v t) -> m v u t", u=2, v=2)
                        pe.matmul(o_halves[rows:rows + T, 1], wdec[par][:, s0:s0 + T], t_halves[:, 1],
                                  start=True, stop=True)
                        last = pe.matmul(o_halves[rows:rows + T // 2, 0], wdec[par][:, s0:s0 + T // 2],
                                         t_halves[:, 0], start=True, stop=True)
                    last.then_inc(S["pv"], 1)
                pe.wait_ge(S["wdec_s"], done(a))
                pe.wait_ge(S["lnw_s"], done(a))
                for p in range(NP):
                    last = pe.transpose(pc(bank5, p), pc(wdec[apar], p), ident)
                last.then_inc(S["wdecT"], 1)
                f_k(n, par)
                pe.wait_ge(S["qk_s"], done(a))
                pe.wait_ge(S["wdec_tok_s"], done(a))
                for p in range(NP):
                    last = pe.matmul(pc(bank2, p), pc(qk, p), pc(wdec_tok, p), start=True, stop=True)
                last.then_inc(S["scores"], 1)
                if outputs:
                    pe.wait_ge(S["mix_s"], done(b))
                    pe.wait_ge(S["gate_th"], done(a))
                    for p in range(NP):
                        last = pe.matmul(pc(bank4, p), pc(mix, p), pc(v_tok[par], p), start=True, stop=True)
                    last.then_inc(S["o"], 1)
                pe.wait_ge(S["siluv"], done(a))
                for p in range(NP):
                    last = pe.transpose(pc(bank5, p), pc(v, p), ident)
                last.then_inc(S["vT"], 1)
                f_v(n, par)
                f_decay_logits(n, par)
                f_w(n, par)
                f_q(n + 1, apar)
                f_decays(n, par)
                if outputs:
                    pe.wait_ge(S["o_tok_s"], done(b))
                    for p in range(NP):
                        last = pe.transpose(pc(bank3, p), pc(o_tok, p), ident)
                    last.then_inc(S["oT"], 1)
                f_gate(n, par, outputs)
                if outputs:
                    pe.wait_ge(S["o_chan_s"], done(b))
                    for p in range(NP):
                        last = pe.matmul(outacc[p // 2][:, p % 2, :], pc(o_chan, p), Wo[:, bass.ts(h, HID)],
                                         start=False, stop=False, skip_group_check=True)
                    last.then_inc(S["wo"], 1)

            def group_start(g):
                pe.wait_ge(group_out, g + 1)
                for n in range(2):
                    pe.matmul(outacc[n][:].rearrange("p a c -> p (a c)"), zeros[:, 0:P], zeros[:],
                              start=True, stop=False, skip_group_check=True)

            run_units(pe, front, merged, group_start=group_start)
            pe.wait_ge(far_s, 3)
            pe.wait_ge(S["convq"], done(UNITS + 2, CONV))
            pe.transpose(bank0[0:1, 0:P], far_any[:], ident).then_inc(far_turned, 1)

        @block.scalar
        def _(act):
            prime(act, "scalar")
            act.wait_ge(consts_set, 4)

            def tap(n, par, bank, dst, col, x_step, conv_step, free_waits):
                act.wait_ge(S[x_step], done(n))
                for s in free_waits:
                    act.wait_ge(S[s], before(n))
                c = W_CONV + TAPS * col + TAPS - 1
                act.activation(dst[:], bank[:], ACT.Copy, scale=hw[par][:, c:c + 1])\
                    .then_inc(S[conv_step], 1)

            def f_tapq(n, par, first=False):
                if not first:
                    act.wait_ge(S["att"], two_before(n))
                tap(n, par, bank0, q[par], 0, "xq", "tapq", [])

            def f_tapk(n, par):
                tap(n, par, bank1, k, 1, "xk", "tapk", ["att"])

            def f_tapv(n, par):
                tap(n, par, bank0, v, 2, "xv", "tapv", ["vT"])

            def f_tapw(n, par):
                tap(n, par, bank1, w, 3, "xw", "tapw", ["w2_s", "wdec_s"])

            def f_log_sigmoid(n, par):
                act.wait_ge(S["gx"], done(n))
                act.wait_ge(S["glog_s"], before(n))
                act.activation(gtmp[:], bank5[:], ACT.Abs).then_inc(S["gabs"], 1)
                act.wait_ge(S["gabs"], done(n))
                act.activation(gtmp[:], gtmp[:], ACT.Exp, scale=-1.0).then_inc(S["gexp"], 1)
                act.wait_ge(S["gexp"], done(n))
                act.activation(gtmp[:], gtmp[:], ACT.Ln, bias=1.0).then_inc(S["gln"], 1)

            def f_decays(n, par):
                act.wait_ge(S["dchan"], done(n))
                act.wait_ge(S["wdec_s"], before(n))
                act.wait_ge(S["range_s"], before(n, 2))
                act.activation(expDneg[:], bank5[:], ACT.Exp, scale=-1.0).then_inc(S["ndecay"], 1)
                act.wait_ge(S["dtok"], done(n))
                act.wait_ge(S["pdec_s"], before(n))
                act.activation(expD[:], bank2[:], ACT.Exp).then_inc(S["decay"], 1)

            def f_silus(n, par, outputs):
                act.preload_act_table_set("silu_and_others")
                for t, c, s in ((w, "convw", "siluw"), (k, "convk", "siluk"), (q[par], "convq", "siluq"),
                                (v, "convv", "siluv")):
                    act.wait_ge(S[c], done(n, CONV))
                    act.activation(t[:], t[:], ACT.Silu).then_inc(S[s], 1)
                act.wait_ge(S["gate_x"], done(n))
                act.wait_ge(S["hbias_s"], done(n))
                if outputs:
                    act.wait_ge(S["o_chan_s"], two_before(n))
                act.activation(gate[par][:], bank4[:], ACT.Tanh, bias=hbias[:], scale=0.5).then_inc(S["gate_th"], 1)
                act.preload_act_table_set("natural_log_exp_and_others")

            def front(n, par):
                f_tapq(n, par, first=True)
                f_tapk(n, par)
                f_log_sigmoid(n, par)
                f_tapv(n, par)
                f_tapw(n, par)
                f_tapq(n + 1, 1 - par)
                f_decays(n, par)
                f_silus(n, par, outputs=False)

            def merged(b, h, par, outputs=True):
                a, apar, n = b + 1, 1 - par, b + 2
                act.wait_ge(S["wsq"], done(a))
                act.activation(lnw[:], pairs(bank5)[:, :, 0], ACT.Ln, bias=l2eps[:]).then_inc(S["lnw_s"], 1)
                act.wait_ge(S["lnw_s"], done(a))
                act.wait_ge(S["coef_s"], before(a))
                act.activation(rw[:], lnw[:], ACT.Exp, scale=-0.5).then_inc(S["rw_s"], 1)
                act.wait_ge(S["wdecT"], done(a))
                act.wait_ge(S["scores"], before(a))
                act.copy(wdec_tok[:], bank5[:]).then_inc(S["wdec_tok_s"], 1)
                f_tapk(n, par)
                act.wait_ge(S["vT"], done(a))
                if outputs:
                    act.wait_ge(S["o"], two_before(a))
                act.copy(v_tok[apar][:], bank5[:]).then_inc(S["v_tok_s"], 1)
                if outputs:
                    act.wait_ge(S["o"], done(b))
                    act.wait_ge(S["y_s"], before(b))
                    for p in range(NP):
                        act.activation(pc(osq, p), pc(bank4, p), ACT.Square, accum_out=ssq[:, p:p + 1])\
                            .then_inc(S["osq_s"], 1)
                f_tapv(n, par)
                act.wait_ge(S["nmax_s"], done(a))
                act.wait_ge(S["pdec_s"], before(a))
                act.wait_ge(S["Zeps_s"], before(a))
                for p in range(NP):
                    act.activation(pc(probs, p), pc(score, p), ACT.Exp, bias=nmax[:, p:p + 1], scale=SCALE,
                                   accum_out=Z[:, p:p + 1]).then_inc(S["exps"], 1)
                if outputs:
                    act.wait_ge(S["y_s"], done(b))
                    act.activation(lny[:], y[:], ACT.Ln).then_inc(S["lny_s"], 1)
                    act.wait_ge(S["lny_s"], done(b))
                    act.wait_ge(S["o_tok_s"], before(b))
                    act.activation(rho[:], lny[:], ACT.Exp, scale=-0.5).then_inc(S["rho_s"], 1)
                f_log_sigmoid(n, par)
                f_tapw(n, par)
                f_tapq(n + 1, apar)
                f_decays(n, par)
                f_silus(n, par, outputs)

            run_units(act, front, merged)

        @block.vector
        def _(dve):
            prime(dve, "vector")
            dve.sem_inc(group_out, 1)
            dve.wait_ge(consts_set, 4)
            dve.memset(widest[:], 1.0).then_inc(range_set, 1)
            dve.memset(narrowest[:], 1.0).then_inc(range_set, 1)
            dve.wait_ge(range_set, 2)

            def conv(n, par, bank, dst, col, tap_step, conv_step):
                x3 = bank[:].rearrange("p (s t) -> p s t", s=NS)
                d3 = dst[:].rearrange("p (s t) -> p s t", s=NS)
                dve.wait_ge(S[tap_step], done(n))
                for shift in range(1, TAPS):
                    if shift > 1:
                        dve.wait_ge(S[conv_step], before(n, CONV) + shift - 1)
                    c = W_CONV + TAPS * col + TAPS - 1 - shift
                    dve.scalar_tensor_tensor(out=d3[:, :, shift:T], in0=x3[:, :, 0:T - shift],
                                             scalar=hw[par][:, c:c + 1], in1=d3[:, :, shift:T],
                                             op0=ALU.mult, op1=ALU.add).then_inc(S[conv_step], 1)

            def f_convq(n, par):
                conv(n, par, bank0, q[par], 0, "tapq", "convq")

            def f_convk(n, par):
                conv(n, par, bank1, k, 1, "tapk", "convk")

            def f_convv(n, par):
                conv(n, par, bank0, v, 2, "tapv", "convv")

            def f_convw(n, par):
                conv(n, par, bank1, w, 3, "tapw", "convw")

            def f_glog(n, par):
                dve.wait_ge(S["gln"], done(n))
                dve.wait_ge(S["dchan"], before(n))
                dve.wait_ge(S["dtok"], before(n))
                dve.scalar_tensor_tensor(out=glog[:], in0=bank5[:], scalar=0.0, in1=gtmp[:], op0=ALU.min,
                                         op1=ALU.subtract).then_inc(S["glog_s"], 1)

            def f_range(n):
                e3 = expDneg[:].rearrange("p (s t) -> p s t", s=NS)
                dve.wait_ge(S["ndecay"], done(n))
                dve.wait_ge(S["range_s"], before(n, 2))
                dve.tensor_tensor(widest[:], widest[:], e3[:, :, T - 1], ALU.max).then_inc(S["range_s"], 1)
                dve.tensor_tensor(narrowest[:], narrowest[:], e3[:, :, 0], ALU.min).then_inc(S["range_s"], 1)

            def beta_of(i):
                return beta.rearrange("p g h q -> p (g h q)")[:, bass.ts(i, NP)]

            def front(n, par):
                f_convq(n, par)
                f_convk(n, par)
                f_convv(n, par)
                f_glog(n, par)
                f_convw(n, par)
                f_convq(n + 1, 1 - par)

            def merged(b, h, par, outputs=True):
                a, apar, n = b + 1, 1 - par, b + 2
                if outputs:
                    dve.wait_ge(S["pdecT"], done(b))
                    dve.wait_ge(S["pv"], before(b))
                    dve.tensor_copy(pdec_chan[:], bank3[:]).then_inc(S["pdec_chan_s"], 1)
                f_range(a)
                dve.wait_ge(S["rw_s"], done(a))
                if outputs:
                    dve.wait_ge(S["mix_s"], two_before(a))
                dve.tensor_tensor(coef[apar][:], rw[:], beta_of(a), ALU.mult).then_inc(S["coef_s"], 1)
                dve.wait_ge(S["coef_s"], done(a))
                dve.wait_ge(S["att"], done(a))
                dve.wait_ge(S["scores"], before(a))
                for p in range(NP):
                    last = dve.scalar_tensor_tensor(out=pc(qk, p), in0=pc(bank2, p), scalar=coef[apar][:, p:p + 1],
                                                    in1=causal, op0=ALU.mult, op1=ALU.mult)
                last.then_inc(S["qk_s"], 1)
                if outputs:
                    dve.wait_ge(S["pv"], done(b))
                    dve.wait_ge(S["o"], before(b))
                    for p in range(NP):
                        last = dve.scalar_tensor_tensor(out=pc(mix, p), in0=pc(bank3, p),
                                                        scalar=coef[par][:, p:p + 1], in1=causal,
                                                        op0=ALU.mult, op1=ALU.mult)
                    last.then_inc(S["mix_s"], 1)
                f_convk(n, par)
                dve.wait_ge(S["scores"], done(a))
                dve.wait_ge(S["exps"], before(a, NP))
                dve.tensor_tensor(score[:], bank2[:], expD[:], ALU.mult).then_inc(S["score_s"], 1)
                dve.wait_ge(S["score_s"], done(a))
                dve.tensor_reduce(smax[:], pairs(score), AX.X, ALU.max).then_inc(S["smax_s"], 1)
                dve.wait_ge(S["smax_s"], done(a))
                dve.tensor_scalar(nmax[:], smax[:], -SCALE, None, ALU.mult).then_inc(S["nmax_s"], 1)
                if outputs:
                    dve.wait_ge(S["osq_s"], done(b, NP))
                    dve.wait_ge(S["Zeps_s"], done(b))
                    dve.wait_ge(S["lny_s"], before(b))
                    dve.scalar_tensor_tensor(out=y[:], in0=ssq[:], scalar=4.0 / P, in1=Zeps[par][:], op0=ALU.mult,
                                             op1=ALU.add).then_inc(S["y_s"], 1)
                f_convv(n, par)
                dve.wait_ge(S["exps"], done(a, NP))
                if outputs:
                    dve.wait_ge(S["y_s"], two_before(a))
                dve.scalar_tensor_tensor(out=Zeps[apar][:], in0=Z[:], scalar=4.0 * EPS, in1=Z[:], op0=ALU.mult,
                                         op1=ALU.mult).then_inc(S["Zeps_s"], 1)
                if outputs:
                    dve.wait_ge(S["rho_s"], done(b))
                    dve.wait_ge(S["oT"], before(b))
                    for p in range(NP):
                        last = dve.tensor_scalar(pc(o_tok, p), pc(bank4, p), rho[:, p:p + 1], None, ALU.mult)
                    last.then_inc(S["o_tok_s"], 1)
                f_glog(n, par)
                f_convw(n, par)
                if outputs:
                    dve.wait_ge(S["oT"], done(b))
                    dve.wait_ge(S["gate_th"], done(b))
                    dve.wait_ge(S["wo"], before(b))
                    dve.scalar_tensor_tensor(out=o_chan[:], in0=gate[par][:], scalar=1.0, in1=bank3[:],
                                             op0=ALU.add, op1=ALU.mult).then_inc(S["o_chan_s"], 1)
                f_convq(n + 1, apar)

            def group_end(g):
                dve.wait_ge(S["wo"], before(g * H + H))
                for m in range(2):
                    xs = x_all[:, bass.ds(g * NP + 2 * m, 2), :]
                    last = dve.tensor_tensor(xs, xs, outacc[m][:], ALU.add)
                last.then_inc(group_out, 1)

            run_units(dve, front, merged, group_end=group_end)
            dve.wait_ge(S["range_s"], done(UNITS, 2))
            dve.tensor_scalar(far[:], widest[:], FAR, None, ALU.is_gt).then_inc(far_s, 1)
            dve.wait_ge(far_s, 1)
            dve.scalar_tensor_tensor(out=far[:], in0=narrowest[:], scalar=1.0 / FAR, in1=far[:], op0=ALU.is_lt,
                                     op1=ALU.max).then_inc(far_s, 1)
            dve.wait_ge(far_s, 2)
            dve.tensor_reduce(far_any[:], far[:], AX.X, ALU.max).then_inc(far_s, 1)
            dve.wait_ge(far_turned, 1)
            dve.tensor_reduce(far_one[:], bank0[0:1, 0:P], AX.X, ALU.max).then_inc(far_s, 1)
            dve.wait_ge(far_s, 4)
            dve.tensor_copy(far_flag[:], far_one[:]).then_inc(far_s, 1)


def gsa_general_block(nc, sems, w_heads, tables_dram, x_all, x_view, xT_all, f1T, g1T, beta, Wo, consts, far_flag,
                      always=False):
    ident, _, _ = consts
    CONV = TAPS - 1
    steps = {}
    steps["front"] = ["statics", "projected", "taps", "gexp", "gln", "conv1", "conv2", "conv3", "silus", "w2",
                      "turned", "lnw", "rw", "coef"]
    steps["scores"] = ["dtok", "decay", "wdec", "qk", "products", "decayed", "summed"]
    steps["softmax"] = ["smax", "nmax", "exps", "Zeps", "probsT", "probs_chan"]
    steps["values"] = ["dchan", "decay", "decayed", "products", "masked", "summed"]
    steps["outputs"] = ["o", "osq", "y", "lny", "rho", "o_tok", "oT", "o_chan", "wo"]
    start, at = {}, 0
    for section, names in steps.items():
        start[section] = at
        at += len(names) * (LEVELS if section in ("scores", "values") else 1)
    UNIT_STEPS = at

    def through(i, section, step, level=0):
        return i * UNIT_STEPS + level * len(steps[section]) + (start[section] + steps[section].index(step) + 2)

    def ahead(i, section, step, level=0):
        return i * UNIT_STEPS + level * len(steps[section]) + (start[section] + steps[section].index(step) + 1)

    with ExitStack() as ctx:
        def sb(name, shape, dt=F32):
            return ctx.enter_context(nc.sbuf_tensor(f"n_{name}", shape, dt))

        def psum(name, shape, dt=F32):
            return ctx.enter_context(nc.psum_tensor(f"n_{name}", shape, dt))

        def sem(name):
            return sems(f"n_{name}")

        hw = sb("head_weights", [P, W_HEAD])
        tables = sb("tables", [P, 2 * P])
        sums, mask = tables[:, 0:P], tables[:, P:2 * P]
        q, k, v, w, f1, glog, gtmp, gate, w2, decay, wdec, adec, w_tok, v_tok, qk, part, score, probs, \
            probs_chan, mix, osq, o_tok, o_chan = (
                sb(n, [P, G]) for n in "q k v w f1 glog gtmp gate w2 decay wdec adec w_tok v_tok qk part score probs "
                "probs_chan mix osq o_tok o_chan".split())
        ones = sb("ones", [P, P])
        half, l2eps, hbias = (sb(n, [P, 1]) for n in ("half", "l2eps", "hbias"))
        zeros = sb("zeros", [P, G], BF16)
        lnw, rw, coef, smax, nmax, Z, Zeps, ssq, y, lny, rho = (
            sb(n, [P, NP]) for n in "lnw rw coef smax nmax Z Zeps ssq y lny rho".split())
        bank = [psum(f"bank{n}", [P, G]) for n in range(6)]
        outacc = [psum(f"outacc{n}", [P, 2, HID]) for n in range(2)]

        turn = sem("turn")
        weights_in = sem("weights_in")
        tables_in = sem("tables_in")
        x_back = sem("x_back")
        consts_set = sem("consts_set")
        group_out = sem("group_out")
        block = ctx.enter_context(nc.Block())

        def pc(t, p):
            return t[:, p * P:(p + 1) * P]

        def pairs(t):
            return t[:].rearrange("p (q c) -> p q c", q=NP)

        def when_far(eng, units, first=None):
            flag = eng.value_load(far_flag[0:1, 0:1], min_val=0, max_val=1)
            with eng.If(flag > 0) if not always else eng.If(flag >= 0):
                if first is not None:
                    first()
                units()

        @block.sync
        def _(sp):
            def units():
                sp.dma_start(x_all[:], x_view).then_inc(x_back, 16)
                with sp.Fori(0, UNITS) as i:
                    sp.wait_ge(turn, ahead(i, "front", "statics"))
                    sp.dma_start(hw[:], w_heads[i % H]).then_inc(weights_in, 16)
                    for n, section in enumerate(("scores", "values")):
                        with sp.Fori(0, LEVELS) as level:
                            sp.wait_ge(turn, ahead(i, section, steps[section][0], level))
                            sp.dma_start(tables[:], tables_dram[level]).then_inc(tables_in, 16)

            when_far(sp, units)

        def tables_count(i, n, level):
            return i * (2 * LEVELS * 16) + level * 16 + (n * LEVELS * 16 + 16)

        @block.gpsimd
        def _(pool):
            def first():
                pool.sem_inc(turn, 1)
                pool.memset(ones[:], 1.0).then_inc(consts_set, 1)
                pool.memset(half[:], 0.5).then_inc(consts_set, 1)
                pool.memset(l2eps[:], L2EPS).then_inc(consts_set, 1)
                pool.memset(zeros[:], 0.0).then_inc(consts_set, 1)
                pool.wait_ge(consts_set, 4)

            def units():
                with pool.Fori(0, UNITS) as i:
                    pool.wait_ge(turn, ahead(i, "front", "statics"))
                    pool.wait_ge(weights_in, 16 * i + 16)
                    pool.tensor_copy(f1[:], f1T[:, bass.ts(i // H, G)])
                    pool.tensor_tensor(hbias[:], hw[:, W_BIAS:W_BIAS + 1], half[:], ALU.mult).then_inc(turn, 1)
                    pool.wait_ge(turn, ahead(i, "front", "w2"))
                    pool.tensor_tensor(w2[:], w[:], w[:], ALU.mult).then_inc(turn, 1)
                    with pool.Fori(0, LEVELS) as level:
                        pool.wait_ge(turn, ahead(i, "scores", "wdec", level))
                        pool.tensor_tensor(wdec[:], w_tok[:], decay[:], ALU.mult).then_inc(turn, 1)
                    with pool.Fori(0, LEVELS) as level:
                        pool.wait_ge(turn, ahead(i, "values", "decayed", level))
                        pool.tensor_tensor(wdec[:], w[:], decay[:], ALU.mult)
                        pool.tensor_tensor(adec[:], probs_chan[:], decay[:], ALU.mult).then_inc(turn, 1)

            when_far(pool, units, first)

        @block.tensor
        def _(pe):
            def units():
                pe.wait_ge(consts_set, 4)
                with pe.Fori(0, GROUPS) as g:
                    pe.wait_ge(group_out, g + 1)
                    for n in range(2):
                        pe.matmul(outacc[n][:].rearrange("p a c -> p (a c)"), zeros[:, 0:P], zeros[:],
                                  start=True, stop=False, skip_group_check=True)
                    with pe.Fori(0, H) as h:
                        unit(g * H + h, g, h)

            def unit(i, g, h):
                cols = bass.ts(g, G)
                pe.wait_ge(turn, ahead(i, "front", "projected"))
                for n, w_col in enumerate((W_Q, W_K, W_V, W_W)):
                    for kk in range(KH):
                        pe.matmul(bank[n][:], hw[:, w_col + kk * P:w_col + (kk + 1) * P], xT_all[:, kk, cols],
                                  start=(kk == 0), stop=(kk == KH - 1))
                for p in range(NP):
                    pe.matmul(pc(bank[4], p), pc(f1, p), hw[:, W_F2:W_F2 + P], start=True, stop=True)
                pe.matmul(bank[5][:], hw[:, W_G2:W_G2 + P], g1T[:, cols], start=True, stop=True).then_inc(turn, 1)
                pe.wait_ge(turn, ahead(i, "front", "turned"))
                for p in range(NP):
                    pe.matmul(pc(bank[0], p), pc(k, p), pc(q, p), start=True, stop=True)
                    pe.transpose(pc(bank[3], p), pc(v, p), ident)
                    pe.matmul(pc(bank[4], p), pc(w2, p), ones[:], start=True, stop=True)
                    last = pe.transpose(pc(bank[5], p), pc(w, p), ident)
                last.then_inc(turn, 1)
                with pe.Fori(0, LEVELS) as level:
                    pe.wait_ge(turn, ahead(i, "scores", "dtok", level))
                    pe.wait_ge(tables_in, tables_count(i, 0, level))
                    pe.matmul(bank[1][:], sums, glog[:], start=True, stop=True).then_inc(turn, 1)
                    pe.wait_ge(turn, ahead(i, "scores", "products", level))
                    for p in range(NP):
                        last = pe.matmul(pc(bank[2], p), pc(qk, p), pc(wdec, p), start=True, stop=True)
                    last.then_inc(turn, 1)
                pe.wait_ge(turn, ahead(i, "softmax", "probsT"))
                for p in range(NP):
                    last = pe.transpose(pc(bank[3], p), pc(probs, p), ident)
                last.then_inc(turn, 1)
                with pe.Fori(0, LEVELS) as level:
                    pe.wait_ge(turn, ahead(i, "values", "dchan", level))
                    pe.wait_ge(tables_in, tables_count(i, 1, level))
                    for p in range(NP):
                        last = pe.matmul(pc(bank[1], p), pc(glog, p), sums, start=True, stop=True)
                    last.then_inc(turn, 1)
                    pe.wait_ge(turn, ahead(i, "values", "products", level))
                    for p in range(NP):
                        last = pe.matmul(pc(bank[2], p), pc(wdec, p), pc(adec, p), start=True, stop=True)
                    last.then_inc(turn, 1)
                pe.wait_ge(turn, ahead(i, "outputs", "o"))
                for p in range(NP):
                    last = pe.matmul(pc(bank[4], p), pc(mix, p), pc(v_tok, p), start=True, stop=True)
                last.then_inc(turn, 1)
                pe.wait_ge(turn, ahead(i, "outputs", "oT"))
                for p in range(NP):
                    last = pe.transpose(pc(bank[5], p), pc(o_tok, p), ident)
                last.then_inc(turn, 1)
                pe.wait_ge(turn, ahead(i, "outputs", "wo"))
                for p in range(NP):
                    last = pe.matmul(outacc[p // 2][:, p % 2, :], pc(o_chan, p), Wo[:, bass.ts(h, HID)],
                                     start=False, stop=False, skip_group_check=True)
                last.then_inc(turn, 1)

            when_far(pe, units)

        @block.scalar
        def _(act):
            def units():
                act.wait_ge(consts_set, 4)
                with act.Fori(0, UNITS) as i:
                    act.wait_ge(turn, ahead(i, "front", "taps"))
                    for n, t in enumerate((q, k, v, w)):
                        c = W_CONV + TAPS * n + TAPS - 1
                        act.activation(t[:], bank[n][:], ACT.Copy, scale=hw[:, c:c + 1])
                    act.activation(gate[:], bank[5][:], ACT.Tanh, bias=hbias[:], scale=0.5)
                    act.activation(gtmp[:], bank[4][:], ACT.Abs).then_inc(turn, 1)
                    act.wait_ge(turn, ahead(i, "front", "gexp"))
                    act.activation(gtmp[:], gtmp[:], ACT.Exp, scale=-1.0).then_inc(turn, 1)
                    act.wait_ge(turn, ahead(i, "front", "gln"))
                    act.activation(gtmp[:], gtmp[:], ACT.Ln, bias=1.0).then_inc(turn, 1)
                    act.wait_ge(turn, ahead(i, "front", "silus"))
                    for t in (q, k, v, w):
                        last = act.activation(t[:], t[:], ACT.Silu)
                    last.then_inc(turn, 1)
                    act.wait_ge(turn, ahead(i, "front", "lnw"))
                    act.copy(v_tok[:], bank[3][:])
                    act.copy(w_tok[:], bank[5][:])
                    act.activation(lnw[:], pairs(bank[4])[:, :, 0], ACT.Ln, bias=l2eps[:]).then_inc(turn, 1)
                    act.wait_ge(turn, ahead(i, "front", "rw"))
                    act.activation(rw[:], lnw[:], ACT.Exp, scale=-0.5).then_inc(turn, 1)
                    with act.Fori(0, LEVELS) as level:
                        act.wait_ge(turn, ahead(i, "scores", "decay", level))
                        act.activation(decay[:], bank[1][:], ACT.Exp).then_inc(turn, 1)
                    act.wait_ge(turn, ahead(i, "softmax", "exps"))
                    for p in range(NP):
                        last = act.activation(pc(probs, p), pc(score, p), ACT.Exp, bias=nmax[:, p:p + 1],
                                              scale=SCALE, accum_out=Z[:, p:p + 1])
                    last.then_inc(turn, 1)
                    act.wait_ge(turn, ahead(i, "softmax", "probs_chan"))
                    act.copy(probs_chan[:], bank[3][:]).then_inc(turn, 1)
                    with act.Fori(0, LEVELS) as level:
                        act.wait_ge(turn, ahead(i, "values", "decay", level))
                        act.activation(decay[:], bank[1][:], ACT.Exp).then_inc(turn, 1)
                    act.wait_ge(turn, ahead(i, "outputs", "osq"))
                    for p in range(NP):
                        last = act.activation(pc(osq, p), pc(bank[4], p), ACT.Square, accum_out=ssq[:, p:p + 1])
                    last.then_inc(turn, 1)
                    act.wait_ge(turn, ahead(i, "outputs", "lny"))
                    act.activation(lny[:], y[:], ACT.Ln).then_inc(turn, 1)
                    act.wait_ge(turn, ahead(i, "outputs", "rho"))
                    act.activation(rho[:], lny[:], ACT.Exp, scale=-0.5).then_inc(turn, 1)

            when_far(act, units)

        @block.vector
        def _(dve):
            def first():
                dve.sem_inc(group_out, 1)
                dve.wait_ge(x_back, 16)

            def units():
                with dve.Fori(0, GROUPS) as g:
                    with dve.Fori(0, H) as h:
                        unit(g * H + h)
                    dve.wait_ge(turn, through(g * H + (H - 1), "outputs", "wo"))
                    for m in range(2):
                        xs = x_all[:, bass.ds(g * NP + 2 * m, 2), :]
                        last = dve.tensor_tensor(xs, xs, outacc[m][:], ALU.add)
                    last.then_inc(group_out, 1)

            def unit(i):
                for shift in range(1, TAPS):
                    dve.wait_ge(turn, ahead(i, "front", f"conv{shift}"))
                    if shift == 1:
                        dve.scalar_tensor_tensor(out=glog[:], in0=bank[4][:], scalar=0.0, in1=gtmp[:], op0=ALU.min,
                                                 op1=ALU.subtract)
                    for n, t in enumerate((q, k, v, w)):
                        x3 = bank[n][:].rearrange("p (s t) -> p s t", s=NS)
                        d3 = t[:].rearrange("p (s t) -> p s t", s=NS)
                        c = W_CONV + TAPS * n + TAPS - 1 - shift
                        last = dve.scalar_tensor_tensor(out=d3[:, :, shift:T], in0=x3[:, :, 0:T - shift],
                                                        scalar=hw[:, c:c + 1], in1=d3[:, :, shift:T],
                                                        op0=ALU.mult, op1=ALU.add)
                    last.then_inc(turn, 1)
                dve.wait_ge(turn, ahead(i, "front", "coef"))
                dve.memset(score[:], 0.0)
                dve.memset(mix[:], 0.0)
                dve.tensor_tensor(coef[:], rw[:], beta.rearrange("p g h q -> p (g h q)")[:, bass.ts(i, NP)],
                                  ALU.mult).then_inc(turn, 1)
                with dve.Fori(0, LEVELS) as level:
                    dve.wait_ge(turn, ahead(i, "scores", "qk", level))
                    for p in range(NP):
                        last = dve.scalar_tensor_tensor(out=pc(qk, p), in0=pc(bank[0], p), scalar=coef[:, p:p + 1],
                                                        in1=mask, op0=ALU.mult, op1=ALU.mult)
                    last.then_inc(turn, 1)
                    dve.wait_ge(turn, ahead(i, "scores", "decayed", level))
                    dve.tensor_tensor(part[:], bank[2][:], decay[:], ALU.mult).then_inc(turn, 1)
                    dve.wait_ge(turn, ahead(i, "scores", "summed", level))
                    dve.tensor_tensor(score[:], score[:], part[:], ALU.add).then_inc(turn, 1)
                dve.wait_ge(turn, ahead(i, "softmax", "smax"))
                dve.tensor_reduce(smax[:], pairs(score), AX.X, ALU.max).then_inc(turn, 1)
                dve.wait_ge(turn, ahead(i, "softmax", "nmax"))
                dve.tensor_scalar(nmax[:], smax[:], -SCALE, None, ALU.mult).then_inc(turn, 1)
                dve.wait_ge(turn, ahead(i, "softmax", "Zeps"))
                dve.scalar_tensor_tensor(out=Zeps[:], in0=Z[:], scalar=4.0 * EPS, in1=Z[:], op0=ALU.mult,
                                         op1=ALU.mult).then_inc(turn, 1)
                with dve.Fori(0, LEVELS) as level:
                    dve.wait_ge(turn, ahead(i, "values", "masked", level))
                    for p in range(NP):
                        last = dve.scalar_tensor_tensor(out=pc(part, p), in0=pc(bank[2], p), scalar=coef[:, p:p + 1],
                                                        in1=mask, op0=ALU.mult, op1=ALU.mult)
                    last.then_inc(turn, 1)
                    dve.wait_ge(turn, ahead(i, "values", "summed", level))
                    dve.tensor_tensor(mix[:], mix[:], part[:], ALU.add).then_inc(turn, 1)
                dve.wait_ge(turn, ahead(i, "outputs", "y"))
                dve.scalar_tensor_tensor(out=y[:], in0=ssq[:], scalar=4.0 / P, in1=Zeps[:], op0=ALU.mult,
                                         op1=ALU.add).then_inc(turn, 1)
                dve.wait_ge(turn, ahead(i, "outputs", "o_tok"))
                for p in range(NP):
                    last = dve.tensor_scalar(pc(o_tok, p), pc(bank[4], p), rho[:, p:p + 1], None, ALU.mult)
                last.then_inc(turn, 1)
                dve.wait_ge(turn, ahead(i, "outputs", "o_chan"))
                dve.scalar_tensor_tensor(out=o_chan[:], in0=gate[:], scalar=1.0, in1=bank[5][:], op0=ALU.add,
                                         op1=ALU.mult).then_inc(turn, 1)

            when_far(dve, units, first)


def context_block(nc, sems, ctx_all, ctxT, gqk, xT_pad, ident, load):
    with ExitStack() as ctx:
        def sem(name):
            return sems(name)

        banks = [ctx.enter_context(nc.psum_tensor(f"ctx_turned{k}", [P, G], F32)) for k in range(2)]
        gq_gk = ctx.enter_context(nc.sbuf_tensor("gq_gk", [P, 2], F32))
        loaded = sem("ctx_loaded")
        turned = sem("ctx_turned")
        kept = sem("ctx_kept")
        gqk_done = sem("gqk_done")
        padded = sem("ctx_padded")
        block = ctx.enter_context(nc.Block())

        @block.sync
        def _(sp):
            for dst, src in load:
                sp.dma_start(gq_gk[:] if dst is None else dst, src).then_inc(loaded, 16)

        @block.gpsimd
        def _(pool):
            pool.memset(ctxT[:, TOKENS:TOKENS + G], 0.0).then_inc(padded, 1)
            pool.memset(xT_pad, 0.0).then_inc(padded, 1)

        @block.tensor
        def _(pe):
            pe.wait_ge(loaded, 16 * len(load))
            for g in range(GROUPS):
                if g >= 2:
                    pe.wait_ge(kept, g - 1)
                for p in range(NP):
                    last = pe.transpose(banks[g % 2][:, p * P:(p + 1) * P], ctx_all[:, g * NP + p, :], ident)
                last.then_inc(turned, 1)

        @block.scalar
        def _(act):
            for g in range(GROUPS):
                act.wait_ge(turned, g + 1)
                act.copy(ctxT[:, g * G:(g + 1) * G], banks[g % 2][:]).then_inc(kept, 1)

        @block.vector
        def _(dve):
            dve.wait_ge(loaded, 16 * len(load))
            dve.tensor_tensor(gqk[:], gq_gk[:, 0:1], gq_gk[:, 1:2], ALU.mult).then_inc(gqk_done, 1)


def cross_block(nc, sems, w_heads, x_all, xT_all, ctxT, gqk, Wo, ident):
    with ExitStack() as ctx:
        def sb(name, shape, dt=F32):
            return ctx.enter_context(nc.sbuf_tensor(f"x_{name}", shape, dt))

        def psum(name, shape, dt=F32):
            return ctx.enter_context(nc.psum_tensor(f"x_{name}", shape, dt))

        def sem(name):
            return sems(f"x_{name}")

        hw = [sb(f"head_weights{i}", [P, X_HEAD]) for i in range(2)]
        ctxg = sb("ctxg", [P, G])
        q = sb("q_chan", [P, G])
        q2 = sb("q2", [P, G])
        ksq = sb("ksq", [P, G])
        k_tok = sb("k_tok", [P, G])
        k = sb("k_chan", [P, G])
        v_tok = sb("v_tok", [P, G])
        score = sb("score", [P, NP, T])
        probs = sb("probs", [P, NP, T])
        wide = sb("wide", [P, NP, P])
        wide_chan = sb("wide_chan", [P, G])
        o_chan = sb("o_chan", [P, G])
        ones = sb("ones", [P, 1])
        eps = sb("eps", [P, 1])
        zeros = sb("zeros", [P, G], BF16)
        ssk = sb("ssk", [P, NP])
        ln2 = sb("ln2", [P, 2, NP])
        rk_rq = sb("rk_rq", [P, 2, NP])
        rq = sb("rq", [P, NP])
        smax = sb("smax", [P, NP])
        Z = sb("Z", [P, NP])
        rZ = sb("rZ", [P, NP])
        bank0, bank1, bank2, bank3, bank4, bank5 = (psum(f"bank{n}", [P, G]) for n in range(6))
        outacc = [psum(f"outacc{n}", [P, 2, HID]) for n in range(2)]

        primed = {
            "tensor": "xq xk xv qss kT scores probsT o wo",
            "scalar": "q_s q2_s ksq_s lnk lnq rkq exps wide_chan_s o_chan_s v_s k_s",
            "vector": "score_s smax_s sub_s Z_s rZ_s wide_s k_tok_s rq_s",
            "gpsimd": "ctxg_s",
        }
        S = {n: sem(n) for names in primed.values() for n in names.split()}
        weights_in = [sem(f"weights_in{i}") for i in range(2)]
        consts_set = sem("consts_set")
        group_out = sem("group_out")
        block = ctx.enter_context(nc.Block())

        def prime(eng, who):
            for n in primed[who].split():
                eng.sem_inc(S[n], 1)

        def done(n, times=1):
            return times * (n + 1) + 1

        def before(n, times=1):
            return times * n + 1

        def run_units(eng, front, merged, group_start=None, group_end=None):
            front(0, 0)
            with eng.Fori(0, GROUPS) as g:
                if group_start is not None:
                    group_start(g)
                with eng.Fori(0, H // 2) as j:
                    for par in range(2):
                        merged(g * H + j * 2 + par, j * 2 + par, par)
                if group_end is not None:
                    group_end(g)

        def pc(t, p):
            return t[:, p * P:(p + 1) * P]

        def over(t, n):
            return t.unsqueeze(2).broadcast_to([P, NP, n])

        @block.sync
        def _(sp):
            def load(n, h, par):
                sp.dma_start(hw[par][:], w_heads[h]).then_inc(weights_in[par], 16)

            load(0, 0, 0)
            load(1, 1, 1)
            with sp.Fori(0, UNITS // 2 - 1) as m:
                for par in range(2):
                    n = 2 * m + par
                    sp.wait_ge(S["xv"], done(n))
                    load(n + 2, (n + 2) % H, par)
            sp.wait_ge(S["xv"], done(UNITS - 2))
            load(UNITS, 0, 0)

        @block.gpsimd
        def _(pool):
            prime(pool, "gpsimd")
            pool.memset(ones[:], 1.0).then_inc(consts_set, 1)
            pool.memset(eps[:], EPS).then_inc(consts_set, 1)
            pool.memset(zeros[:], 0.0).then_inc(consts_set, 1)
            pool.memset(wide[:], 0.0).then_inc(consts_set, 1)

            def front(n, par):
                pool.wait_ge(S["xv"], before(n))
                pool.tensor_copy(ctxg[:], ctxT[:, bass.ts(n // H, G)]).then_inc(S["ctxg_s"], 1)

            def merged(i, h, par):
                front(i + 1, 1 - par)

            run_units(pool, front, merged)

        @block.tensor
        def _(pe):
            prime(pe, "tensor")
            pe.wait_ge(consts_set, 4)

            def f_q(n, par):
                pe.wait_ge(weights_in[par], 16 * (n // 2 + 1))
                pe.wait_ge(S["lnq"], before(n))
                for kk in range(KH):
                    last = pe.matmul(bank0[:], hw[par][:, X_Q + kk * P:X_Q + (kk + 1) * P],
                                     xT_all[:, kk, bass.ts(n // H, G)], start=(kk == 0), stop=(kk == KH - 1))
                last.then_inc(S["xq"], 1)

            def f_k(n, par):
                pe.wait_ge(S["ctxg_s"], done(n))
                pe.wait_ge(S["k_tok_s"], before(n))
                for p in range(NP):
                    last = pe.matmul(pc(bank1, p), pc(ctxg, p), hw[par][:, X_K:X_K + P], start=True, stop=True)
                last.then_inc(S["xk"], 1)

            def f_v(n, par):
                pe.wait_ge(S["v_s"], before(n))
                for p in range(NP):
                    last = pe.matmul(pc(bank4, p), pc(ctxg, p), hw[par][:, X_V:X_V + P], start=True, stop=True)
                last.then_inc(S["xv"], 1)

            def f_qss(n, par):
                pe.wait_ge(S["q2_s"], done(n))
                pe.wait_ge(S["q_s"], done(n))
                for p in range(NP):
                    last = pe.matmul(bank0[:, p:p + 1], pc(q2, p), ones[:], start=True, stop=True)
                last.then_inc(S["qss"], 1)

            def f_kT(n, par):
                pe.wait_ge(S["k_tok_s"], done(n))
                pe.wait_ge(S["k_s"], before(n))
                for p in range(NP):
                    last = pe.transpose(pc(bank3, p), pc(k_tok, p), ident)
                last.then_inc(S["kT"], 1)

            def front(n, par):
                f_q(n, par)
                f_k(n, par)
                f_v(n, par)
                f_qss(n, par)
                f_kT(n, par)

            def merged(i, h, par):
                n, npar = i + 1, 1 - par
                pe.wait_ge(S["k_s"], done(i))
                pe.wait_ge(S["q_s"], done(i))
                pe.wait_ge(S["o_chan_s"], before(i))
                for p in range(NP):
                    for half in range(2):
                        at = slice(p * P + half * T, p * P + (half + 1) * T)
                        last = pe.matmul(bank2[half * T:(half + 1) * T, p * T:(p + 1) * T], q[:, at], k[:, at],
                                         start=True, stop=True)
                last.then_inc(S["scores"], 1)
                f_q(n, npar)
                f_k(n, npar)
                pe.wait_ge(S["wide_s"], done(i, 2))
                pe.wait_ge(S["wide_chan_s"], before(i))
                for p in range(NP):
                    last = pe.transpose(pc(bank5, p), wide[:, p, :], ident)
                last.then_inc(S["probsT"], 1)
                f_v(n, npar)
                f_qss(n, npar)
                pe.wait_ge(S["wide_chan_s"], done(i))
                for p in range(NP):
                    last = pe.matmul(pc(bank2, p), pc(v_tok, p), pc(wide_chan, p), start=True, stop=True)
                last.then_inc(S["o"], 1)
                f_kT(n, npar)
                pe.wait_ge(S["o_chan_s"], done(i))
                for p in range(NP):
                    last = pe.matmul(outacc[p // 2][:, p % 2, :], pc(o_chan, p), Wo[:, bass.ts(h, HID)],
                                     start=False, stop=False, skip_group_check=True)
                last.then_inc(S["wo"], 1)

            def group_start(g):
                pe.wait_ge(group_out, g + 1)
                for n in range(2):
                    pe.matmul(outacc[n][:].rearrange("p a c -> p (a c)"), zeros[:, 0:P], zeros[:],
                              start=True, stop=False, skip_group_check=True)

            run_units(pe, front, merged, group_start=group_start)

        @block.scalar
        def _(act):
            act.preload_act_table_set("natural_log_exp_and_others")
            prime(act, "scalar")
            act.wait_ge(consts_set, 4)

            def f_q(n, par):
                act.wait_ge(S["xq"], done(n))
                act.wait_ge(S["scores"], before(n))
                act.copy(q[:], bank0[:]).then_inc(S["q_s"], 1)
                act.wait_ge(S["qss"], before(n))
                act.activation(q2[:], bank0[:], ACT.Square).then_inc(S["q2_s"], 1)

            def f_ksq(n, par):
                act.wait_ge(S["xk"], done(n))
                act.wait_ge(S["lnk"], before(n))
                for p in range(NP):
                    act.activation(pc(ksq, p), pc(bank1, p), ACT.Square, accum_out=ssk[:, p:p + 1])\
                        .then_inc(S["ksq_s"], 1)

            def f_norms(n, par):
                act.wait_ge(S["ksq_s"], done(n, NP))
                act.wait_ge(S["rkq"], before(n))
                act.activation(ln2[:, 0, :], ssk[:], ACT.Ln, bias=eps[:], scale=1.0 / P).then_inc(S["lnk"], 1)
                act.wait_ge(S["qss"], done(n))
                act.activation(ln2[:, 1, :], bank0[:, 0:NP], ACT.Ln, bias=eps[:], scale=1.0 / P)\
                    .then_inc(S["lnq"], 1)
                act.wait_ge(S["lnk"], done(n))
                act.wait_ge(S["lnq"], done(n))
                act.wait_ge(S["k_tok_s"], before(n))
                act.wait_ge(S["rq_s"], before(n))
                act.activation(rk_rq[:], ln2[:], ACT.Exp, scale=-0.5).then_inc(S["rkq"], 1)

            def f_v(n, par):
                act.wait_ge(S["xv"], done(n))
                act.wait_ge(S["o"], before(n))
                act.copy(v_tok[:], bank4[:]).then_inc(S["v_s"], 1)

            def f_k(n, par):
                act.wait_ge(S["kT"], done(n))
                act.wait_ge(S["scores"], before(n))
                act.activation(k[:], bank3[:], ACT.Copy, scale=gqk[:]).then_inc(S["k_s"], 1)

            def front(n, par):
                f_q(n, par)
                f_ksq(n, par)
                f_norms(n, par)
                f_v(n, par)
                f_k(n, par)

            def merged(i, h, par):
                n, npar = i + 1, 1 - par
                act.wait_ge(S["sub_s"], done(i))
                act.wait_ge(S["wide_s"], before(i, 2))
                act.activation(probs[:], score[:], ACT.Exp, scale=SCALE).then_inc(S["exps"], 1)
                f_q(n, npar)
                f_ksq(n, npar)
                act.wait_ge(S["probsT"], done(i))
                act.wait_ge(S["o"], before(i))
                act.copy(wide_chan[:], bank5[:]).then_inc(S["wide_chan_s"], 1)
                f_norms(n, npar)
                act.wait_ge(S["o"], done(i))
                act.wait_ge(S["wo"], before(i))
                act.copy(o_chan[:], bank2[:]).then_inc(S["o_chan_s"], 1)
                f_v(n, npar)
                f_k(n, npar)

            run_units(act, front, merged)

        @block.vector
        def _(dve):
            prime(dve, "vector")
            dve.sem_inc(group_out, 1)
            dve.wait_ge(consts_set, 4)

            def front(n, par):
                dve.wait_ge(S["rkq"], done(n))
                dve.wait_ge(S["score_s"], before(n))
                dve.tensor_copy(rq[:], rk_rq[:, 1, :]).then_inc(S["rq_s"], 1)
                dve.wait_ge(S["kT"], before(n))
                for p in range(NP):
                    last = dve.tensor_scalar(pc(k_tok, p), pc(bank1, p), rk_rq[:, 0, p:p + 1], None, ALU.mult)
                last.then_inc(S["k_tok_s"], 1)

            def merged(i, h, par):
                s3 = bank2[:, 0:NP * T].rearrange("p (q t) -> p q t", q=NP)
                dve.wait_ge(S["scores"], done(i))
                dve.wait_ge(S["rq_s"], done(i))
                dve.wait_ge(S["exps"], before(i))
                dve.tensor_tensor(score[:], s3, over(rq[:], T), ALU.mult).then_inc(S["score_s"], 1)
                dve.wait_ge(S["score_s"], done(i))
                dve.tensor_reduce(smax[:], score[:], AX.X, ALU.max).then_inc(S["smax_s"], 1)
                dve.wait_ge(S["smax_s"], done(i))
                dve.tensor_tensor(score[:], score[:], over(smax[:], T), ALU.subtract).then_inc(S["sub_s"], 1)
                dve.wait_ge(S["exps"], done(i))
                dve.tensor_reduce(Z[:], probs[:], AX.X, ALU.add).then_inc(S["Z_s"], 1)
                dve.wait_ge(S["Z_s"], done(i))
                dve.reciprocal(rZ[:], Z[:]).then_inc(S["rZ_s"], 1)
                dve.wait_ge(S["rZ_s"], done(i))
                dve.wait_ge(S["probsT"], before(i))
                for half in range(2):
                    rows = slice(half * T, (half + 1) * T)
                    dve.tensor_tensor(wide[rows, :, half * T:(half + 1) * T], probs[rows, :, :],
                                      over(rZ[:], T)[rows], ALU.mult).then_inc(S["wide_s"], 1)
                front(i + 1, 1 - par)

            def group_end(g):
                dve.wait_ge(S["wo"], before(g * H + H))
                for m in range(2):
                    xs = x_all[:, bass.ds(g * NP + 2 * m, 2), :]
                    last = dve.tensor_tensor(xs, xs, outacc[m][:], ALU.add)
                last.then_inc(group_out, 1)

            run_units(dve, front, merged, group_end=group_end)


def experts_block(nc, sems, x_all, xT_all, gate_w, experts, expert_b, lower, ident, load, out_view):
    EP = E // 2
    RING = 4
    with ExitStack() as ctx:
        def sb(name, shape, dt=F32):
            return ctx.enter_context(nc.sbuf_tensor(f"e_{name}", shape, dt))

        def psum(name, shape, dt=F32):
            return ctx.enter_context(nc.psum_tensor(f"e_{name}", shape, dt))

        def sem(name):
            return sems(f"e_{name}")

        xg = [sb(f"xg{i}", [P, KH, G]) for i in range(2)]
        logits = sb("logits", [P, NP, E])
        above = sb("above", [P, NP, E, E])
        ties = sb("ties", [P, NP, E, E])
        rank = sb("rank", [P, NP, E])
        top = sb("top", [P, NP])
        shifted = sb("shifted", [P, NP, E])
        ex = sb("ex", [P, NP, E])
        chosen = sb("chosen", [P, NP, E])
        Z = sb("Z", [P, NP])
        rZ = sb("rZ", [P, NP])
        gates = sb("gates", [P, NP, E])
        gatesT = sb("gatesT", [E, G])
        y = [psum(f"y{i}", [P, 2, HID]) for i in range(RING)]
        small = psum("small", [P, NP, E])
        gT = psum("gT", [E, G])
        bias = [psum(f"bias{i}", [P, 2, HID]) for i in range(2)]

        primed = {
            "tensor": "logit gatesT_x bias_x y_x",
            "scalar": "exps gatesT_s",
            "vector": "logits_s above_s ties_s tied_s beats_s rank_s top_s shifted_s chosen_s Z_s rZ_s gates_s "
                      "biased y_s",
            "gpsimd": "xg_s",
        }
        S = {n: sem(n) for names in primed.values() for n in names.split()}
        loaded = sem("loaded")
        stored = sem("stored")
        block = ctx.enter_context(nc.Block())
        YS = NP * EP

        def prime(eng, who):
            for n in primed[who].split():
                eng.sem_inc(S[n], 1)

        def done(n, times=1):
            return times * (n + 1) + 1

        def before(n, times=1):
            return times * n + 1

        def over(t, n):
            return t.unsqueeze(2).broadcast_to([P, NP, n])

        @block.sync
        def _(sp):
            for dst, src in load:
                sp.dma_start(dst, src).then_inc(loaded, 16)
            with sp.Fori(0, GROUPS) as g:
                sp.wait_ge(S["y_s"], done(g, 2 * YS))
                sp.dma_start(out_view[:, bass.ds(g * NP, NP), :], x_all[:, bass.ds(g * NP, NP), :])\
                    .then_inc(stored, 16)
            sp.wait_ge(stored, 16 * GROUPS)

        @block.gpsimd
        def _(pool):
            prime(pool, "gpsimd")
            with pool.Fori(0, GROUPS // 2) as m:
                for par in range(2):
                    g = 2 * m + par
                    pool.wait_ge(S["y_x"], before(g, YS))
                    pool.tensor_copy(xg[par][:], xT_all[:, :, bass.ts(g, G)]).then_inc(S["xg_s"], 1)

        @block.tensor
        def _(pe):
            prime(pe, "tensor")
            pe.wait_ge(loaded, 16 * len(load))
            with pe.Fori(0, GROUPS // 2) as m:
                for par in range(2):
                    g = 2 * m + par
                    pe.wait_ge(S["xg_s"], done(g))
                    pe.wait_ge(S["logits_s"], before(g))
                    for p in range(NP):
                        for k in range(KH):
                            last = pe.matmul(small[:, p, :], xg[par][:, k, p * P:(p + 1) * P], gate_w[:, k, :],
                                             start=(k == 0), stop=(k == KH - 1))
                    last.then_inc(S["logit"], 1)
                    for p in range(NP):
                        for ep in range(EP):
                            u = p * EP + ep
                            pe.wait_ge(S["y_s"], before(g, 2 * YS) + 2 * (u + 1 - RING) if u >= RING
                                       else before(g, 2 * YS))
                            for k in range(KH):
                                last = pe.matmul(y[u % RING][:].rearrange("p a c -> p (a c)"),
                                                 xg[par][:, k, p * P:(p + 1) * P],
                                                 experts[:, k, 2 * ep:2 * ep + 2, :].rearrange("p a c -> p (a c)"),
                                                 start=(k == 0), stop=(k == KH - 1))
                            last.then_inc(S["y_x"], 1)
                            if u == RING - 1:
                                pe.wait_ge(S["gates_s"], done(g))
                                for pp in range(NP):
                                    last = pe.transpose(gT[:, pp * P:(pp + 1) * P], gates[:, pp, :], ident)
                                last.then_inc(S["gatesT_x"], 1)
                                pe.wait_ge(S["gatesT_s"], done(g))
                                pe.wait_ge(S["biased"], before(g))
                                for pp in range(NP):
                                    last = pe.matmul(bias[pp // 2][:, pp % 2, :], gatesT[:, pp * P:(pp + 1) * P],
                                                     expert_b[:], start=True, stop=True)
                                last.then_inc(S["bias_x"], 1)

        @block.scalar
        def _(act):
            prime(act, "scalar")
            with act.Fori(0, GROUPS) as g:
                act.wait_ge(S["shifted_s"], done(g))
                act.wait_ge(S["chosen_s"], before(g))
                act.activation(ex[:], shifted[:], ACT.Exp).then_inc(S["exps"], 1)
                act.wait_ge(S["gatesT_x"], done(g))
                act.wait_ge(S["bias_x"], before(g))
                act.copy(gatesT[:], gT[:]).then_inc(S["gatesT_s"], 1)

        @block.vector
        def _(dve):
            prime(dve, "vector")
            dve.wait_ge(loaded, 16 * len(load))
            theirs = logits[:].unsqueeze(2).broadcast_to([P, NP, E, E])
            own = logits[:].unsqueeze(3).broadcast_to([P, NP, E, E])
            earlier = lower.rearrange("p (a b) -> p a b", a=E).unsqueeze(1).broadcast_to([P, NP, E, E])
            with dve.Fori(0, GROUPS) as g:
                dve.wait_ge(S["logit"], done(g))
                dve.wait_ge(S["shifted_s"], before(g))
                dve.tensor_copy(logits[:], small[:]).then_inc(S["logits_s"], 1)
                dve.wait_ge(S["logits_s"], done(g))
                dve.tensor_tensor(above[:], theirs, own, ALU.is_gt).then_inc(S["above_s"], 1)
                dve.tensor_tensor(ties[:], theirs, own, ALU.is_equal).then_inc(S["ties_s"], 1)
                dve.wait_ge(S["ties_s"], done(g))
                dve.tensor_tensor(ties[:], ties[:], earlier, ALU.mult).then_inc(S["tied_s"], 1)
                dve.wait_ge(S["tied_s"], done(g))
                dve.wait_ge(S["above_s"], done(g))
                dve.tensor_tensor(above[:], above[:], ties[:], ALU.add).then_inc(S["beats_s"], 1)
                dve.wait_ge(S["beats_s"], done(g))
                dve.tensor_reduce(rank[:], above[:], AX.X, ALU.add).then_inc(S["rank_s"], 1)
                dve.tensor_reduce(top[:], logits[:], AX.X, ALU.max).then_inc(S["top_s"], 1)
                dve.wait_ge(S["top_s"], done(g))
                dve.wait_ge(S["exps"], before(g))
                dve.tensor_tensor(shifted[:], logits[:], over(top[:], E), ALU.subtract).then_inc(S["shifted_s"], 1)
                dve.wait_ge(S["exps"], done(g))
                dve.wait_ge(S["rank_s"], done(g))
                dve.scalar_tensor_tensor(out=chosen[:], in0=rank[:], scalar=TOPK - 0.5, in1=ex[:], op0=ALU.is_lt,
                                         op1=ALU.mult).then_inc(S["chosen_s"], 1)
                dve.wait_ge(S["chosen_s"], done(g))
                dve.tensor_reduce(Z[:], chosen[:], AX.X, ALU.add).then_inc(S["Z_s"], 1)
                dve.wait_ge(S["Z_s"], done(g))
                dve.reciprocal(rZ[:], Z[:]).then_inc(S["rZ_s"], 1)
                dve.wait_ge(S["rZ_s"], done(g))
                dve.wait_ge(S["bias_x"], before(g))
                dve.tensor_tensor(gates[:], chosen[:], over(rZ[:], E), ALU.mult).then_inc(S["gates_s"], 1)
                dve.wait_ge(S["gates_s"], done(g))
                for p in range(NP):
                    xp = x_all[:, g * NP + p, :]
                    for ex_ in range(E):
                        u = p * EP + ex_ // 2
                        dve.wait_ge(S["y_x"], before(g, YS) + u + 1)
                        if p + ex_ > 0:
                            dve.wait_ge(S["y_s"], before(g, 2 * YS) + p * E + ex_)
                        dve.scalar_tensor_tensor(out=xp, in0=y[u % RING][:, ex_ % 2, :],
                                                 scalar=gates[:, p, ex_:ex_ + 1], in1=xp, op0=ALU.mult,
                                                 op1=ALU.add).then_inc(S["y_s"], 1)
                    if p == 0:
                        dve.wait_ge(S["bias_x"], done(g))
                        dve.wait_ge(S["y_s"], before(g, 2 * YS) + E)
                        for m in range(2):
                            xs = x_all[:, bass.ds(g * NP + 2 * m, 2), :]
                            last = dve.tensor_tensor(xs, xs, bias[m][:], ALU.add)
                        last.then_inc(S["biased"], 1)
                        dve.wait_ge(S["biased"], done(g))


def decoder_layer(nc, ins, outs):
    with ExitStack() as ctx:
        def sb(name, shape, dt=F32):
            return ctx.enter_context(nc.sbuf_tensor(name, shape, dt))

        x_all = sb("x_all", [P, PAIRS, HID])
        cst = sb("cst", [P, 3 * P + E * E])
        lower = cst[:, 3 * P:3 * P + E * E]
        ident, span, causal = cst[:, 0:P], cst[:, P:2 * P], cst[:, 2 * P:3 * P]
        far_flag = sb("far_flag", [1, 1], mybir.dt.int32)
        x_view = ins["x"].rearrange("b t c -> (b t) c").rearrange("(q p) c -> p q c", p=P)
        o_view = outs[0].rearrange("b t c -> (b t) c").rearrange("(q p) c -> p q c", p=P)

        with ExitStack() as stage:
            sems = stage.enter_context(stage_semaphores(nc))

            def st(name, shape, dt=F32):
                return stage.enter_context(nc.sbuf_tensor(name, shape, dt))

            xT_all = st("xT_all", [P, KH, TOKENS + G])
            f1T = st("f1T", [P, TOKENS + G])
            g1T = st("g1T", [P, TOKENS + G])
            beta = st("beta", [P, GROUPS + 1, H, NP])
            Wf1g1 = st("Wf1g1", [P, KH, 2, P])
            Wb = st("Wb", [P, KH, H])
            Wo = st("Wo", [P, H * HID])
            norm_w = st("norm_w", [P, 1])
            layernorm_block(nc, sems, "ln1", x_all, xT_all, ident, load=[
                (cst[:], ins["consts"]), (x_all[:], x_view), (Wf1g1[:], ins["Wf1g1"]), (Wb[:], ins["Wb"]),
                (norm_w[:], ins["norm_w"]), (Wo[:], ins["Wo"])])
            lowrank_block(nc, sems, xT_all, f1T, g1T, beta[:, 0:GROUPS], Wf1g1, Wb, ident, None)
            wo_scaled = sems("wo_scaled")
            with nc.Block() as block:
                @block.vector
                def _(dve):
                    dve.tensor_scalar(Wo[:], Wo[:], norm_w[:], None, ALU.mult).then_inc(wo_scaled, 1)

                @block.gpsimd
                def _(pool):
                    pool.memset(xT_all[:, :, TOKENS:TOKENS + G], 0.0).then_inc(wo_scaled, 1)
                    pool.memset(f1T[:, TOKENS:TOKENS + G], 0.0).then_inc(wo_scaled, 1)
                    pool.memset(g1T[:, TOKENS:TOKENS + G], 0.0).then_inc(wo_scaled, 1)
                    pool.memset(beta[:, GROUPS:GROUPS + 1], 0.0).then_inc(wo_scaled, 1)
            gsa_block(nc, sems, ins["w_heads"], x_all, xT_all, f1T, g1T, beta[:], Wo, (ident, span, causal),
                      far_flag)
            with stage_semaphores(nc) as general_sems:
                gsa_general_block(nc, general_sems, ins["w_heads"], ins["tables"], x_all, x_view, xT_all, f1T, g1T,
                                  beta[:], Wo, (ident, span, causal), far_flag)
        with ExitStack() as stage:
            sems = stage.enter_context(stage_semaphores(nc))

            def st(name, shape, dt=F32):
                return stage.enter_context(nc.sbuf_tensor(name, shape, dt))

            xT_all = st("xT2_all", [P, KH, TOKENS + G])
            ctxT = st("ctxT", [P, TOKENS + G])
            ctx_all = st("ctx_all", [P, PAIRS, CDIM])
            gqk = st("gqk", [P, 1])
            xWo = st("xWo", [P, H * HID])
            c_view = ins["ctx"].rearrange("b t c -> (b t) c").rearrange("(q p) c -> p q c", p=P)
            layernorm_block(nc, sems, "ln2", x_all, xT_all, ident)
            context_block(nc, sems, ctx_all, ctxT, gqk, xT_all[:, :, TOKENS:TOKENS + G], ident,
                          [(ctx_all[:], c_view), (None, ins["gq_gk"]), (xWo[:], ins["xWo"])])
            cross_block(nc, sems, ins["x_heads"], x_all, xT_all, ctxT, gqk, xWo, ident)
        with ExitStack() as stage:
            sems = stage.enter_context(stage_semaphores(nc))

            def st(name, shape, dt=F32):
                return stage.enter_context(nc.sbuf_tensor(name, shape, dt))

            xT_all = st("xT3_all", [P, KH, TOKENS])
            gate_w = st("gate_w", [P, KH, E])
            experts = st("experts", [P, KH, E, HID])
            expert_b = st("expert_b", [E, HID])
            layernorm_block(nc, sems, "ln3", x_all, xT_all, ident)
            experts_block(nc, sems, x_all, xT_all, gate_w, experts, expert_b, lower, ident,
                          [(gate_w[:], ins["gate_w"]), (experts[:], ins["experts"]), (expert_b[:], ins["expert_b"])],
                          o_view)


def layout(inputs):
    a = {n: np.ascontiguousarray(v) for n, v in inputs.items()}

    def by_head(w):
        rows = w.shape[0]
        return w.reshape(rows // P, P, H, P).transpose(2, 1, 0, 3).reshape(H, P, -1)

    conv = np.stack([a[f"L0_attn_c{n}"].reshape(H, P, TAPS) for n in "qkv"] +
                    [a["L0_attn_cv"].reshape(H, P, TAPS)], axis=2).reshape(H, P, 4 * TAPS)
    w_heads = np.concatenate(
        [by_head(a[f"L0_attn_W{n}"]) for n in "qkvw"] + [by_head(a["L0_attn_Wf2"]), by_head(a["L0_attn_Wg2"]),
         conv, a["L0_attn_bg2"].reshape(H, P, 1)], axis=2)
    f1g1 = np.stack([a["L0_attn_Wf1"].reshape(KH, P, P), a["L0_attn_Wg1"].reshape(KH, P, P)], axis=2)
    return {
        "x": a["x"],
        "consts": shape_constants(),
        "tables": level_tables(),
        "w_heads": w_heads,
        "Wf1g1": f1g1.transpose(1, 0, 2, 3),
        "Wb": a["L0_attn_Wb"].reshape(KH, P, H).transpose(1, 0, 2),
        "norm_w": a["L0_attn_norm_w"].reshape(P, 1),
        "ctx": a["ctx_1024"],
        "x_heads": np.concatenate([by_head(a[f"L0_xattn_W{n}"]) for n in "qkv"], axis=2),
        "gq_gk": np.stack([a["L0_xattn_gq"], a["L0_xattn_gk"]], axis=1),
        "xWo": a["L0_xattn_Wo"].reshape(H, P, HID).transpose(1, 0, 2).reshape(P, H * HID),
        "gate_w": a["L0_ffn_gate_w"].T.reshape(KH, P, E).transpose(1, 0, 2),
        "experts": a["L0_ffn_expert_w"].reshape(E, KH, P, HID).transpose(2, 1, 0, 3),
        "expert_b": a["L0_ffn_expert_b"],
        "Wo": a["L0_attn_Wo"].reshape(H, P, HID).transpose(1, 0, 2).reshape(P, H * HID),
    }


def kernel(**inputs):
    import concourse.bacc as _bacc
    from concourse.bass_utils import run_bass_kernel_spmd as _run

    nc = _bacc.Bacc("TRN2", target_bir_lowering=False, num_devices=1)
    arrays, aps = {}, {}
    for name, a in layout(inputs).items():
        a = np.ascontiguousarray(a)
        arrays[f"in_{name}"] = a
        aps[name] = nc.dram_tensor(f"in_{name}", a.shape, mybir.dt.from_np(a.dtype), kind="ExternalInput").ap()
    out = nc.dram_tensor("out_0", (B, T, HID), F32, kind="ExternalOutput").ap()
    decoder_layer(nc, aps, [out])
    r = _run(nc, [arrays], core_ids=[0])
    return r.results[0]["out_0"]
```

```python
from contextlib import ExitStack, contextmanager

import numpy as np

import concourse.bass as bass
from concourse import mybir

F32 = mybir.dt.float32
BF16 = mybir.dt.bfloat16
F32R = mybir.dt.float32r
ALU = mybir.AluOpType
ACT = mybir.ActivationFunctionType
AX = mybir.AxisListType

P = 128
B, T, HID = 32, 64, 256
TOKENS = B * T
CDIM = 128
H = 16
KH = HID // P
PAIRS = TOKENS // P
G = 512
NP = G // P
NS = G // T
GROUPS = TOKENS // G
UNITS = GROUPS * H
TAPS = 4
E = 8
TOPK = 2
EPS = 1e-5
L2EPS = 1e-6
SCALE = float(P) ** -0.5
FAR = float(np.exp(70.0))
HALVES = [T >> n for n in range(1, 7)]
LEVELS = len(HALVES) + 1

W_Q, W_K, W_V, W_W = (n * KH * P for n in range(4))
W_F2 = 4 * KH * P
W_G2 = W_F2 + P
W_CONV = W_G2 + P
W_BIAS = W_CONV + 4 * TAPS
W_HEAD = W_BIAS + 1
X_Q, X_K = 0, KH * P
X_HEAD = KH * P + P


def shape_constants():
    s, t = np.meshgrid(np.arange(P), np.arange(P), indexing="ij")
    same = (s // T) == (t // T)
    mid = T // 2
    after = same & (s % T >= mid) & (s <= t)
    before = same & (s % T < mid) & (s > t)
    span = after.astype(np.float32) - before.astype(np.float32)
    causal = (same & (s <= t)).astype(np.float32)
    earlier = np.tril(np.ones((E, E), np.float32), -1).reshape(1, E * E).repeat(P, axis=0)
    return np.concatenate([np.eye(P, dtype=np.float32), span, causal, earlier], axis=1)


def level_tables():
    s, t = np.meshgrid(np.arange(P), np.arange(P), indexing="ij")
    tables = []
    for c in HALVES:
        same = (s // (2 * c)) == (t // (2 * c))
        s_late, t_late = (s // c) % 2 == 1, (t // c) % 2 == 1
        sums = same & ((t_late & s_late & (s <= t)) | (~t_late & ~s_late & (s > t)))
        tables.append(np.concatenate([sums, same & ~s_late & t_late], axis=1))
    tables.append(np.concatenate([np.zeros((P, P), bool), np.eye(P, dtype=bool)], axis=1))
    return np.stack(tables).astype(np.float32)


@contextmanager
def stage_semaphores(nc):
    with ExitStack() as ctx:
        used = []

        def sem(name):
            used.append(ctx.enter_context(nc.semaphore(name)))
            return used[-1]

        yield sem
        with nc.Block() as block:
            @block.sync
            def _(sp):
                for s in used:
                    sp.sem_clear(s)


def layernorm_block(nc, sems, tag, x_all, xT_all, ident, load=None, prefetch=(), prefetched=None):
    with ExitStack() as ctx:
        def sb(name, shape, dt=F32):
            return ctx.enter_context(nc.sbuf_tensor(f"{tag}_{name}", shape, dt))

        def sem(name):
            return sems(f"{tag}_{name}")

        stats = sb("stats", [P, PAIRS, 6])
        moments = sb("moments", [P, PAIRS, 2])
        eps = sb("eps", [P, 1])
        std = sb("std", [P, PAIRS])
        rstd = sb("rstd", [P, PAIRS])
        xn = sb("xn", [P, 2, NP, HID])
        turned = [ctx.enter_context(nc.psum_tensor(f"{tag}_turned{k}", [P, G], F32)) for k in range(2 * KH)]
        loaded = sem("loaded")
        eps_set = sem("eps_set")
        stats_done = sem("stats_done")
        moments_done = sem("moments_done")
        std_done = sem("std_done")
        rstd_done = sem("rstd_done")
        xn_done = sem("xn_done")
        turned_done = sem("turned_done")
        kept = sem("kept")
        block = ctx.enter_context(nc.Block())

        @block.sync
        def _(sp):
            if load is not None:
                for dst, src in load:
                    sp.dma_start(dst, src).then_inc(loaded, 16)
            for dst, src in prefetch:
                sp.dma_start(dst, src).then_inc(prefetched, 16)

        @block.vector
        def _(dve):
            dve.memset(eps[:], EPS).then_inc(eps_set, 1)
            if load is not None:
                dve.wait_ge(loaded, 16 * len(load))
            for p in range(PAIRS):
                dve.bn_stats(stats[:, p, :], x_all[:, p, :]).then_inc(stats_done, 1)
            for p in range(PAIRS):
                dve.wait_ge(stats_done, p + 1)
                last = dve.bn_aggr(moments[:, p, :], stats[:, p, :])
            last.then_inc(moments_done, 1)
            dve.wait_ge(std_done, 1)
            dve.reciprocal(rstd[:], std[:]).then_inc(rstd_done, 1)
            dve.wait_ge(rstd_done, 1)
            for g in range(GROUPS):
                if g >= 2:
                    dve.wait_ge(turned_done, g - 1)
                for p in range(NP):
                    q = g * NP + p
                    last = dve.tensor_scalar(xn[:, g % 2, p, :], x_all[:, q, :], moments[:, q, 0:1],
                                             rstd[:, q:q + 1], ALU.subtract, ALU.mult)
                last.then_inc(xn_done, 1)

        @block.scalar
        def _(act):
            act.wait_ge(eps_set, 1)
            act.wait_ge(moments_done, 1)
            act.activation(std[:], moments[:, :, 1], ACT.Sqrt, bias=eps[:]).then_inc(std_done, 1)
            for g in range(GROUPS):
                act.wait_ge(turned_done, g + 1)
                for k in range(KH):
                    last = act.copy(xT_all[:, k, g * G:(g + 1) * G], turned[g % 2 * KH + k][:])
                last.then_inc(kept, 1)

        @block.tensor
        def _(pe):
            for g in range(GROUPS):
                pe.wait_ge(xn_done, g + 1)
                if g >= 2:
                    pe.wait_ge(kept, g - 1)
                for k in range(KH):
                    for p in range(NP):
                        last = pe.transpose(turned[g % 2 * KH + k][:, p * P:(p + 1) * P],
                                            xn[:, g % 2, p, k * P:(k + 1) * P], ident)
                last.then_inc(turned_done, 1)


def lowrank_block(nc, sems, xT_all, f1T, g1T, beta, Wf1g1, Wb, ident):
    with ExitStack() as ctx:
        def sb(name, shape, dt=F32):
            return ctx.enter_context(nc.sbuf_tensor(name, shape, dt))

        def sem(name):
            return sems(name)

        bT = sb("bT", [H, TOKENS])
        banks = [ctx.enter_context(nc.psum_tensor(f"low{k}", [P, G], F32)) for k in range(3)]
        beta_ps = ctx.enter_context(nc.psum_tensor("beta_ps", [P, PAIRS, H], F32))
        low_done = sem("low_done")
        low_kept = sem("low_kept")
        bT_kept = sem("bT_kept")
        beta_turned = sem("beta_turned")
        beta_done = sem("beta_done")
        block = ctx.enter_context(nc.Block())

        @block.tensor
        def _(pe):
            for g in range(GROUPS):
                cols = slice(g * G, (g + 1) * G)
                if g >= 1:
                    pe.wait_ge(low_kept, 2 * g)
                    pe.wait_ge(bT_kept, g)
                for n in range(2):
                    for k in range(KH):
                        last = pe.matmul(banks[n][:], Wf1g1[:, k, n, :], xT_all[:, k, cols],
                                         start=(k == 0), stop=(k == KH - 1))
                for k in range(KH):
                    last = pe.matmul(banks[2][0:H, :], Wb[:, k, :], xT_all[:, k, cols],
                                     start=(k == 0), stop=(k == KH - 1))
                last.then_inc(low_done, 1)
            pe.wait_ge(bT_kept, GROUPS)
            for q in range(PAIRS):
                last = pe.transpose(beta_ps[:, q, :], bT[:, q * P:(q + 1) * P], ident[0:H, 0:H])
            last.then_inc(beta_turned, 1)

        @block.scalar
        def _(act):
            for g in range(GROUPS):
                cols = slice(g * G, (g + 1) * G)
                act.wait_ge(low_done, g + 1)
                act.activation(bT[:, cols], banks[2][0:H, :], ACT.Sigmoid).then_inc(bT_kept, 1)
                act.copy(f1T[:, cols], banks[0][:]).then_inc(low_kept, 1)

        @block.vector
        def _(dve):
            for g in range(GROUPS):
                dve.wait_ge(low_done, g + 1)
                dve.tensor_copy(g1T[:, g * G:(g + 1) * G], banks[1][:]).then_inc(low_kept, 1)
            dve.wait_ge(beta_turned, 1)
            dve.tensor_copy(beta.rearrange("p g h q -> p g q h"),
                            beta_ps[:].rearrange("p (g q) h -> p g q h", g=GROUPS)).then_inc(beta_done, 1)


def gsa_block(nc, sems, w_heads, x_all, xT_all, f1T, g1T, beta, Wo, consts, far_flag):
    ident, span, causal = consts
    with ExitStack() as ctx:
        def sb(name, shape, dt=F32):
            return ctx.enter_context(nc.sbuf_tensor(name, shape, dt))

        def psum(name, shape, dt=F32):
            return ctx.enter_context(nc.psum_tensor(name, shape, dt))

        def sem(name):
            return sems(name)

        hw = [sb(f"head_weights{i}", [P, W_HEAD]) for i in range(2)]
        w_high = [sb(f"w_high{i}", [P, W_F2], F32R) for i in range(2)]
        w_low = [sb(f"w_low{i}", [P, W_F2], F32R) for i in range(2)]
        x_high = sb("x_high", [P, 2, KH, G], F32R)
        x_low = sb("x_low", [P, 2, KH, G], F32R)
        q = [sb(f"q_chan{i}", [P, G]) for i in range(2)]
        k, v, w = (sb(f"{n}_chan", [P, G]) for n in "kvw")
        f1 = sb("f1_static", [P, G])
        glog = sb("glog", [P, G])
        gtmp = sb("gtmp", [P, G])
        expD = sb("expD", [P, G])
        expDneg = sb("expDneg", [P, G])
        gate = [sb(f"gate{i}", [P, G]) for i in range(2)]
        w2 = sb("w2", [P, G])
        wdec = [sb(f"wdec{i}", [P, G]) for i in range(2)]
        wdec_tok = sb("wdec_tok", [P, G])
        v_tok = [sb(f"v_tok{i}", [P, G]) for i in range(2)]
        qk = sb("qk", [P, G])
        score = sb("score", [P, G])
        probs = sb("probs", [P, G])
        pdec = sb("pdec", [P, G])
        pdec_chan = sb("pdec_chan", [P, G])
        mix = sb("mix", [P, G])
        osq = sb("osq", [P, G])
        o_tok = sb("o_tok", [P, G])
        o_chan = sb("o_chan", [P, G])
        ones = sb("ones", [P, P])
        half = sb("half", [P, 1])
        l2eps = sb("l2eps", [P, 1])
        zeros = sb("zeros", [P, G], BF16)
        hbias = sb("hbias", [P, 1])
        widest = sb("widest", [P, NS])
        narrowest = sb("narrowest", [P, NS])
        far = sb("far", [P, NS])
        far_any = sb("far_any", [P, 1])
        far_one = sb("far_one", [1, 1])
        lnw = sb("lnw", [P, NP])
        rw = sb("rw", [P, NP])
        coef = [sb(f"coef{i}", [P, NP]) for i in range(2)]
        smax = sb("smax", [P, NP])
        nmax = sb("nmax", [P, NP])
        Z = sb("Z", [P, NP])
        Zeps = [sb(f"Zeps{i}", [P, NP]) for i in range(2)]
        ssq = sb("ssq", [P, NP])
        y = sb("y", [P, NP])
        lny = sb("lny", [P, NP])
        rho = sb("rho", [P, NP])

        bank0, bank1, bank2, bank3, bank4, bank5 = (psum(f"bank{n}", [P, G]) for n in range(6))
        outacc = [psum(f"outacc{n}", [P, 2, HID]) for n in range(2)]

        primed = {
            "tensor": "xq xk xv xw gx gate_x dtok dchan wsq att wdecT vT scores pdecT pv o oT wo",
            "scalar": "tapq tapk tapv tapw gabs gexp gln decay ndecay gate_th siluq siluk siluv siluw lnw_s rw_s "
                      "wdec_tok_s v_tok_s exps osq_s lny_s rho_s",
            "vector": "convq convk convv convw glog_s coef_s qk_s score_s smax_s nmax_s Zeps_s y_s mix_s "
                      "o_tok_s o_chan_s pdec_chan_s range_s",
            "gpsimd": "w2_s wdec_s f1_s hbias_s pdec_s w_high_s w_low_s x_high_s x_low_s",
        }
        S = {n: sem(n) for names in primed.values() for n in names.split()}
        weights_in = [sem(f"weights_in{i}") for i in range(2)]
        consts_set = sem("consts_set")
        group_out = sem("group_out")
        range_set = sem("range_set")
        far_s = sem("far_s")
        far_turned = sem("far_turned")
        block = ctx.enter_context(nc.Block())

        CONV = TAPS - 1

        def prime(eng, who):
            for n in primed[who].split():
                eng.sem_inc(S[n], 1)

        def done(n, times=1):
            return times * (n + 1) + 1

        def before(n, times=1):
            return times * n + 1

        def two_before(n):
            return n

        def run_units(eng, front, merged, group_start=None, group_end=None):
            front(0, 0)
            merged(-1, None, 1, outputs=False)
            with eng.Fori(0, GROUPS) as g:
                if group_start is not None:
                    group_start(g)
                with eng.Fori(0, H // 2) as j:
                    for par in range(2):
                        merged(g * H + j * 2 + par, j * 2 + par, par)
                if group_end is not None:
                    group_end(g)

        def pairs(t):
            return t[:].rearrange("p (q c) -> p q c", q=NP)

        def pc(t, p):
            return t[:, p * P:(p + 1) * P]

        @block.sync
        def _(sp):
            def load(n, h, par):
                sp.dma_start(hw[par][:], w_heads[h]).then_inc(weights_in[par], 16)

            load(0, 0, 0)
            load(1, 1, 1)
            with sp.Fori(0, UNITS // 2) as m:
                for par in range(2):
                    n = 2 * m + par
                    sp.wait_ge(S["gate_x"], done(n))
                    sp.wait_ge(S["hbias_s"], done(n))
                    sp.wait_ge(S["convw"], done(n, CONV))
                    sp.wait_ge(S["w_low_s"], done(n))
                    load(n + 2, (n + 2) % H, par)
            sp.wait_ge(S["gate_x"], done(UNITS))
            sp.wait_ge(S["hbias_s"], done(UNITS))
            sp.wait_ge(S["convw"], done(UNITS, CONV))
            sp.wait_ge(S["w_low_s"], done(UNITS))
            load(UNITS + 2, 0, 0)

        @block.gpsimd
        def _(pool):
            prime(pool, "gpsimd")
            pool.memset(ones[:], 1.0).then_inc(consts_set, 1)
            pool.memset(half[:], 0.5).then_inc(consts_set, 1)
            pool.memset(l2eps[:], L2EPS).then_inc(consts_set, 1)
            pool.memset(zeros[:], 0.0).then_inc(consts_set, 1)
            pool.wait_ge(consts_set, 4)

            def split_weights(n, par):
                pool.tensor_copy(w_high[par][:], hw[par][:, 0:W_F2]).then_inc(S["w_high_s"], 1)
                pool.wait_ge(S["w_high_s"], done(n))
                pool.tensor_tensor(w_low[par][:], hw[par][:, 0:W_F2], w_high[par][:], ALU.subtract)\
                    .then_inc(S["w_low_s"], 1)

            def split_inputs(g, turn):
                cols = bass.ts(g, G)
                pool.tensor_copy(x_high[:, turn], xT_all[:, :, cols]).then_inc(S["x_high_s"], 1)
                pool.wait_ge(S["x_high_s"], done(g))
                pool.tensor_tensor(x_low[:, turn], xT_all[:, :, cols], x_high[:, turn], ALU.subtract)\
                    .then_inc(S["x_low_s"], 1)

            def front(n, par):
                pool.wait_ge(S["gx"], before(n))
                pool.tensor_copy(f1[:], f1T[:, bass.ts(n // H, G)]).then_inc(S["f1_s"], 1)
                pool.wait_ge(weights_in[par], 16 * (n // 2 + 1))
                pool.wait_ge(S["gate_th"], before(n))
                pool.wait_ge(weights_in[1 - par], 16 * ((n + 1) // 2 + 1))
                pool.wait_ge(S["xw"], before(n))
                pool.tensor_tensor(hbias[:], hw[par][:, W_BIAS:W_BIAS + 1], half[:], ALU.mult)\
                    .then_inc(S["hbias_s"], 1)
                split_weights(n + 1, 1 - par)

            def group_start(g):
                pool.wait_ge(S["xw"], before(g * H))
                split_inputs(g + 1, (g + 1) % 2)

            def merged(b, h, par, outputs=True):
                a, apar, n = b + 1, 1 - par, b + 2
                pool.wait_ge(S["siluw"], done(a))
                pool.wait_ge(S["wsq"], before(a))
                pool.tensor_tensor(w2[:], w[:], w[:], ALU.mult).then_inc(S["w2_s"], 1)
                pool.wait_ge(S["ndecay"], done(a))
                if outputs:
                    pool.wait_ge(S["pv"], two_before(a))
                pool.tensor_tensor(wdec[apar][:], w[:], expDneg[:], ALU.mult).then_inc(S["wdec_s"], 1)
                front(n, par)
                pool.wait_ge(S["exps"], done(a, NP))
                pool.wait_ge(S["pdecT"], before(a))
                pool.tensor_tensor(pdec[:], probs[:], expD[:], ALU.mult).then_inc(S["pdec_s"], 1)

            split_inputs(0, 0)
            pool.wait_ge(weights_in[0], 16)
            split_weights(0, 0)
            run_units(pool, front, merged, group_start=group_start)

        @block.tensor
        def _(pe):
            prime(pe, "tensor")
            pe.wait_ge(consts_set, 4)

            def project(n, par, bank, w_col, step):
                turn = n // H % 2
                for kk in range(KH):
                    cols = slice(w_col + kk * P, w_col + (kk + 1) * P)
                    for i, (weights, inputs) in enumerate(((w_high, x_high), (w_high, x_low), (w_low, x_high))):
                        last = pe.matmul(bank[:], weights[par][:, cols], inputs[:, turn, kk, :],
                                         start=(kk + i == 0), stop=(kk == KH - 1 and i == 2))
                last.then_inc(S[step], 1)

            def f_q(n, par):
                pe.wait_ge(weights_in[par], 16 * (n // 2 + 1))
                pe.wait_ge(S["w_low_s"], done(n))
                pe.wait_ge(S["x_low_s"], done(n // H))
                pe.wait_ge(S["convv"], before(n, CONV))
                project(n, par, bank0, W_Q, "xq")

            def f_k(n, par):
                pe.wait_ge(S["convw"], before(n, CONV))
                project(n, par, bank1, W_K, "xk")

            def f_v(n, par):
                pe.wait_ge(S["convq"], done(n, CONV))
                project(n, par, bank0, W_V, "xv")

            def f_w(n, par):
                pe.wait_ge(S["convk"], done(n, CONV))
                project(n, par, bank1, W_W, "xw")

            def f_decay_logits(n, par):
                pe.wait_ge(S["f1_s"], done(n))
                pe.wait_ge(S["v_tok_s"], before(n))
                for p in range(NP):
                    last = pe.matmul(pc(bank5, p), pc(f1, p), hw[par][:, W_F2:W_F2 + P], start=True, stop=True)
                last.then_inc(S["gx"], 1)

            def f_decays(n, par):
                pe.wait_ge(S["glog_s"], done(n))
                for p in range(NP):
                    last = pe.matmul(pc(bank5, p), pc(glog, p), span, start=True, stop=True)
                last.then_inc(S["dchan"], 1)
                pe.wait_ge(S["score_s"], before(n))
                pe.matmul(bank2[:], span, glog[:], start=True, stop=True).then_inc(S["dtok"], 1)

            def f_gate(n, par, outputs=True):
                if outputs:
                    pe.wait_ge(S["o_tok_s"], two_before(n))
                cols = bass.ts(n // H, G)
                if not outputs:
                    pe.wait_ge(S["gate_th"], before(n))
                pe.matmul(bank4[:], hw[par][:, W_G2:W_G2 + P], g1T[:, cols], start=True, stop=True)\
                    .then_inc(S["gate_x"], 1)

            def front(n, par):
                f_q(n, par)
                f_k(n, par)
                f_decay_logits(n, par)
                f_v(n, par)
                f_w(n, par)
                f_q(n + 1, 1 - par)
                f_decays(n, par)
                f_gate(n, par, outputs=False)

            def merged(b, h, par, outputs=True):
                a, apar, n = b + 1, 1 - par, b + 2
                if outputs:
                    pe.wait_ge(S["pdec_s"], done(b))
                    pe.wait_ge(S["o_chan_s"], before(b))
                    for p in range(NP):
                        last = pe.transpose(pc(bank3, p), pc(pdec, p), ident)
                    last.then_inc(S["pdecT"], 1)
                pe.wait_ge(S["siluk"], done(a))
                pe.wait_ge(S["siluq"], done(a))
                pe.wait_ge(S["decay"], done(a))
                for p in range(NP):
                    last = pe.matmul(pc(bank2, p), pc(k, p), pc(q[apar], p), start=True, stop=True)
                last.then_inc(S["att"], 1)
                pe.wait_ge(S["w2_s"], done(a))
                pe.wait_ge(S["ndecay"], done(a))
                for p in range(NP):
                    last = pe.matmul(pc(bank5, p), pc(w2, p), ones[:], start=True, stop=True)
                last.then_inc(S["wsq"], 1)
                if outputs:
                    pe.wait_ge(S["pdec_chan_s"], done(b))
                    for s0 in range(0, G, T):
                        rows, p0 = s0 % P, s0 // P * P
                        t_halves = pdec_chan[:, p0:p0 + P].rearrange("m (u v t) -> m v u t", u=2, v=2)
                        o_halves = bank3[:, p0:p0 + P].rearrange("m (u v t) -> m v u t", u=2, v=2)
                        pe.matmul(o_halves[rows:rows + T, 1], wdec[par][:, s0:s0 + T], t_halves[:, 1],
                                  start=True, stop=True)
                        last = pe.matmul(o_halves[rows:rows + T // 2, 0], wdec[par][:, s0:s0 + T // 2],
                                         t_halves[:, 0], start=True, stop=True)
                    last.then_inc(S["pv"], 1)
                pe.wait_ge(S["wdec_s"], done(a))
                pe.wait_ge(S["lnw_s"], done(a))
                for p in range(NP):
                    last = pe.transpose(pc(bank5, p), pc(wdec[apar], p), ident)
                last.then_inc(S["wdecT"], 1)
                f_k(n, par)
                pe.wait_ge(S["qk_s"], done(a))
                pe.wait_ge(S["wdec_tok_s"], done(a))
                for p in range(NP):
                    last = pe.matmul(pc(bank2, p), pc(qk, p), pc(wdec_tok, p), start=True, stop=True)
                last.then_inc(S["scores"], 1)
                if outputs:
                    pe.wait_ge(S["mix_s"], done(b))
                    pe.wait_ge(S["gate_th"], done(a))
                    for p in range(NP):
                        last = pe.matmul(pc(bank4, p), pc(mix, p), pc(v_tok[par], p), start=True, stop=True)
                    last.then_inc(S["o"], 1)
                pe.wait_ge(S["siluv"], done(a))
                for p in range(NP):
                    last = pe.transpose(pc(bank5, p), pc(v, p), ident)
                last.then_inc(S["vT"], 1)
                f_v(n, par)
                f_decay_logits(n, par)
                f_w(n, par)
                f_q(n + 1, apar)
                f_decays(n, par)
                if outputs:
                    pe.wait_ge(S["o_tok_s"], done(b))
                    for p in range(NP):
                        last = pe.transpose(pc(bank3, p), pc(o_tok, p), ident)
                    last.then_inc(S["oT"], 1)
                f_gate(n, par, outputs)
                if outputs:
                    pe.wait_ge(S["o_chan_s"], done(b))
                    for p in range(NP):
                        last = pe.matmul(outacc[p // 2][:, p % 2, :], pc(o_chan, p), Wo[:, bass.ts(h, HID)],
                                         start=False, stop=False, skip_group_check=True)
                    last.then_inc(S["wo"], 1)

            def group_start(g):
                pe.wait_ge(group_out, g + 1)
                for n in range(2):
                    pe.matmul(outacc[n][:].rearrange("p a c -> p (a c)"), zeros[:, 0:P], zeros[:],
                              start=True, stop=False, skip_group_check=True)

            run_units(pe, front, merged, group_start=group_start)
            pe.wait_ge(far_s, 3)
            pe.wait_ge(S["convq"], done(UNITS + 2, CONV))
            pe.transpose(bank0[0:1, 0:P], far_any[:], ident).then_inc(far_turned, 1)

        @block.scalar
        def _(act):
            prime(act, "scalar")
            act.wait_ge(consts_set, 4)

            def tap(n, par, bank, dst, col, x_step, conv_step, free_waits):
                act.wait_ge(S[x_step], done(n))
                for s in free_waits:
                    act.wait_ge(S[s], before(n))
                c = W_CONV + TAPS * col + TAPS - 1
                act.activation(dst[:], bank[:], ACT.Copy, scale=hw[par][:, c:c + 1])\
                    .then_inc(S[conv_step], 1)

            def f_tapq(n, par, first=False):
                if not first:
                    act.wait_ge(S["att"], two_before(n))
                tap(n, par, bank0, q[par], 0, "xq", "tapq", [])

            def f_tapk(n, par):
                tap(n, par, bank1, k, 1, "xk", "tapk", ["att"])

            def f_tapv(n, par):
                tap(n, par, bank0, v, 2, "xv", "tapv", ["vT"])

            def f_tapw(n, par):
                tap(n, par, bank1, w, 3, "xw", "tapw", ["w2_s", "wdec_s"])

            def f_log_sigmoid(n, par):
                act.wait_ge(S["gx"], done(n))
                act.wait_ge(S["glog_s"], before(n))
                act.activation(gtmp[:], bank5[:], ACT.Abs).then_inc(S["gabs"], 1)
                act.wait_ge(S["gabs"], done(n))
                act.activation(gtmp[:], gtmp[:], ACT.Exp, scale=-1.0).then_inc(S["gexp"], 1)
                act.wait_ge(S["gexp"], done(n))
                act.activation(gtmp[:], gtmp[:], ACT.Ln, bias=1.0).then_inc(S["gln"], 1)

            def f_decays(n, par):
                act.wait_ge(S["dchan"], done(n))
                act.wait_ge(S["wdec_s"], before(n))
                act.wait_ge(S["range_s"], before(n, 2))
                act.activation(expDneg[:], bank5[:], ACT.Exp, scale=-1.0).then_inc(S["ndecay"], 1)
                act.wait_ge(S["dtok"], done(n))
                act.wait_ge(S["pdec_s"], before(n))
                act.activation(expD[:], bank2[:], ACT.Exp).then_inc(S["decay"], 1)

            def f_silus(n, par, outputs):
                act.preload_act_table_set("silu_and_others")
                for t, c, s in ((w, "convw", "siluw"), (k, "convk", "siluk"), (q[par], "convq", "siluq"),
                                (v, "convv", "siluv")):
                    act.wait_ge(S[c], done(n, CONV))
                    act.activation(t[:], t[:], ACT.Silu).then_inc(S[s], 1)
                act.wait_ge(S["gate_x"], done(n))
                act.wait_ge(S["hbias_s"], done(n))
                if outputs:
                    act.wait_ge(S["o_chan_s"], two_before(n))
                act.activation(gate[par][:], bank4[:], ACT.Tanh, bias=hbias[:], scale=0.5).then_inc(S["gate_th"], 1)
                act.preload_act_table_set("natural_log_exp_and_others")

            def front(n, par):
                f_tapq(n, par, first=True)
                f_tapk(n, par)
                f_log_sigmoid(n, par)
                f_tapv(n, par)
                f_tapw(n, par)
                f_tapq(n + 1, 1 - par)
                f_decays(n, par)
                f_silus(n, par, outputs=False)

            def merged(b, h, par, outputs=True):
                a, apar, n = b + 1, 1 - par, b + 2
                act.wait_ge(S["wsq"], done(a))
                act.activation(lnw[:], pairs(bank5)[:, :, 0], ACT.Ln, bias=l2eps[:]).then_inc(S["lnw_s"], 1)
                act.wait_ge(S["lnw_s"], done(a))
                act.wait_ge(S["coef_s"], before(a))
                act.activation(rw[:], lnw[:], ACT.Exp, scale=-0.5).then_inc(S["rw_s"], 1)
                act.wait_ge(S["wdecT"], done(a))
                act.wait_ge(S["scores"], before(a))
                act.copy(wdec_tok[:], bank5[:]).then_inc(S["wdec_tok_s"], 1)
                f_tapk(n, par)
                act.wait_ge(S["vT"], done(a))
                if outputs:
                    act.wait_ge(S["o"], two_before(a))
                act.copy(v_tok[apar][:], bank5[:]).then_inc(S["v_tok_s"], 1)
                if outputs:
                    act.wait_ge(S["o"], done(b))
                    act.wait_ge(S["y_s"], before(b))
                    for p in range(NP):
                        act.activation(pc(osq, p), pc(bank4, p), ACT.Square, accum_out=ssq[:, p:p + 1])\
                            .then_inc(S["osq_s"], 1)
                f_tapv(n, par)
                f_log_sigmoid(n, par)
                f_tapw(n, par)
                act.wait_ge(S["nmax_s"], done(a))
                act.wait_ge(S["pdec_s"], before(a))
                act.wait_ge(S["Zeps_s"], before(a))
                for p in range(NP):
                    act.activation(pc(probs, p), pc(score, p), ACT.Exp, bias=nmax[:, p:p + 1], scale=SCALE,
                                   accum_out=Z[:, p:p + 1]).then_inc(S["exps"], 1)
                if outputs:
                    act.wait_ge(S["y_s"], done(b))
                    act.activation(lny[:], y[:], ACT.Ln).then_inc(S["lny_s"], 1)
                    act.wait_ge(S["lny_s"], done(b))
                    act.wait_ge(S["o_tok_s"], before(b))
                    act.activation(rho[:], lny[:], ACT.Exp, scale=-0.5).then_inc(S["rho_s"], 1)
                f_tapq(n + 1, apar)
                f_decays(n, par)
                f_silus(n, par, outputs)

            run_units(act, front, merged)

        @block.vector
        def _(dve):
            prime(dve, "vector")
            dve.sem_inc(group_out, 1)
            dve.wait_ge(consts_set, 4)
            dve.memset(widest[:], 1.0).then_inc(range_set, 1)
            dve.memset(narrowest[:], 1.0).then_inc(range_set, 1)
            dve.wait_ge(range_set, 2)

            def conv(n, par, bank, dst, col, tap_step, conv_step):
                x3 = bank[:].rearrange("p (s t) -> p s t", s=NS)
                d3 = dst[:].rearrange("p (s t) -> p s t", s=NS)
                dve.wait_ge(S[tap_step], done(n))
                for shift in range(1, TAPS):
                    if shift > 1:
                        dve.wait_ge(S[conv_step], before(n, CONV) + shift - 1)
                    c = W_CONV + TAPS * col + TAPS - 1 - shift
                    dve.scalar_tensor_tensor(out=d3[:, :, shift:T], in0=x3[:, :, 0:T - shift],
                                             scalar=hw[par][:, c:c + 1], in1=d3[:, :, shift:T],
                                             op0=ALU.mult, op1=ALU.add).then_inc(S[conv_step], 1)

            def f_convq(n, par):
                conv(n, par, bank0, q[par], 0, "tapq", "convq")

            def f_convk(n, par):
                conv(n, par, bank1, k, 1, "tapk", "convk")

            def f_convv(n, par):
                conv(n, par, bank0, v, 2, "tapv", "convv")

            def f_convw(n, par):
                conv(n, par, bank1, w, 3, "tapw", "convw")

            def f_glog(n, par):
                dve.wait_ge(S["gln"], done(n))
                dve.wait_ge(S["dchan"], before(n))
                dve.wait_ge(S["dtok"], before(n))
                dve.scalar_tensor_tensor(out=glog[:], in0=bank5[:], scalar=0.0, in1=gtmp[:], op0=ALU.min,
                                         op1=ALU.subtract).then_inc(S["glog_s"], 1)

            def f_range(n):
                e3 = expDneg[:].rearrange("p (s t) -> p s t", s=NS)
                dve.wait_ge(S["ndecay"], done(n))
                dve.wait_ge(S["range_s"], before(n, 2))
                dve.tensor_tensor(widest[:], widest[:], e3[:, :, T - 1], ALU.max).then_inc(S["range_s"], 1)
                dve.tensor_tensor(narrowest[:], narrowest[:], e3[:, :, 0], ALU.min).then_inc(S["range_s"], 1)

            def beta_of(i):
                return beta.rearrange("p g h q -> p (g h q)")[:, bass.ts(i, NP)]

            def front(n, par):
                f_convq(n, par)
                f_convk(n, par)
                f_convv(n, par)
                f_glog(n, par)
                f_convw(n, par)
                f_convq(n + 1, 1 - par)

            def merged(b, h, par, outputs=True):
                a, apar, n = b + 1, 1 - par, b + 2
                if outputs:
                    dve.wait_ge(S["pdecT"], done(b))
                    dve.wait_ge(S["pv"], before(b))
                    dve.tensor_copy(pdec_chan[:], bank3[:]).then_inc(S["pdec_chan_s"], 1)
                f_range(a)
                dve.wait_ge(S["rw_s"], done(a))
                if outputs:
                    dve.wait_ge(S["mix_s"], two_before(a))
                dve.tensor_tensor(coef[apar][:], rw[:], beta_of(a), ALU.mult).then_inc(S["coef_s"], 1)
                dve.wait_ge(S["coef_s"], done(a))
                dve.wait_ge(S["att"], done(a))
                dve.wait_ge(S["scores"], before(a))
                for p in range(NP):
                    last = dve.scalar_tensor_tensor(out=pc(qk, p), in0=pc(bank2, p), scalar=coef[apar][:, p:p + 1],
                                                    in1=causal, op0=ALU.mult, op1=ALU.mult)
                last.then_inc(S["qk_s"], 1)
                if outputs:
                    dve.wait_ge(S["pv"], done(b))
                    dve.wait_ge(S["o"], before(b))
                    for p in range(NP):
                        last = dve.scalar_tensor_tensor(out=pc(mix, p), in0=pc(bank3, p),
                                                        scalar=coef[par][:, p:p + 1], in1=causal,
                                                        op0=ALU.mult, op1=ALU.mult)
                    last.then_inc(S["mix_s"], 1)
                f_convk(n, par)
                dve.wait_ge(S["scores"], done(a))
                dve.wait_ge(S["exps"], before(a, NP))
                dve.tensor_tensor(score[:], bank2[:], expD[:], ALU.mult).then_inc(S["score_s"], 1)
                dve.wait_ge(S["score_s"], done(a))
                dve.tensor_reduce(smax[:], pairs(score), AX.X, ALU.max).then_inc(S["smax_s"], 1)
                dve.wait_ge(S["smax_s"], done(a))
                dve.tensor_scalar(nmax[:], smax[:], -SCALE, None, ALU.mult).then_inc(S["nmax_s"], 1)
                if outputs:
                    dve.wait_ge(S["osq_s"], done(b, NP))
                    dve.wait_ge(S["Zeps_s"], done(b))
                    dve.wait_ge(S["lny_s"], before(b))
                    dve.scalar_tensor_tensor(out=y[:], in0=ssq[:], scalar=4.0 / P, in1=Zeps[par][:], op0=ALU.mult,
                                             op1=ALU.add).then_inc(S["y_s"], 1)
                f_convv(n, par)
                f_glog(n, par)
                f_convw(n, par)
                dve.wait_ge(S["exps"], done(a, NP))
                if outputs:
                    dve.wait_ge(S["y_s"], two_before(a))
                dve.scalar_tensor_tensor(out=Zeps[apar][:], in0=Z[:], scalar=4.0 * EPS, in1=Z[:], op0=ALU.mult,
                                         op1=ALU.mult).then_inc(S["Zeps_s"], 1)
                if outputs:
                    dve.wait_ge(S["rho_s"], done(b))
                    dve.wait_ge(S["oT"], before(b))
                    for p in range(NP):
                        last = dve.tensor_scalar(pc(o_tok, p), pc(bank4, p), rho[:, p:p + 1], None, ALU.mult)
                    last.then_inc(S["o_tok_s"], 1)
                if outputs:
                    dve.wait_ge(S["oT"], done(b))
                    dve.wait_ge(S["gate_th"], done(b))
                    dve.wait_ge(S["wo"], before(b))
                    dve.scalar_tensor_tensor(out=o_chan[:], in0=gate[par][:], scalar=1.0, in1=bank3[:],
                                             op0=ALU.add, op1=ALU.mult).then_inc(S["o_chan_s"], 1)
                f_convq(n + 1, apar)

            def group_end(g):
                dve.wait_ge(S["wo"], before(g * H + H))
                for m in range(2):
                    xs = x_all[:, bass.ds(g * NP + 2 * m, 2), :]
                    last = dve.tensor_tensor(xs, xs, outacc[m][:], ALU.add)
                last.then_inc(group_out, 1)

            run_units(dve, front, merged, group_end=group_end)
            dve.wait_ge(S["range_s"], done(UNITS, 2))
            dve.tensor_scalar(far[:], widest[:], FAR, None, ALU.is_gt).then_inc(far_s, 1)
            dve.wait_ge(far_s, 1)
            dve.scalar_tensor_tensor(out=far[:], in0=narrowest[:], scalar=1.0 / FAR, in1=far[:], op0=ALU.is_lt,
                                     op1=ALU.max).then_inc(far_s, 1)
            dve.wait_ge(far_s, 2)
            dve.tensor_reduce(far_any[:], far[:], AX.X, ALU.max).then_inc(far_s, 1)
            dve.wait_ge(far_turned, 1)
            dve.tensor_reduce(far_one[:], bank0[0:1, 0:P], AX.X, ALU.max).then_inc(far_s, 1)
            dve.wait_ge(far_s, 4)
            dve.tensor_copy(far_flag[:], far_one[:]).then_inc(far_s, 1)


def gsa_general_block(nc, sems, w_heads, tables_dram, x_all, x_view, xT_all, f1T, g1T, beta, Wo, consts, far_flag,
                      always=False):
    ident, _, _ = consts
    CONV = TAPS - 1
    steps = {}
    steps["front"] = ["statics", "projected", "taps", "gexp", "gln", "conv1", "conv2", "conv3", "silus", "w2",
                      "turned", "lnw", "rw", "coef"]
    steps["scores"] = ["dtok", "decay", "wdec", "qk", "products", "decayed", "summed"]
    steps["softmax"] = ["smax", "nmax", "exps", "Zeps", "probsT", "probs_chan"]
    steps["values"] = ["dchan", "decay", "decayed", "products", "masked", "summed"]
    steps["outputs"] = ["o", "osq", "y", "lny", "rho", "o_tok", "oT", "o_chan", "wo"]
    start, at = {}, 0
    for section, names in steps.items():
        start[section] = at
        at += len(names) * (LEVELS if section in ("scores", "values") else 1)
    UNIT_STEPS = at

    def through(i, section, step, level=0):
        return i * UNIT_STEPS + level * len(steps[section]) + (start[section] + steps[section].index(step) + 2)

    def ahead(i, section, step, level=0):
        return i * UNIT_STEPS + level * len(steps[section]) + (start[section] + steps[section].index(step) + 1)

    with ExitStack() as ctx:
        def sb(name, shape, dt=F32):
            return ctx.enter_context(nc.sbuf_tensor(f"n_{name}", shape, dt))

        def psum(name, shape, dt=F32):
            return ctx.enter_context(nc.psum_tensor(f"n_{name}", shape, dt))

        def sem(name):
            return sems(f"n_{name}")

        hw = sb("head_weights", [P, W_HEAD])
        tables = sb("tables", [P, 2 * P])
        sums, mask = tables[:, 0:P], tables[:, P:2 * P]
        q, k, v, w, f1, glog, gtmp, gate, w2, decay, wdec, adec, w_tok, v_tok, qk, part, score, probs, \
            probs_chan, mix, osq, o_tok, o_chan = (
                sb(n, [P, G]) for n in "q k v w f1 glog gtmp gate w2 decay wdec adec w_tok v_tok qk part score probs "
                "probs_chan mix osq o_tok o_chan".split())
        ones = sb("ones", [P, P])
        half, l2eps, hbias = (sb(n, [P, 1]) for n in ("half", "l2eps", "hbias"))
        zeros = sb("zeros", [P, G], BF16)
        lnw, rw, coef, smax, nmax, Z, Zeps, ssq, y, lny, rho = (
            sb(n, [P, NP]) for n in "lnw rw coef smax nmax Z Zeps ssq y lny rho".split())
        bank = [psum(f"bank{n}", [P, G]) for n in range(6)]
        outacc = [psum(f"outacc{n}", [P, 2, HID]) for n in range(2)]

        turn = sem("turn")
        weights_in = sem("weights_in")
        tables_in = sem("tables_in")
        x_back = sem("x_back")
        consts_set = sem("consts_set")
        group_out = sem("group_out")
        block = ctx.enter_context(nc.Block())

        def pc(t, p):
            return t[:, p * P:(p + 1) * P]

        def pairs(t):
            return t[:].rearrange("p (q c) -> p q c", q=NP)

        def when_far(eng, units, first=None):
            flag = eng.value_load(far_flag[0:1, 0:1], min_val=0, max_val=1)
            with eng.If(flag > 0) if not always else eng.If(flag >= 0):
                if first is not None:
                    first()
                units()

        @block.sync
        def _(sp):
            def units():
                sp.dma_start(x_all[:], x_view).then_inc(x_back, 16)
                with sp.Fori(0, UNITS) as i:
                    sp.wait_ge(turn, ahead(i, "front", "statics"))
                    sp.dma_start(hw[:], w_heads[i % H]).then_inc(weights_in, 16)
                    for n, section in enumerate(("scores", "values")):
                        with sp.Fori(0, LEVELS) as level:
                            sp.wait_ge(turn, ahead(i, section, steps[section][0], level))
                            sp.dma_start(tables[:], tables_dram[level]).then_inc(tables_in, 16)

            when_far(sp, units)

        def tables_count(i, n, level):
            return i * (2 * LEVELS * 16) + level * 16 + (n * LEVELS * 16 + 16)

        @block.gpsimd
        def _(pool):
            def first():
                pool.sem_inc(turn, 1)
                pool.memset(ones[:], 1.0).then_inc(consts_set, 1)
                pool.memset(half[:], 0.5).then_inc(consts_set, 1)
                pool.memset(l2eps[:], L2EPS).then_inc(consts_set, 1)
                pool.memset(zeros[:], 0.0).then_inc(consts_set, 1)
                pool.wait_ge(consts_set, 4)

            def units():
                with pool.Fori(0, UNITS) as i:
                    pool.wait_ge(turn, ahead(i, "front", "statics"))
                    pool.wait_ge(weights_in, 16 * i + 16)
                    pool.tensor_copy(f1[:], f1T[:, bass.ts(i // H, G)])
                    pool.tensor_tensor(hbias[:], hw[:, W_BIAS:W_BIAS + 1], half[:], ALU.mult).then_inc(turn, 1)
                    pool.wait_ge(turn, ahead(i, "front", "w2"))
                    pool.tensor_tensor(w2[:], w[:], w[:], ALU.mult).then_inc(turn, 1)
                    with pool.Fori(0, LEVELS) as level:
                        pool.wait_ge(turn, ahead(i, "scores", "wdec", level))
                        pool.tensor_tensor(wdec[:], w_tok[:], decay[:], ALU.mult).then_inc(turn, 1)
                    with pool.Fori(0, LEVELS) as level:
                        pool.wait_ge(turn, ahead(i, "values", "decayed", level))
                        pool.tensor_tensor(wdec[:], w[:], decay[:], ALU.mult)
                        pool.tensor_tensor(adec[:], probs_chan[:], decay[:], ALU.mult).then_inc(turn, 1)

            when_far(pool, units, first)

        @block.tensor
        def _(pe):
            def units():
                pe.wait_ge(consts_set, 4)
                with pe.Fori(0, GROUPS) as g:
                    pe.wait_ge(group_out, g + 1)
                    for n in range(2):
                        pe.matmul(outacc[n][:].rearrange("p a c -> p (a c)"), zeros[:, 0:P], zeros[:],
                                  start=True, stop=False, skip_group_check=True)
                    with pe.Fori(0, H) as h:
                        unit(g * H + h, g, h)

            def unit(i, g, h):
                cols = bass.ts(g, G)
                pe.wait_ge(turn, ahead(i, "front", "projected"))
                for n, w_col in enumerate((W_Q, W_K, W_V, W_W)):
                    for kk in range(KH):
                        pe.matmul(bank[n][:], hw[:, w_col + kk * P:w_col + (kk + 1) * P], xT_all[:, kk, cols],
                                  start=(kk == 0), stop=(kk == KH - 1))
                for p in range(NP):
                    pe.matmul(pc(bank[4], p), pc(f1, p), hw[:, W_F2:W_F2 + P], start=True, stop=True)
                pe.matmul(bank[5][:], hw[:, W_G2:W_G2 + P], g1T[:, cols], start=True, stop=True).then_inc(turn, 1)
                pe.wait_ge(turn, ahead(i, "front", "turned"))
                for p in range(NP):
                    pe.matmul(pc(bank[0], p), pc(k, p), pc(q, p), start=True, stop=True)
                    pe.transpose(pc(bank[3], p), pc(v, p), ident)
                    pe.matmul(pc(bank[4], p), pc(w2, p), ones[:], start=True, stop=True)
                    last = pe.transpose(pc(bank[5], p), pc(w, p), ident)
                last.then_inc(turn, 1)
                with pe.Fori(0, LEVELS) as level:
                    pe.wait_ge(turn, ahead(i, "scores", "dtok", level))
                    pe.wait_ge(tables_in, tables_count(i, 0, level))
                    pe.matmul(bank[1][:], sums, glog[:], start=True, stop=True).then_inc(turn, 1)
                    pe.wait_ge(turn, ahead(i, "scores", "products", level))
                    for p in range(NP):
                        last = pe.matmul(pc(bank[2], p), pc(qk, p), pc(wdec, p), start=True, stop=True)
                    last.then_inc(turn, 1)
                pe.wait_ge(turn, ahead(i, "softmax", "probsT"))
                for p in range(NP):
                    last = pe.transpose(pc(bank[3], p), pc(probs, p), ident)
                last.then_inc(turn, 1)
                with pe.Fori(0, LEVELS) as level:
                    pe.wait_ge(turn, ahead(i, "values", "dchan", level))
                    pe.wait_ge(tables_in, tables_count(i, 1, level))
                    for p in range(NP):
                        last = pe.matmul(pc(bank[1], p), pc(glog, p), sums, start=True, stop=True)
                    last.then_inc(turn, 1)
                    pe.wait_ge(turn, ahead(i, "values", "products", level))
                    for p in range(NP):
                        last = pe.matmul(pc(bank[2], p), pc(wdec, p), pc(adec, p), start=True, stop=True)
                    last.then_inc(turn, 1)
                pe.wait_ge(turn, ahead(i, "outputs", "o"))
                for p in range(NP):
                    last = pe.matmul(pc(bank[4], p), pc(mix, p), pc(v_tok, p), start=True, stop=True)
                last.then_inc(turn, 1)
                pe.wait_ge(turn, ahead(i, "outputs", "oT"))
                for p in range(NP):
                    last = pe.transpose(pc(bank[5], p), pc(o_tok, p), ident)
                last.then_inc(turn, 1)
                pe.wait_ge(turn, ahead(i, "outputs", "wo"))
                for p in range(NP):
                    last = pe.matmul(outacc[p // 2][:, p % 2, :], pc(o_chan, p), Wo[:, bass.ts(h, HID)],
                                     start=False, stop=False, skip_group_check=True)
                last.then_inc(turn, 1)

            when_far(pe, units)

        @block.scalar
        def _(act):
            def units():
                act.wait_ge(consts_set, 4)
                with act.Fori(0, UNITS) as i:
                    act.wait_ge(turn, ahead(i, "front", "taps"))
                    for n, t in enumerate((q, k, v, w)):
                        c = W_CONV + TAPS * n + TAPS - 1
                        act.activation(t[:], bank[n][:], ACT.Copy, scale=hw[:, c:c + 1])
                    act.activation(gate[:], bank[5][:], ACT.Tanh, bias=hbias[:], scale=0.5)
                    act.activation(gtmp[:], bank[4][:], ACT.Abs).then_inc(turn, 1)
                    act.wait_ge(turn, ahead(i, "front", "gexp"))
                    act.activation(gtmp[:], gtmp[:], ACT.Exp, scale=-1.0).then_inc(turn, 1)
                    act.wait_ge(turn, ahead(i, "front", "gln"))
                    act.activation(gtmp[:], gtmp[:], ACT.Ln, bias=1.0).then_inc(turn, 1)
                    act.wait_ge(turn, ahead(i, "front", "silus"))
                    for t in (q, k, v, w):
                        last = act.activation(t[:], t[:], ACT.Silu)
                    last.then_inc(turn, 1)
                    act.wait_ge(turn, ahead(i, "front", "lnw"))
                    act.copy(v_tok[:], bank[3][:])
                    act.copy(w_tok[:], bank[5][:])
                    act.activation(lnw[:], pairs(bank[4])[:, :, 0], ACT.Ln, bias=l2eps[:]).then_inc(turn, 1)
                    act.wait_ge(turn, ahead(i, "front", "rw"))
                    act.activation(rw[:], lnw[:], ACT.Exp, scale=-0.5).then_inc(turn, 1)
                    with act.Fori(0, LEVELS) as level:
                        act.wait_ge(turn, ahead(i, "scores", "decay", level))
                        act.activation(decay[:], bank[1][:], ACT.Exp).then_inc(turn, 1)
                    act.wait_ge(turn, ahead(i, "softmax", "exps"))
                    for p in range(NP):
                        last = act.activation(pc(probs, p), pc(score, p), ACT.Exp, bias=nmax[:, p:p + 1],
                                              scale=SCALE, accum_out=Z[:, p:p + 1])
                    last.then_inc(turn, 1)
                    act.wait_ge(turn, ahead(i, "softmax", "probs_chan"))
                    act.copy(probs_chan[:], bank[3][:]).then_inc(turn, 1)
                    with act.Fori(0, LEVELS) as level:
                        act.wait_ge(turn, ahead(i, "values", "decay", level))
                        act.activation(decay[:], bank[1][:], ACT.Exp).then_inc(turn, 1)
                    act.wait_ge(turn, ahead(i, "outputs", "osq"))
                    for p in range(NP):
                        last = act.activation(pc(osq, p), pc(bank[4], p), ACT.Square, accum_out=ssq[:, p:p + 1])
                    last.then_inc(turn, 1)
                    act.wait_ge(turn, ahead(i, "outputs", "lny"))
                    act.activation(lny[:], y[:], ACT.Ln).then_inc(turn, 1)
                    act.wait_ge(turn, ahead(i, "outputs", "rho"))
                    act.activation(rho[:], lny[:], ACT.Exp, scale=-0.5).then_inc(turn, 1)

            when_far(act, units)

        @block.vector
        def _(dve):
            def first():
                dve.sem_inc(group_out, 1)
                dve.wait_ge(x_back, 16)

            def units():
                with dve.Fori(0, GROUPS) as g:
                    with dve.Fori(0, H) as h:
                        unit(g * H + h)
                    dve.wait_ge(turn, through(g * H + (H - 1), "outputs", "wo"))
                    for m in range(2):
                        xs = x_all[:, bass.ds(g * NP + 2 * m, 2), :]
                        last = dve.tensor_tensor(xs, xs, outacc[m][:], ALU.add)
                    last.then_inc(group_out, 1)

            def unit(i):
                for shift in range(1, TAPS):
                    dve.wait_ge(turn, ahead(i, "front", f"conv{shift}"))
                    if shift == 1:
                        dve.scalar_tensor_tensor(out=glog[:], in0=bank[4][:], scalar=0.0, in1=gtmp[:], op0=ALU.min,
                                                 op1=ALU.subtract)
                    for n, t in enumerate((q, k, v, w)):
                        x3 = bank[n][:].rearrange("p (s t) -> p s t", s=NS)
                        d3 = t[:].rearrange("p (s t) -> p s t", s=NS)
                        c = W_CONV + TAPS * n + TAPS - 1 - shift
                        last = dve.scalar_tensor_tensor(out=d3[:, :, shift:T], in0=x3[:, :, 0:T - shift],
                                                        scalar=hw[:, c:c + 1], in1=d3[:, :, shift:T],
                                                        op0=ALU.mult, op1=ALU.add)
                    last.then_inc(turn, 1)
                dve.wait_ge(turn, ahead(i, "front", "coef"))
                dve.memset(score[:], 0.0)
                dve.memset(mix[:], 0.0)
                dve.tensor_tensor(coef[:], rw[:], beta.rearrange("p g h q -> p (g h q)")[:, bass.ts(i, NP)],
                                  ALU.mult).then_inc(turn, 1)
                with dve.Fori(0, LEVELS) as level:
                    dve.wait_ge(turn, ahead(i, "scores", "qk", level))
                    for p in range(NP):
                        last = dve.scalar_tensor_tensor(out=pc(qk, p), in0=pc(bank[0], p), scalar=coef[:, p:p + 1],
                                                        in1=mask, op0=ALU.mult, op1=ALU.mult)
                    last.then_inc(turn, 1)
                    dve.wait_ge(turn, ahead(i, "scores", "decayed", level))
                    dve.tensor_tensor(part[:], bank[2][:], decay[:], ALU.mult).then_inc(turn, 1)
                    dve.wait_ge(turn, ahead(i, "scores", "summed", level))
                    dve.tensor_tensor(score[:], score[:], part[:], ALU.add).then_inc(turn, 1)
                dve.wait_ge(turn, ahead(i, "softmax", "smax"))
                dve.tensor_reduce(smax[:], pairs(score), AX.X, ALU.max).then_inc(turn, 1)
                dve.wait_ge(turn, ahead(i, "softmax", "nmax"))
                dve.tensor_scalar(nmax[:], smax[:], -SCALE, None, ALU.mult).then_inc(turn, 1)
                dve.wait_ge(turn, ahead(i, "softmax", "Zeps"))
                dve.scalar_tensor_tensor(out=Zeps[:], in0=Z[:], scalar=4.0 * EPS, in1=Z[:], op0=ALU.mult,
                                         op1=ALU.mult).then_inc(turn, 1)
                with dve.Fori(0, LEVELS) as level:
                    dve.wait_ge(turn, ahead(i, "values", "masked", level))
                    for p in range(NP):
                        last = dve.scalar_tensor_tensor(out=pc(part, p), in0=pc(bank[2], p), scalar=coef[:, p:p + 1],
                                                        in1=mask, op0=ALU.mult, op1=ALU.mult)
                    last.then_inc(turn, 1)
                    dve.wait_ge(turn, ahead(i, "values", "summed", level))
                    dve.tensor_tensor(mix[:], mix[:], part[:], ALU.add).then_inc(turn, 1)
                dve.wait_ge(turn, ahead(i, "outputs", "y"))
                dve.scalar_tensor_tensor(out=y[:], in0=ssq[:], scalar=4.0 / P, in1=Zeps[:], op0=ALU.mult,
                                         op1=ALU.add).then_inc(turn, 1)
                dve.wait_ge(turn, ahead(i, "outputs", "o_tok"))
                for p in range(NP):
                    last = dve.tensor_scalar(pc(o_tok, p), pc(bank[4], p), rho[:, p:p + 1], None, ALU.mult)
                last.then_inc(turn, 1)
                dve.wait_ge(turn, ahead(i, "outputs", "o_chan"))
                dve.scalar_tensor_tensor(out=o_chan[:], in0=gate[:], scalar=1.0, in1=bank[5][:], op0=ALU.add,
                                         op1=ALU.mult).then_inc(turn, 1)

            when_far(dve, units, first)


def context_block(nc, sems, ctx_all, ctxT, gq_gk, gqk, WvT, Wo, xT_pad, ident, loaded, loaded_count):
    with ExitStack() as ctx:
        def sem(name):
            return sems(name)

        banks = [ctx.enter_context(nc.psum_tensor(f"ctx_turned{k}", [P, G], F32)) for k in range(2)]
        WvWo = [ctx.enter_context(nc.psum_tensor(f"WvWo{k}", [P, 2, HID], F32)) for k in range(2)]
        turned = sem("ctx_turned")
        kept = sem("ctx_kept")
        gqk_done = sem("gqk_done")
        padded = sem("ctx_padded")
        product = sem("WvWo_product")
        product_kept = sem("WvWo_kept")
        block = ctx.enter_context(nc.Block())

        @block.gpsimd
        def _(pool):
            pool.memset(ctxT[:, TOKENS:TOKENS + G], 0.0).then_inc(padded, 1)
            pool.memset(xT_pad, 0.0).then_inc(padded, 1)

        @block.tensor
        def _(pe):
            pe.wait_ge(loaded, loaded_count)
            for g in range(GROUPS):
                if g >= 2:
                    pe.wait_ge(kept, g - 1)
                for p in range(NP):
                    last = pe.transpose(banks[g % 2][:, p * P:(p + 1) * P], ctx_all[:, g * NP + p, :], ident)
                last.then_inc(turned, 1)
            for m in range(H // 2):
                if m >= 2:
                    pe.wait_ge(product_kept, m - 1)
                for n in range(2):
                    h = 2 * m + n
                    last = pe.matmul(WvWo[m % 2][:, n, :], WvT[:, h, :], Wo[:, h * HID:(h + 1) * HID],
                                     start=True, stop=True)
                last.then_inc(product, 1)

        @block.scalar
        def _(act):
            for g in range(GROUPS):
                act.wait_ge(turned, g + 1)
                act.copy(ctxT[:, g * G:(g + 1) * G], banks[g % 2][:]).then_inc(kept, 1)

        @block.vector
        def _(dve):
            dve.wait_ge(loaded, loaded_count)
            dve.tensor_tensor(gqk[:], gq_gk[:, 0:1], gq_gk[:, 1:2], ALU.mult).then_inc(gqk_done, 1)
            for m in range(H // 2):
                dve.wait_ge(product, m + 1)
                dve.tensor_copy(Wo[:, 2 * m * HID:(2 * m + 2) * HID], WvWo[m % 2][:].rearrange("p a c -> p (a c)"))\
                    .then_inc(product_kept, 1)


def cross_block(nc, sems, w_heads, x_all, xT_all, ctx_all, ctxT, gqk, WvWo, ident):
    with ExitStack() as ctx:
        def sb(name, shape, dt=F32):
            return ctx.enter_context(nc.sbuf_tensor(f"x_{name}", shape, dt))

        def psum(name, shape, dt=F32):
            return ctx.enter_context(nc.psum_tensor(f"x_{name}", shape, dt))

        def sem(name):
            return sems(f"x_{name}")

        hw = [sb(f"head_weights{i}", [P, X_HEAD]) for i in range(2)]
        xg = sb("xg", [P, KH, G])
        ctxTg = sb("ctxTg", [P, G])
        ctxg = sb("ctxg", [P, NP, CDIM])
        squares = sb("squares", [P, G])
        k_tok = sb("k_tok", [P, G])
        q_tok = sb("q_tok", [P, G])
        k = sb("k_chan", [P, G])
        q = sb("q_chan", [P, G])
        score = sb("score", [P, NP, T])
        probs = sb("probs", [P, NP, T])
        wide = sb("wide", [P, NP, P])
        wide_chan = sb("wide_chan", [P, G])
        pc_chan = sb("pc_chan", [P, G])
        eps = sb("eps", [P, 1])
        zeros = sb("zeros", [P, G], BF16)
        ssk, lnk, rk = sb("ssk", [P, NP]), sb("lnk", [P, NP]), sb("rk", [P, NP])
        ssq, lnq, rq = sb("ssq", [P, NP]), sb("lnq", [P, NP]), sb("rq", [P, NP])
        smax = sb("smax", [P, NP])
        Z = sb("Z", [P, NP])
        rZ = sb("rZ", [P, NP])
        k_raw, q_raw, kT, qT, scores_ps, out_ps = (
            psum(n, [P, G]) for n in ("k_raw", "q_raw", "kT", "qT", "scores_ps", "out_ps"))
        outacc = [psum(f"outacc{n}", [P, 2, HID]) for n in range(2)]

        primed = {
            "tensor": "k_x q_x turned_x scores_x probsT_x pc_x wo_x",
            "scalar": "ssk_s lnk_s rk_s ssq_s lnq_s rq_s k_s exps wide_chan_s pc_chan_s",
            "vector": "q_s k_tok_s q_tok_s smax_s sub_s Z_s rZ_s wide_s",
        }
        S = {n: sem(n) for names in primed.values() for n in names.split()}
        weights_in = [sem(f"weights_in{i}") for i in range(2)]
        consts_set = sem("consts_set")
        group_in = sem("group_in")
        group_ctx_in = sem("group_ctx_in")
        group_out = sem("group_out")
        block = ctx.enter_context(nc.Block())

        def prime(eng, who):
            for n in primed[who].split():
                eng.sem_inc(S[n], 1)

        def done(n, times=1):
            return times * (n + 1) + 1

        def before(n, times=1):
            return times * n + 1

        def run_units(eng, first, second, merged, group_start=None, group_end=None):
            first()
            second()
            with eng.Fori(0, GROUPS) as g:
                if group_start is not None:
                    group_start(g)
                with eng.Fori(0, H // 2) as i:
                    for par in range(2):
                        merged(g * H + i * 2 + par, i * 2 + par, par)
                if group_end is not None:
                    group_end(g)

        def pc(t, p):
            return t[:, p * P:(p + 1) * P]

        def over(t, n):
            return t.unsqueeze(2).broadcast_to([P, NP, n])

        @block.sync
        def _(sp):
            def load(n, h, par):
                sp.dma_start(hw[par][:], w_heads[h]).then_inc(weights_in[par], 16)

            load(0, 0, 0)
            load(1, 1, 1)
            with sp.Fori(0, UNITS // 2) as m:
                for par in range(2):
                    n = 2 * m + par
                    sp.wait_ge(S["q_x"], done(n))
                    load(n + 2, (n + 2) % H, par)

        @block.gpsimd
        def _(pool):
            pool.memset(eps[:], EPS).then_inc(consts_set, 1)
            pool.memset(zeros[:], 0.0).then_inc(consts_set, 1)
            pool.memset(wide[:], 0.0).then_inc(consts_set, 1)
            with pool.Fori(0, GROUPS) as g:
                pool.wait_ge(S["k_x"], before(g * H))
                pool.tensor_copy(ctxTg[:], ctxT[:, bass.ts(g, G)]).then_inc(group_in, 1)
                pool.wait_ge(S["q_x"], before(g * H))
                pool.tensor_copy(xg[:], xT_all[:, :, bass.ts(g, G)]).then_inc(group_in, 1)
                pool.wait_ge(S["pc_x"], before(g * H))
                pool.tensor_copy(ctxg[:], ctx_all[:, bass.ts(g, NP), :]).then_inc(group_ctx_in, 1)
            pool.wait_ge(S["k_x"], before(UNITS))
            pool.tensor_copy(ctxTg[:], ctxT[:, TOKENS:TOKENS + G]).then_inc(group_in, 1)
            pool.wait_ge(S["q_x"], before(UNITS))
            pool.tensor_copy(xg[:], xT_all[:, :, TOKENS:TOKENS + G]).then_inc(group_in, 1)

        @block.tensor
        def _(pe):
            prime(pe, "tensor")
            pe.wait_ge(consts_set, 3)

            def project_k(n, par):
                pe.wait_ge(weights_in[par], 16 * (n // 2 + 1))
                pe.wait_ge(group_in, 2 * (n // H + 1))
                pe.wait_ge(S["k_tok_s"], before(n))
                for p in range(NP):
                    last = pe.matmul(pc(k_raw, p), pc(ctxTg, p), hw[par][:, X_K:X_K + P], start=True, stop=True)
                last.then_inc(S["k_x"], 1)

            def project_q(n, par):
                pe.wait_ge(S["q_tok_s"], before(n))
                for p in range(NP):
                    for kk in range(KH):
                        last = pe.matmul(pc(q_raw, p), xg[:, kk, p * P:(p + 1) * P],
                                         hw[par][:, X_Q + kk * P:X_Q + (kk + 1) * P],
                                         start=(kk == 0), stop=(kk == KH - 1))
                last.then_inc(S["q_x"], 1)

            def turn(m):
                pe.wait_ge(S["k_tok_s"], done(m))
                pe.wait_ge(S["k_s"], before(m))
                for p in range(NP):
                    pe.transpose(pc(kT, p), pc(k_tok, p), ident)
                pe.wait_ge(S["q_tok_s"], done(m))
                pe.wait_ge(S["q_s"], before(m))
                for p in range(NP):
                    last = pe.transpose(pc(qT, p), pc(q_tok, p), ident)
                last.then_inc(S["turned_x"], 1)

            def scores(m):
                pe.wait_ge(S["k_s"], done(m))
                pe.wait_ge(S["q_s"], done(m))
                pe.wait_ge(S["sub_s"], before(m))
                for p in range(NP):
                    for half in range(2):
                        at = slice(p * P + half * T, p * P + (half + 1) * T)
                        last = pe.matmul(scores_ps[half * T:(half + 1) * T, p * T:(p + 1) * T], q[:, at], k[:, at],
                                         start=True, stop=True)
                last.then_inc(S["scores_x"], 1)

            def merged(j, h, par):
                turn(j + 1)
                project_k(j + 2, par)
                pe.wait_ge(S["wide_s"], done(j, 2))
                pe.wait_ge(S["pc_chan_s"], before(j))
                for p in range(NP):
                    last = pe.transpose(pc(out_ps, p), wide[:, p, :], ident)
                last.then_inc(S["probsT_x"], 1)
                project_q(j + 2, par)
                pe.wait_ge(group_ctx_in, j // H + 1)
                pe.wait_ge(S["wide_chan_s"], done(j))
                for p in range(NP):
                    last = pe.matmul(pc(out_ps, p), ctxg[:, p, :], pc(wide_chan, p), start=True, stop=True)
                last.then_inc(S["pc_x"], 1)
                scores(j + 1)
                pe.wait_ge(S["pc_chan_s"], done(j))
                for p in range(NP):
                    last = pe.matmul(outacc[p // 2][:, p % 2, :], pc(pc_chan, p), WvWo[:, bass.ts(h, HID)],
                                     start=False, stop=False, skip_group_check=True)
                last.then_inc(S["wo_x"], 1)

            def first():
                project_k(0, 0)
                project_q(0, 0)

            def second():
                turn(0)
                project_k(1, 1)
                project_q(1, 1)
                scores(0)

            def group_start(g):
                pe.wait_ge(group_out, g + 1)
                for n in range(2):
                    pe.matmul(outacc[n][:].rearrange("p a c -> p (a c)"), zeros[:, 0:P], zeros[:],
                              start=True, stop=False, skip_group_check=True)

            run_units(pe, first, second, merged, group_start=group_start)

        @block.scalar
        def _(act):
            act.preload_act_table_set("natural_log_exp_and_others")
            prime(act, "scalar")
            act.wait_ge(consts_set, 3)

            def rms(n, raw, raw_step, ss, ln, r, ss_step, ln_step, r_step, scaled_step):
                act.wait_ge(S[ln_step], before(n))
                act.wait_ge(S[raw_step], done(n))
                for p in range(NP):
                    act.activation(pc(squares, p), pc(raw, p), ACT.Square, accum_out=ss[:, p:p + 1])\
                        .then_inc(S[ss_step], 1)
                act.wait_ge(S[ss_step], done(n, NP))
                act.wait_ge(S[r_step], before(n))
                act.activation(ln[:], ss[:], ACT.Ln, bias=eps[:], scale=1.0 / P).then_inc(S[ln_step], 1)
                act.wait_ge(S[ln_step], done(n))
                act.wait_ge(S[scaled_step], before(n))
                act.activation(r[:], ln[:], ACT.Exp, scale=-0.5).then_inc(S[r_step], 1)

            def rms_k(n):
                rms(n, k_raw, "k_x", ssk, lnk, rk, "ssk_s", "lnk_s", "rk_s", "k_tok_s")

            def rms_q(n):
                rms(n, q_raw, "q_x", ssq, lnq, rq, "ssq_s", "lnq_s", "rq_s", "q_tok_s")

            def keep_k(m):
                act.wait_ge(S["turned_x"], done(m))
                act.wait_ge(S["scores_x"], before(m))
                act.activation(k[:], kT[:], ACT.Copy, scale=gqk[:]).then_inc(S["k_s"], 1)

            def exps(m):
                act.wait_ge(S["sub_s"], done(m))
                act.wait_ge(S["wide_s"], before(m, 2))
                act.activation(probs[:], score[:], ACT.Exp, scale=SCALE).then_inc(S["exps"], 1)

            def first():
                rms_k(0)
                rms_q(0)

            def second():
                keep_k(0)
                rms_k(1)
                rms_q(1)
                exps(0)

            def merged(j, h, par):
                keep_k(j + 1)
                rms_k(j + 2)
                act.wait_ge(S["probsT_x"], done(j))
                act.wait_ge(S["pc_x"], before(j))
                act.copy(wide_chan[:], out_ps[:]).then_inc(S["wide_chan_s"], 1)
                rms_q(j + 2)
                act.wait_ge(S["pc_x"], done(j))
                act.wait_ge(S["wo_x"], before(j))
                act.copy(pc_chan[:], out_ps[:]).then_inc(S["pc_chan_s"], 1)
                exps(j + 1)

            run_units(act, first, second, merged)

        @block.vector
        def _(dve):
            prime(dve, "vector")
            dve.sem_inc(group_out, 1)
            dve.wait_ge(consts_set, 3)

            def normalise(n):
                dve.wait_ge(S["rk_s"], done(n))
                dve.wait_ge(S["turned_x"], before(n))
                for p in range(NP):
                    last = dve.tensor_scalar(pc(k_tok, p), pc(k_raw, p), rk[:, p:p + 1], None, ALU.mult)
                last.then_inc(S["k_tok_s"], 1)
                dve.wait_ge(S["rq_s"], done(n))
                for p in range(NP):
                    last = dve.tensor_scalar(pc(q_tok, p), pc(q_raw, p), rq[:, p:p + 1], None, ALU.mult)
                last.then_inc(S["q_tok_s"], 1)

            def keep_q(m):
                dve.wait_ge(S["turned_x"], done(m))
                dve.wait_ge(S["scores_x"], before(m))
                dve.tensor_copy(q[:], qT[:]).then_inc(S["q_s"], 1)

            def softmax(m):
                s3 = scores_ps[:, 0:NP * T].rearrange("p (q t) -> p q t", q=NP)
                dve.wait_ge(S["scores_x"], done(m))
                dve.tensor_reduce(smax[:], s3, AX.X, ALU.max).then_inc(S["smax_s"], 1)
                dve.wait_ge(S["smax_s"], done(m))
                dve.wait_ge(S["exps"], before(m))
                dve.tensor_tensor(score[:], s3, over(smax[:], T), ALU.subtract).then_inc(S["sub_s"], 1)
                dve.wait_ge(S["exps"], done(m))
                dve.tensor_reduce(Z[:], probs[:], AX.X, ALU.add).then_inc(S["Z_s"], 1)
                dve.wait_ge(S["Z_s"], done(m))
                dve.reciprocal(rZ[:], Z[:]).then_inc(S["rZ_s"], 1)
                dve.wait_ge(S["rZ_s"], done(m))
                dve.wait_ge(S["probsT_x"], before(m))
                for half in range(2):
                    rows = slice(half * T, (half + 1) * T)
                    dve.tensor_tensor(wide[rows, :, half * T:(half + 1) * T], probs[rows, :, :],
                                      over(rZ[:], T)[rows], ALU.mult).then_inc(S["wide_s"], 1)

            def first():
                normalise(0)

            def second():
                keep_q(0)
                normalise(1)
                softmax(0)

            def merged(j, h, par):
                keep_q(j + 1)
                normalise(j + 2)
                softmax(j + 1)

            def group_end(g):
                dve.wait_ge(S["wo_x"], before(g * H + H))
                for m in range(2):
                    xs = x_all[:, bass.ds(g * NP + 2 * m, 2), :]
                    last = dve.tensor_tensor(xs, xs, outacc[m][:], ALU.add)
                last.then_inc(group_out, 1)

            run_units(dve, first, second, merged, group_end=group_end)


def experts_block(nc, sems, x_all, xT_all, gate_w, experts, expert_b, lower, ident, loaded, loaded_count, out_view):
    EP = E // 2
    RING = 4
    with ExitStack() as ctx:
        def sb(name, shape, dt=F32):
            return ctx.enter_context(nc.sbuf_tensor(f"e_{name}", shape, dt))

        def psum(name, shape, dt=F32):
            return ctx.enter_context(nc.psum_tensor(f"e_{name}", shape, dt))

        def sem(name):
            return sems(f"e_{name}")

        xg = [sb(f"xg{i}", [P, KH, G]) for i in range(2)]
        logits = sb("logits", [P, NP, E])
        above = sb("above", [P, NP, E, E])
        ties = sb("ties", [P, NP, E, E])
        rank = sb("rank", [P, NP, E])
        top = sb("top", [P, NP])
        shifted = sb("shifted", [P, NP, E])
        ex = sb("ex", [P, NP, E])
        chosen = sb("chosen", [P, NP, E])
        Z = sb("Z", [P, NP])
        rZ = sb("rZ", [P, NP])
        gates = sb("gates", [P, NP, E])
        gatesT = sb("gatesT", [E, G])
        y = [psum(f"y{i}", [P, 2, HID]) for i in range(RING)]
        small = psum("small", [P, NP, E])
        gT = psum("gT", [E, G])
        bias = [psum(f"bias{i}", [P, 2, HID]) for i in range(2)]

        primed = {
            "tensor": "logit gatesT_x bias_x y_x",
            "scalar": "exps gatesT_s",
            "vector": "logits_s above_s ties_s tied_s beats_s rank_s top_s shifted_s chosen_s Z_s rZ_s gates_s "
                      "biased y_s",
            "gpsimd": "xg_s",
        }
        S = {n: sem(n) for names in primed.values() for n in names.split()}
        stored = sem("stored")
        block = ctx.enter_context(nc.Block())
        YS = NP * EP

        def prime(eng, who):
            for n in primed[who].split():
                eng.sem_inc(S[n], 1)

        def done(n, times=1):
            return times * (n + 1) + 1

        def before(n, times=1):
            return times * n + 1

        def over(t, n):
            return t.unsqueeze(2).broadcast_to([P, NP, n])

        @block.sync
        def _(sp):
            with sp.Fori(0, GROUPS) as g:
                sp.wait_ge(S["y_s"], done(g, 2 * YS))
                sp.dma_start(out_view[:, bass.ds(g * NP, NP), :], x_all[:, bass.ds(g * NP, NP), :])\
                    .then_inc(stored, 16)
            sp.wait_ge(stored, 16 * GROUPS)

        @block.gpsimd
        def _(pool):
            prime(pool, "gpsimd")
            with pool.Fori(0, GROUPS // 2) as m:
                for par in range(2):
                    g = 2 * m + par
                    pool.wait_ge(S["y_x"], before(g, YS))
                    pool.tensor_copy(xg[par][:], xT_all[:, :, bass.ts(g, G)]).then_inc(S["xg_s"], 1)

        @block.tensor
        def _(pe):
            prime(pe, "tensor")
            pe.wait_ge(loaded, loaded_count)
            with pe.Fori(0, GROUPS // 2) as m:
                for par in range(2):
                    g = 2 * m + par
                    pe.wait_ge(S["xg_s"], done(g))
                    pe.wait_ge(S["logits_s"], before(g))
                    for p in range(NP):
                        for k in range(KH):
                            last = pe.matmul(small[:, p, :], xg[par][:, k, p * P:(p + 1) * P], gate_w[:, k, :],
                                             start=(k == 0), stop=(k == KH - 1))
                    last.then_inc(S["logit"], 1)
                    for p in range(NP):
                        for ep in range(EP):
                            u = p * EP + ep
                            pe.wait_ge(S["y_s"], before(g, 2 * YS) + 2 * (u + 1 - RING) if u >= RING
                                       else before(g, 2 * YS))
                            for k in range(KH):
                                last = pe.matmul(y[u % RING][:].rearrange("p a c -> p (a c)"),
                                                 xg[par][:, k, p * P:(p + 1) * P],
                                                 experts[:, k, 2 * ep:2 * ep + 2, :].rearrange("p a c -> p (a c)"),
                                                 start=(k == 0), stop=(k == KH - 1))
                            last.then_inc(S["y_x"], 1)
                            if u == RING - 1:
                                pe.wait_ge(S["gates_s"], done(g))
                                for pp in range(NP):
                                    last = pe.transpose(gT[:, pp * P:(pp + 1) * P], gates[:, pp, :], ident)
                                last.then_inc(S["gatesT_x"], 1)
                                pe.wait_ge(S["gatesT_s"], done(g))
                                pe.wait_ge(S["biased"], before(g))
                                for pp in range(NP):
                                    last = pe.matmul(bias[pp // 2][:, pp % 2, :], gatesT[:, pp * P:(pp + 1) * P],
                                                     expert_b[:], start=True, stop=True)
                                last.then_inc(S["bias_x"], 1)

        @block.scalar
        def _(act):
            prime(act, "scalar")
            with act.Fori(0, GROUPS) as g:
                act.wait_ge(S["shifted_s"], done(g))
                act.wait_ge(S["chosen_s"], before(g))
                act.activation(ex[:], shifted[:], ACT.Exp).then_inc(S["exps"], 1)
                act.wait_ge(S["gatesT_x"], done(g))
                act.wait_ge(S["bias_x"], before(g))
                act.copy(gatesT[:], gT[:]).then_inc(S["gatesT_s"], 1)

        @block.vector
        def _(dve):
            prime(dve, "vector")
            dve.wait_ge(loaded, loaded_count)
            theirs = logits[:].unsqueeze(2).broadcast_to([P, NP, E, E])
            own = logits[:].unsqueeze(3).broadcast_to([P, NP, E, E])
            earlier = lower.rearrange("p (a b) -> p a b", a=E).unsqueeze(1).broadcast_to([P, NP, E, E])
            with dve.Fori(0, GROUPS) as g:
                dve.wait_ge(S["logit"], done(g))
                dve.wait_ge(S["shifted_s"], before(g))
                dve.tensor_copy(logits[:], small[:]).then_inc(S["logits_s"], 1)
                dve.wait_ge(S["logits_s"], done(g))
                dve.tensor_tensor(above[:], theirs, own, ALU.is_gt).then_inc(S["above_s"], 1)
                dve.tensor_tensor(ties[:], theirs, own, ALU.is_equal).then_inc(S["ties_s"], 1)
                dve.wait_ge(S["ties_s"], done(g))
                dve.tensor_tensor(ties[:], ties[:], earlier, ALU.mult).then_inc(S["tied_s"], 1)
                dve.wait_ge(S["tied_s"], done(g))
                dve.wait_ge(S["above_s"], done(g))
                dve.tensor_tensor(above[:], above[:], ties[:], ALU.add).then_inc(S["beats_s"], 1)
                dve.wait_ge(S["beats_s"], done(g))
                dve.tensor_reduce(rank[:], above[:], AX.X, ALU.add).then_inc(S["rank_s"], 1)
                dve.tensor_reduce(top[:], logits[:], AX.X, ALU.max).then_inc(S["top_s"], 1)
                dve.wait_ge(S["top_s"], done(g))
                dve.wait_ge(S["exps"], before(g))
                dve.tensor_tensor(shifted[:], logits[:], over(top[:], E), ALU.subtract).then_inc(S["shifted_s"], 1)
                dve.wait_ge(S["exps"], done(g))
                dve.wait_ge(S["rank_s"], done(g))
                dve.scalar_tensor_tensor(out=chosen[:], in0=rank[:], scalar=TOPK - 0.5, in1=ex[:], op0=ALU.is_lt,
                                         op1=ALU.mult).then_inc(S["chosen_s"], 1)
                dve.wait_ge(S["chosen_s"], done(g))
                dve.tensor_reduce(Z[:], chosen[:], AX.X, ALU.add).then_inc(S["Z_s"], 1)
                dve.wait_ge(S["Z_s"], done(g))
                dve.reciprocal(rZ[:], Z[:]).then_inc(S["rZ_s"], 1)
                dve.wait_ge(S["rZ_s"], done(g))
                dve.wait_ge(S["bias_x"], before(g))
                dve.tensor_tensor(gates[:], chosen[:], over(rZ[:], E), ALU.mult).then_inc(S["gates_s"], 1)
                dve.wait_ge(S["gates_s"], done(g))
                for p in range(NP):
                    xp = x_all[:, g * NP + p, :]
                    for ex_ in range(E):
                        u = p * EP + ex_ // 2
                        dve.wait_ge(S["y_x"], before(g, YS) + u + 1)
                        if p + ex_ > 0:
                            dve.wait_ge(S["y_s"], before(g, 2 * YS) + p * E + ex_)
                        dve.scalar_tensor_tensor(out=xp, in0=y[u % RING][:, ex_ % 2, :],
                                                 scalar=gates[:, p, ex_:ex_ + 1], in1=xp, op0=ALU.mult,
                                                 op1=ALU.add).then_inc(S["y_s"], 1)
                    if p == 0:
                        dve.wait_ge(S["bias_x"], done(g))
                        dve.wait_ge(S["y_s"], before(g, 2 * YS) + E)
                        for m in range(2):
                            xs = x_all[:, bass.ds(g * NP + 2 * m, 2), :]
                            last = dve.tensor_tensor(xs, xs, bias[m][:], ALU.add)
                        last.then_inc(S["biased"], 1)
                        dve.wait_ge(S["biased"], done(g))


def decoder_layer(nc, ins, outs):
    with ExitStack() as ctx:
        def sb(name, shape, dt=F32):
            return ctx.enter_context(nc.sbuf_tensor(name, shape, dt))

        x_all = sb("x_all", [P, PAIRS, HID])
        cst = sb("cst", [P, 3 * P + E * E])
        lower = cst[:, 3 * P:3 * P + E * E]
        ident, span, causal = cst[:, 0:P], cst[:, P:2 * P], cst[:, 2 * P:3 * P]
        far_flag = sb("far_flag", [1, 1], mybir.dt.int32)
        x_view = ins["x"].rearrange("b t c -> (b t) c").rearrange("(q p) c -> p q c", p=P)
        o_view = outs[0].rearrange("b t c -> (b t) c").rearrange("(q p) c -> p q c", p=P)

        with ExitStack() as stage:
            sems = stage.enter_context(stage_semaphores(nc))

            def st(name, shape, dt=F32):
                return stage.enter_context(nc.sbuf_tensor(name, shape, dt))

            xT_all = st("xT_all", [P, KH, TOKENS + G])
            f1T = st("f1T", [P, TOKENS + G])
            g1T = st("g1T", [P, TOKENS + G])
            beta = st("beta", [P, GROUPS + 1, H, NP])
            Wf1g1 = st("Wf1g1", [P, KH, 2, P])
            Wb = st("Wb", [P, KH, H])
            Wo = st("Wo", [P, H * HID])
            norm_w = st("norm_w", [P, 1])
            layernorm_block(nc, sems, "ln1", x_all, xT_all, ident, load=[
                (cst[:], ins["consts"]), (x_all[:], x_view), (Wf1g1[:], ins["Wf1g1"]), (Wb[:], ins["Wb"]),
                (norm_w[:], ins["norm_w"]), (Wo[:], ins["Wo"])])
            lowrank_block(nc, sems, xT_all, f1T, g1T, beta[:, 0:GROUPS], Wf1g1, Wb, ident)
            wo_scaled = sems("wo_scaled")
            with nc.Block() as block:
                @block.vector
                def _(dve):
                    dve.tensor_scalar(Wo[:], Wo[:], norm_w[:], None, ALU.mult).then_inc(wo_scaled, 1)

                @block.gpsimd
                def _(pool):
                    pool.memset(xT_all[:, :, TOKENS:TOKENS + G], 0.0).then_inc(wo_scaled, 1)
                    pool.memset(f1T[:, TOKENS:TOKENS + G], 0.0).then_inc(wo_scaled, 1)
                    pool.memset(g1T[:, TOKENS:TOKENS + G], 0.0).then_inc(wo_scaled, 1)
                    pool.memset(beta[:, GROUPS:GROUPS + 1], 0.0).then_inc(wo_scaled, 1)
            gsa_block(nc, sems, ins["w_heads"], x_all, xT_all, f1T, g1T, beta[:], Wo, (ident, span, causal),
                      far_flag)
            with stage_semaphores(nc) as general_sems:
                gsa_general_block(nc, general_sems, ins["w_heads"], ins["tables"], x_all, x_view, xT_all, f1T, g1T,
                                  beta[:], Wo, (ident, span, causal), far_flag)
        with ExitStack() as stage:
            sems = stage.enter_context(stage_semaphores(nc))

            def st(name, shape, dt=F32):
                return stage.enter_context(nc.sbuf_tensor(name, shape, dt))

            xT_all = st("xT2_all", [P, KH, TOKENS + G])
            ctxT = st("ctxT", [P, TOKENS + G])
            ctx_all = st("ctx_all", [P, PAIRS, CDIM])
            gq_gk = st("gq_gk", [P, 2])
            gqk = st("gqk", [P, 1])
            xWo = st("xWo", [P, H * HID])
            WvT = st("WvT", [P, H, CDIM])
            gate_w = st("gate_w", [P, KH, E])
            experts = st("experts", [P, KH, E, HID])
            expert_b = st("expert_b", [E, HID])
            c_view = ins["ctx"].rearrange("b t c -> (b t) c").rearrange("(q p) c -> p q c", p=P)
            context_in, experts_in = sems("context_in"), sems("experts_in")
            from_dram = [(ctx_all[:], c_view), (gq_gk[:], ins["gq_gk"]), (WvT[:], ins["xWvT"]),
                         (xWo[:], ins["xWo"])]
            layernorm_block(nc, sems, "ln2", x_all, xT_all, ident, prefetch=from_dram, prefetched=context_in)
            context_block(nc, sems, ctx_all, ctxT, gq_gk, gqk, WvT, xWo, xT_all[:, :, TOKENS:TOKENS + G], ident,
                          context_in, 16 * len(from_dram))
            cross_block(nc, sems, ins["x_heads"], x_all, xT_all, ctx_all, ctxT, gqk, xWo, ident)
            from_dram = [(gate_w[:], ins["gate_w"]), (experts[:], ins["experts"]), (expert_b[:], ins["expert_b"])]
            layernorm_block(nc, sems, "ln3", x_all, xT_all, ident, prefetch=from_dram, prefetched=experts_in)
            experts_block(nc, sems, x_all, xT_all, gate_w, experts, expert_b, lower, ident, experts_in,
                          16 * len(from_dram), o_view)


def layout(inputs):
    a = {n: np.ascontiguousarray(v) for n, v in inputs.items()}

    def by_head(w):
        rows = w.shape[0]
        return w.reshape(rows // P, P, H, P).transpose(2, 1, 0, 3).reshape(H, P, -1)

    conv = np.stack([a[f"L0_attn_c{n}"].reshape(H, P, TAPS) for n in "qkv"] +
                    [a["L0_attn_cv"].reshape(H, P, TAPS)], axis=2).reshape(H, P, 4 * TAPS)
    w_heads = np.concatenate(
        [by_head(a[f"L0_attn_W{n}"]) for n in "qkvw"] + [by_head(a["L0_attn_Wf2"]), by_head(a["L0_attn_Wg2"]),
         conv, a["L0_attn_bg2"].reshape(H, P, 1)], axis=2)
    f1g1 = np.stack([a["L0_attn_Wf1"].reshape(KH, P, P), a["L0_attn_Wg1"].reshape(KH, P, P)], axis=2)
    return {
        "x": a["x"],
        "consts": shape_constants(),
        "tables": level_tables(),
        "w_heads": w_heads,
        "Wf1g1": f1g1.transpose(1, 0, 2, 3),
        "Wb": a["L0_attn_Wb"].reshape(KH, P, H).transpose(1, 0, 2),
        "norm_w": a["L0_attn_norm_w"].reshape(P, 1),
        "ctx": a["ctx_1024"],
        "x_heads": np.concatenate([by_head(a[f"L0_xattn_W{n}"]) for n in "qk"], axis=2),
        "xWvT": a["L0_xattn_Wv"].reshape(CDIM, H, P).transpose(2, 1, 0),
        "gq_gk": np.stack([a["L0_xattn_gq"], a["L0_xattn_gk"]], axis=1),
        "xWo": a["L0_xattn_Wo"].reshape(H, P, HID).transpose(1, 0, 2).reshape(P, H * HID),
        "gate_w": a["L0_ffn_gate_w"].T.reshape(KH, P, E).transpose(1, 0, 2),
        "experts": a["L0_ffn_expert_w"].reshape(E, KH, P, HID).transpose(2, 1, 0, 3),
        "expert_b": a["L0_ffn_expert_b"],
        "Wo": a["L0_attn_Wo"].reshape(H, P, HID).transpose(1, 0, 2).reshape(P, H * HID),
    }


def kernel(**inputs):
    import concourse.bacc as _bacc
    from concourse.bass_utils import run_bass_kernel_spmd as _run

    nc = _bacc.Bacc("TRN2", target_bir_lowering=False, num_devices=1)
    arrays, aps = {}, {}
    for name, a in layout(inputs).items():
        a = np.ascontiguousarray(a)
        arrays[f"in_{name}"] = a
        aps[name] = nc.dram_tensor(f"in_{name}", a.shape, mybir.dt.from_np(a.dtype), kind="ExternalInput").ap()
    out = nc.dram_tensor("out_0", (B, T, HID), F32, kind="ExternalOutput").ap()
    decoder_layer(nc, aps, [out])
    r = _run(nc, [arrays], core_ids=[0])
    return r.results[0]["out_0"]
```
